# Optimizing a Trainium2 kernel written in Bass

```python
import numpy as np
import jax
import jax.numpy as jnp

def _softmax(x, axis=-1):
    return jax.nn.softmax(x, axis=axis)

def _gelu(x):
    return jax.nn.gelu(x, approximate=True)

def _silu(x):
    return jax.nn.silu(x)

def _sigmoid(x):
    return jax.nn.sigmoid(x)

def _layernorm(x, axis=-1, eps=1e-05):
    m = jnp.mean(x, axis=axis, keepdims=True)
    v = jnp.var(x, axis=axis, keepdims=True)
    return (x - m) / jnp.sqrt(v + eps)

def _scatter_add(tgt, idx, src, axis=0):
    return tgt.at[idx].add(src)

def _segment_sum(src, seg, n):
    return jax.ops.segment_sum(src, seg, n)
kernel_name = 'mk_gnn_ffn_d2_gnn_r32_b27778'

def setup_inputs(seed: int=0):
    np.random.seed(seed)
    _w = jnp.asarray

    def _rec_inputs():
        import jax
        import jax.numpy as jnp
        _gk = jax.random.key(seed)
        x = -6.415e-05 + 1 * jax.random.normal(jax.random.fold_in(_gk, 1), (3125, 256), jnp.float32)
        src = jax.random.randint(jax.random.fold_in(_gk, 2), (50000,), 0, 3125, jnp.int32)
        dst = jax.random.randint(jax.random.fold_in(_gk, 3), (50000,), 0, 3125, jnp.int32)
        _o = jnp.argsort(dst, stable=True)
        src = src[_o]
        dst = dst[_o]
        return (x, src, dst)
    x, src, dst = _rec_inputs()

    def _L0_gnn_setup():
        import jax, jax.numpy as jnp
        import numpy as np
        N = 1250
        E = 20000
        D = 256
        H = 8
        DH = D // H
        DFF = 4 * D
        SCALE = D ** (-0.5)
        EPS = 1e-05

        def layernorm(x, g, b):
            mu = jnp.mean(x, axis=-1, keepdims=True)
            var = jnp.mean(jnp.square(x - mu), axis=-1, keepdims=True)
            return (x - mu) * jax.lax.rsqrt(var + EPS) * g + b
        key = jax.random.key(seed)
        ks = jax.random.split(key, 12)
        inv = 1.0 / np.sqrt(D)
        invf = 1.0 / np.sqrt(DFF)
        return {'triplet_h': jax.random.normal(ks[0], (N, D), dtype=jnp.float32), 'src': jax.random.randint(ks[1], (E,), 0, N, dtype=jnp.int32), 'dst': jax.random.randint(ks[2], (E,), 0, N, dtype=jnp.int32), 'Wqkv': jax.random.uniform(ks[3], (D, 3 * D), jnp.float32, -inv, inv), 'bqkv': jax.random.uniform(ks[4], (3 * D,), jnp.float32, -inv, inv), 'ln_attn_g': jnp.ones((D,), jnp.float32), 'ln_attn_b': jnp.zeros((D,), jnp.float32), 'ln_res_g': jnp.ones((D,), jnp.float32), 'ln_res_b': jnp.zeros((D,), jnp.float32), 'W_in': jax.random.uniform(ks[5], (D, DFF), jnp.float32, -inv, inv), 'b_in': jax.random.uniform(ks[6], (DFF,), jnp.float32, -inv, inv), 'W_out': jax.random.uniform(ks[7], (DFF, D), jnp.float32, -invf, invf), 'b_out': jax.random.uniform(ks[8], (D,), jnp.float32, -invf, invf)}
    _L0_gnn_all = _L0_gnn_setup()
    _L0_gnn_in = {k: v for k, v in _L0_gnn_all.items() if k in ('Wqkv', 'bqkv', 'ln_attn_g', 'ln_attn_b', 'ln_res_g', 'ln_res_b', 'W_in', 'b_in', 'W_out', 'b_out')}
    del _L0_gnn_all

    def _L0_ffn_setup():
        import jax, jax.numpy as jnp
        import numpy as np
        B, S, H, F, E, K = (8, 128, 256, 512, 16, 2)
        EPS = 1e-05
        key = jax.random.key(seed)
        ks = jax.random.split(key, 9)
        sc = 0.02
        return {'x': jax.random.normal(ks[0], (B, S, H), dtype=jnp.float32), 'gate_w': jax.random.normal(ks[1], (H, E), dtype=jnp.float32) * sc, 'gate_b': jnp.zeros((E,), dtype=jnp.float32), 'w1': jax.random.normal(ks[2], (E, H, F), dtype=jnp.float32) * sc, 'b1': jnp.zeros((E, F), dtype=jnp.float32), 'w2': jax.random.normal(ks[3], (E, F, H), dtype=jnp.float32) * sc, 'b2': jnp.zeros((E, H), dtype=jnp.float32), 'gamma': jnp.ones((H,), dtype=jnp.float32), 'beta': jnp.zeros((H,), dtype=jnp.float32)}
    _L0_ffn_all = _L0_ffn_setup()
    _L0_ffn_in = {k: v for k, v in _L0_ffn_all.items() if k in ('gate_w', 'gate_b', 'w1', 'b1', 'w2', 'b2', 'gamma', 'beta')}
    del _L0_ffn_all

    def _L1_gnn_setup():
        import jax, jax.numpy as jnp
        import numpy as np
        N_NODES = 3125
        BN_EPS = 1e-05

        def gcn_conv(x, src, dst, W, b, n):
            h = x @ W
            loop = jnp.arange(n, dtype=src.dtype)
            s = jnp.concatenate([src, loop])
            d = jnp.concatenate([dst, loop])
            deg = jax.ops.segment_sum(jnp.ones(s.shape, h.dtype), d, num_segments=n)
            dinv = jnp.where(deg > 0, jax.lax.rsqrt(jnp.maximum(deg, 1.0)), 0.0)
            norm = dinv[s] * dinv[d]
            msg = h[s] * norm[:, None]
            out = jax.ops.segment_sum(msg, d, num_segments=n)
            return out + b

        def batch_norm(x, gamma, beta):
            mean = jnp.mean(x, axis=0)
            var = jnp.mean(jnp.square(x - mean), axis=0)
            return (x - mean) * jax.lax.rsqrt(var + BN_EPS) * gamma + beta
        key = jax.random.key(seed)
        ks = jax.random.split(key, 10)
        d0, d1, d2 = (256, 128, 64)
        d_cat = d0 + d1 + d2
        inp = {'node_features': jax.random.normal(ks[0], (N_NODES, d0), jnp.float32), 'edge_idx': jax.random.randint(ks[1], (2, 50000), 0, N_NODES, jnp.int64), 'W1': jax.random.normal(ks[2], (d0, d1), jnp.float32) * (1.0 / np.sqrt(d0)), 'b1': jnp.zeros((d1,), jnp.float32), 'g1': jnp.ones((d1,), jnp.float32), 'be1': jnp.zeros((d1,), jnp.float32), 'W2': jax.random.normal(ks[3], (d1, d2), jnp.float32) * (1.0 / np.sqrt(d1)), 'b2': jnp.zeros((d2,), jnp.float32), 'g2': jnp.ones((d2,), jnp.float32), 'be2': jnp.zeros((d2,), jnp.float32), 'Wfc': jax.random.normal(ks[4], (d_cat, d0), jnp.float32) * (1.0 / np.sqrt(d_cat)), 'bfc': jnp.zeros((d0,), jnp.float32)}
        return inp
    _L1_gnn_all = _L1_gnn_setup()
    _L1_gnn_in = {k: v for k, v in _L1_gnn_all.items() if k in ('W1', 'b1', 'g1', 'be1', 'W2', 'b2', 'g2', 'be2', 'Wfc', 'bfc')}
    del _L1_gnn_all

    def _L1_ffn_setup():
        import jax, jax.numpy as jnp
        import numpy as np
        B, N, D = (16, 128, 256)
        NUM_EXPERTS, TOP_K, HEADS = (4, 2, 4)
        N_EDGES = 32768
        LN_EPS = 1e-05

        def _layernorm(x, g, b):
            mu = x.mean(-1, keepdims=True)
            var = ((x - mu) ** 2).mean(-1, keepdims=True)
            return (x - mu) * jax.lax.rsqrt(var + LN_EPS) * g + b

        def _forward(x, edge_index, W_gat, att_src, att_dst, b_gat, ln_gamma, ln_beta, W1, b1, W2, b2):
            Bc, Nc, Dc = x.shape
            M = Bc * Nc
            x_flat = x.reshape(M, Dc)
            h = (x_flat @ W_gat).reshape(M, HEADS, NUM_EXPERTS)
            loops = jnp.arange(M, dtype=edge_index.dtype)
            src = jnp.concatenate([edge_index[0], loops])
            dst = jnp.concatenate([edge_index[1], loops])
            a_src = (h * att_src).sum(-1)
            a_dst = (h * att_dst).sum(-1)
            e = jax.nn.leaky_relu(a_src[src] + a_dst[dst], negative_slope=0.2)
            e_max = jax.ops.segment_max(e, dst, num_segments=M)
            ee = jnp.exp(e - e_max[dst])
            denom = jax.ops.segment_sum(ee, dst, num_segments=M)
            alpha = ee / (denom[dst] + 1e-16)
            msg = h[src] * alpha[:, :, None]
            agg = jax.ops.segment_sum(msg, dst, num_segments=M).reshape(M, HEADS * NUM_EXPERTS) + b_gat
            scores = _layernorm(agg, ln_gamma, ln_beta).reshape(M, HEADS, NUM_EXPERTS).mean(1)
            scores = scores.reshape(Bc, Nc, NUM_EXPERTS)
            topk_s, topk_i = jax.lax.top_k(scores, TOP_K)
            w = jax.nn.softmax(topk_s, axis=-1)
            out = jnp.zeros_like(x)
            for ei in range(NUM_EXPERTS):
                g = jnp.where(topk_i == ei, w, 0.0).sum(-1)
                hh = jax.nn.gelu(x @ W1[ei] + b1[ei], approximate=False)
                out = out + g[..., None] * (hh @ W2[ei] + b2[ei])
            return out
        key = jax.random.key(seed)
        ks = jax.random.split(key, 8)
        s = 0.05
        return {'x': jax.random.normal(ks[0], (B, N, D), jnp.float32), 'W_gat': jax.random.normal(ks[1], (D, HEADS * NUM_EXPERTS), jnp.float32) * s, 'att_src': jax.random.normal(ks[2], (HEADS, NUM_EXPERTS), jnp.float32) * s, 'att_dst': jax.random.normal(ks[3], (HEADS, NUM_EXPERTS), jnp.float32) * s, 'b_gat': jnp.zeros((HEADS * NUM_EXPERTS,), jnp.float32), 'ln_gamma': jnp.ones((HEADS * NUM_EXPERTS,), jnp.float32), 'ln_beta': jnp.zeros((HEADS * NUM_EXPERTS,), jnp.float32), 'W1': jax.random.normal(ks[4], (NUM_EXPERTS, D, 2 * D), jnp.float32) * s, 'b1': jnp.zeros((NUM_EXPERTS, 2 * D), jnp.float32), 'W2': jax.random.normal(ks[5], (NUM_EXPERTS, 2 * D, D), jnp.float32) * s, 'b2': jnp.zeros((NUM_EXPERTS, D), jnp.float32), 'edge_index': jax.random.randint(ks[6], (2, N_EDGES), 0, B * N, jnp.int32)}
    _L1_ffn_all = _L1_ffn_setup()
    _L1_ffn_in = {k: v for k, v in _L1_ffn_all.items() if k in ('W_gat', 'att_src', 'att_dst', 'b_gat', 'ln_gamma', 'ln_beta', 'W1', 'b1', 'W2', 'b2', 'edge_index')}
    del _L1_ffn_all
    return {'x': x, 'src': src, 'dst': dst, 'L0_gnn_Wqkv': _L0_gnn_in['Wqkv'], 'L0_gnn_bqkv': _L0_gnn_in['bqkv'], 'L0_gnn_ln_attn_g': _L0_gnn_in['ln_attn_g'], 'L0_gnn_ln_attn_b': _L0_gnn_in['ln_attn_b'], 'L0_gnn_ln_res_g': _L0_gnn_in['ln_res_g'], 'L0_gnn_ln_res_b': _L0_gnn_in['ln_res_b'], 'L0_gnn_W_in': _L0_gnn_in['W_in'], 'L0_gnn_b_in': _L0_gnn_in['b_in'], 'L0_gnn_W_out': _L0_gnn_in['W_out'], 'L0_gnn_b_out': _L0_gnn_in['b_out'], 'L0_ffn_gate_w': _L0_ffn_in['gate_w'], 'L0_ffn_gate_b': _L0_ffn_in['gate_b'], 'L0_ffn_w1': _L0_ffn_in['w1'], 'L0_ffn_b1': _L0_ffn_in['b1'], 'L0_ffn_w2': _L0_ffn_in['w2'], 'L0_ffn_b2': _L0_ffn_in['b2'], 'L0_ffn_gamma': _L0_ffn_in['gamma'], 'L0_ffn_beta': _L0_ffn_in['beta'], 'L1_gnn_W1': _L1_gnn_in['W1'], 'L1_gnn_b1': _L1_gnn_in['b1'], 'L1_gnn_g1': _L1_gnn_in['g1'], 'L1_gnn_be1': _L1_gnn_in['be1'], 'L1_gnn_W2': _L1_gnn_in['W2'], 'L1_gnn_b2': _L1_gnn_in['b2'], 'L1_gnn_g2': _L1_gnn_in['g2'], 'L1_gnn_be2': _L1_gnn_in['be2'], 'L1_gnn_Wfc': _L1_gnn_in['Wfc'], 'L1_gnn_bfc': _L1_gnn_in['bfc'], 'L1_ffn_W_gat': _L1_ffn_in['W_gat'], 'L1_ffn_att_src': _L1_ffn_in['att_src'], 'L1_ffn_att_dst': _L1_ffn_in['att_dst'], 'L1_ffn_b_gat': _L1_ffn_in['b_gat'], 'L1_ffn_ln_gamma': _L1_ffn_in['ln_gamma'], 'L1_ffn_ln_beta': _L1_ffn_in['ln_beta'], 'L1_ffn_W1': _L1_ffn_in['W1'], 'L1_ffn_b1': _L1_ffn_in['b1'], 'L1_ffn_W2': _L1_ffn_in['W2'], 'L1_ffn_b2': _L1_ffn_in['b2'], 'L1_ffn_edge_index': _L1_ffn_in['edge_index']}

def reference(x, src, dst, L0_gnn_Wqkv, L0_gnn_bqkv, L0_gnn_ln_attn_g, L0_gnn_ln_attn_b, L0_gnn_ln_res_g, L0_gnn_ln_res_b, L0_gnn_W_in, L0_gnn_b_in, L0_gnn_W_out, L0_gnn_b_out, L0_ffn_gate_w, L0_ffn_gate_b, L0_ffn_w1, L0_ffn_b1, L0_ffn_w2, L0_ffn_b2, L0_ffn_gamma, L0_ffn_beta, L1_gnn_W1, L1_gnn_b1, L1_gnn_g1, L1_gnn_be1, L1_gnn_W2, L1_gnn_b2, L1_gnn_g2, L1_gnn_be2, L1_gnn_Wfc, L1_gnn_bfc, L1_ffn_W_gat, L1_ffn_att_src, L1_ffn_att_dst, L1_ffn_b_gat, L1_ffn_ln_gamma, L1_ffn_ln_beta, L1_ffn_W1, L1_ffn_b1, L1_ffn_W2, L1_ffn_b2, L1_ffn_edge_index):
    import jax
    import jax.numpy as jnp

    def _L0_gnn_ref(triplet_h, src, dst, Wqkv, bqkv, ln_attn_g, ln_attn_b, ln_res_g, ln_res_b, W_in, b_in, W_out, b_out):
        import jax, jax.numpy as jnp
        import numpy as np
        N = 1250
        E = 20000
        D = 256
        H = 8
        DH = D // H
        DFF = 4 * D
        SCALE = D ** (-0.5)
        EPS = 1e-05

        def layernorm(x, g, b):
            mu = jnp.mean(x, axis=-1, keepdims=True)
            var = jnp.mean(jnp.square(x - mu), axis=-1, keepdims=True)
            return (x - mu) * jax.lax.rsqrt(var + EPS) * g + b
        n = triplet_h.shape[0]
        h = layernorm(triplet_h, ln_attn_g, ln_attn_b)
        qkv = (h @ Wqkv + bqkv).reshape(n, 3, H, DH)
        q = qkv[:, 0] * SCALE
        k = qkv[:, 1]
        v = qkv[:, 2]
        scores = jnp.einsum('ehd,ehd->eh', q[src], k[dst])
        m = jax.ops.segment_max(scores, dst, num_segments=n)
        e = jnp.exp(scores - m[dst])
        s = jax.ops.segment_sum(e, dst, num_segments=n)
        sa = e / s[dst]
        he = (v[src] * sa[:, :, None]).reshape(-1, D)
        agg = jax.ops.segment_sum(he, dst, num_segments=n)
        x = triplet_h + agg
        y = layernorm(x, ln_res_g, ln_res_b)
        y = jax.nn.gelu(y @ W_in + b_in, approximate=False) @ W_out + b_out
        return x + y

    def _L0_ffn_ref(x, gate_w, gate_b, w1, b1, w2, b2, gamma, beta):
        import jax, jax.numpy as jnp
        import numpy as np
        B, S, H, F, E, K = (8, 128, 256, 512, 16, 2)
        EPS = 1e-05
        gate_logits = x @ gate_w + gate_b
        topk_vals, topk_idx = jax.lax.top_k(gate_logits, K)
        topk_w = jax.nn.softmax(topk_vals, axis=-1)
        h = jax.nn.relu(jnp.einsum('bsh,ehf->bsef', x, w1) + b1)
        expert_out = jnp.einsum('bsef,efh->bseh', h, w2) + b2
        sel = jnp.take_along_axis(expert_out, topk_idx[:, :, :, None], axis=2)
        moe = jnp.sum(topk_w[..., None] * sel, axis=2)
        y = x + moe
        mu = jnp.mean(y, axis=-1, keepdims=True)
        var = jnp.var(y, axis=-1, keepdims=True)
        return (y - mu) / jnp.sqrt(var + EPS) * gamma + beta

    def _L1_gnn_ref(node_features, edge_idx, W1, b1, g1, be1, W2, b2, g2, be2, Wfc, bfc):
        import jax, jax.numpy as jnp
        import numpy as np
        N_NODES = 3125
        BN_EPS = 1e-05

        def gcn_conv(x, src, dst, W, b, n):
            h = x @ W
            loop = jnp.arange(n, dtype=src.dtype)
            s = jnp.concatenate([src, loop])
            d = jnp.concatenate([dst, loop])
            deg = jax.ops.segment_sum(jnp.ones(s.shape, h.dtype), d, num_segments=n)
            dinv = jnp.where(deg > 0, jax.lax.rsqrt(jnp.maximum(deg, 1.0)), 0.0)
            norm = dinv[s] * dinv[d]
            msg = h[s] * norm[:, None]
            out = jax.ops.segment_sum(msg, d, num_segments=n)
            return out + b

        def batch_norm(x, gamma, beta):
            mean = jnp.mean(x, axis=0)
            var = jnp.mean(jnp.square(x - mean), axis=0)
            return (x - mean) * jax.lax.rsqrt(var + BN_EPS) * gamma + beta
        n = node_features.shape[0]
        src, dst = (edge_idx[0], edge_idx[1])
        feats = [node_features]
        x = node_features
        x = gcn_conv(x, src, dst, W1, b1, n)
        x = jax.nn.relu(batch_norm(x, g1, be1))
        feats.append(x)
        x = gcn_conv(x, src, dst, W2, b2, n)
        x = jax.nn.relu(batch_norm(x, g2, be2))
        feats.append(x)
        cat = jnp.concatenate(feats, axis=1)
        return jax.nn.relu(cat @ Wfc + bfc)

    def _L1_ffn_ref(x, W_gat, att_src, att_dst, b_gat, ln_gamma, ln_beta, W1, b1, W2, b2, edge_index):
        import jax, jax.numpy as jnp
        import numpy as np
        B, N, D = (16, 128, 256)
        NUM_EXPERTS, TOP_K, HEADS = (4, 2, 4)
        N_EDGES = 32768
        LN_EPS = 1e-05

        def _layernorm(x, g, b):
            mu = x.mean(-1, keepdims=True)
            var = ((x - mu) ** 2).mean(-1, keepdims=True)
            return (x - mu) * jax.lax.rsqrt(var + LN_EPS) * g + b

        def _forward(x, edge_index, W_gat, att_src, att_dst, b_gat, ln_gamma, ln_beta, W1, b1, W2, b2):
            Bc, Nc, Dc = x.shape
            M = Bc * Nc
            x_flat = x.reshape(M, Dc)
            h = (x_flat @ W_gat).reshape(M, HEADS, NUM_EXPERTS)
            loops = jnp.arange(M, dtype=edge_index.dtype)
            src = jnp.concatenate([edge_index[0], loops])
            dst = jnp.concatenate([edge_index[1], loops])
            a_src = (h * att_src).sum(-1)
            a_dst = (h * att_dst).sum(-1)
            e = jax.nn.leaky_relu(a_src[src] + a_dst[dst], negative_slope=0.2)
            e_max = jax.ops.segment_max(e, dst, num_segments=M)
            ee = jnp.exp(e - e_max[dst])
            denom = jax.ops.segment_sum(ee, dst, num_segments=M)
            alpha = ee / (denom[dst] + 1e-16)
            msg = h[src] * alpha[:, :, None]
            agg = jax.ops.segment_sum(msg, dst, num_segments=M).reshape(M, HEADS * NUM_EXPERTS) + b_gat
            scores = _layernorm(agg, ln_gamma, ln_beta).reshape(M, HEADS, NUM_EXPERTS).mean(1)
            scores = scores.reshape(Bc, Nc, NUM_EXPERTS)
            topk_s, topk_i = jax.lax.top_k(scores, TOP_K)
            w = jax.nn.softmax(topk_s, axis=-1)
            out = jnp.zeros_like(x)
            for ei in range(NUM_EXPERTS):
                g = jnp.where(topk_i == ei, w, 0.0).sum(-1)
                hh = jax.nn.gelu(x @ W1[ei] + b1[ei], approximate=False)
                out = out + g[..., None] * (hh @ W2[ei] + b2[ei])
            return out
        return _forward(x, edge_index, W_gat, att_src, att_dst, b_gat, ln_gamma, ln_beta, W1, b1, W2, b2)
    edge_index = jnp.stack([src, dst])
    x = x + _L0_gnn_ref(_layernorm(x, axis=-1), src, dst, L0_gnn_Wqkv, L0_gnn_bqkv, L0_gnn_ln_attn_g, L0_gnn_ln_attn_b, L0_gnn_ln_res_g, L0_gnn_ln_res_b, L0_gnn_W_in, L0_gnn_b_in, L0_gnn_W_out, L0_gnn_b_out)
    x = x + _L0_ffn_ref(_layernorm(x, axis=-1)[None], L0_ffn_gate_w, L0_ffn_gate_b, L0_ffn_w1, L0_ffn_b1, L0_ffn_w2, L0_ffn_b2, L0_ffn_gamma, L0_ffn_beta)[0]
    x = x + _L1_gnn_ref(_layernorm(x, axis=-1), edge_index, L1_gnn_W1, L1_gnn_b1, L1_gnn_g1, L1_gnn_be1, L1_gnn_W2, L1_gnn_b2, L1_gnn_g2, L1_gnn_be2, L1_gnn_Wfc, L1_gnn_bfc)
    x = x + _L1_ffn_ref(_layernorm(x, axis=-1)[None], L1_ffn_W_gat, L1_ffn_att_src, L1_ffn_att_dst, L1_ffn_b_gat, L1_ffn_ln_gamma, L1_ffn_ln_beta, L1_ffn_W1, L1_ffn_b1, L1_ffn_W2, L1_ffn_b2, L1_ffn_edge_index)[0]
    return x

_drawn_inputs = setup_inputs


def setup_inputs(seed=0):
    import zlib

    import numpy as np

    out = dict(_drawn_inputs(seed))
    spreads = {'L0_gnn_ln_attn_g': (1.0, 0.6),
     'L0_gnn_ln_attn_b': (0.0, 0.1),
     'L0_gnn_ln_res_g': (1.0, 0.6),
     'L0_gnn_ln_res_b': (0.0, 0.454),
     'L0_ffn_gate_b': (0.0, 0.31),
     'L0_ffn_b1': (0.0, 0.749),
     'L0_ffn_b2': (0.0, 0.268),
     'L0_ffn_gamma': (1.0, 0.2),
     'L0_ffn_beta': (0.0, 0.1),
     'L1_gnn_b1': (0.0, 0.8),
     'L1_gnn_g1': (1.0, 0.6),
     'L1_gnn_be1': (0.0, 0.626),
     'L1_gnn_b2': (0.0, 0.8),
     'L1_gnn_g2': (1.0, 0.6),
     'L1_gnn_be2': (0.0, 0.724),
     'L1_gnn_bfc': (0.0, 0.273),
     'L1_ffn_b_gat': (0.0, 0.1),
     'L1_ffn_ln_gamma': (1.0, 0.2),
     'L1_ffn_ln_beta': (0.0, 0.275),
     'L1_ffn_b1': (0.0, 0.435),
     'L1_ffn_b2': (0.0, 0.332)}
    factors = {'L0_gnn_b_in': 4.559,
     'L0_gnn_b_out': 3.673,
     'L1_ffn_att_src': 3.749,
     'L1_ffn_att_dst': 5.416}
    for name, (base, spread) in spreads.items():
        noise = np.random.default_rng([zlib.crc32(name.encode()), seed]).standard_normal(out[name].shape)
        drawn = base * np.exp(spread * noise) if base else spread * noise
        out[name] = jnp.asarray(drawn.astype(out[name].dtype))
    for name, factor in factors.items():
        out[name] = (out[name] * factor).astype(out[name].dtype)
    return out
```

```python
from contextlib import ExitStack

import numpy as np
import concourse.bass as bass
from concourse import mybir

F32 = mybir.dt.float32
BF16 = mybir.dt.bfloat16
I32 = mybir.dt.int32
U32 = mybir.dt.uint32
ALU = mybir.AluOpType
ACT = mybir.ActivationFunctionType
AX = mybir.AxisListType

P = 128
N, D = 3125, 256
TN, NT = 125, 25
E1, E2 = 50000, 32768
PB, RING = 4, 4
TURN = PB * RING
H = 8
GH, GE = 4, 4
BIG = 1e30
NO_DST, NO_KEY = 8191.0, -7.0
EPS = 1e-5


class Phase:

    def __init__(self, nc, name):
        self.nc, self.name = nc, name

    def __enter__(self):
        self.ctx, self.sems = ExitStack(), []
        return self

    def sb(self, name, shape, dt=F32):
        return self.ctx.enter_context(self.nc.sbuf_tensor(f"{self.name}_{name}", shape, dt))

    def psum(self, name, shape, dt=F32):
        return self.ctx.enter_context(self.nc.psum_tensor(f"{self.name}_{name}", shape, dt))

    def sem(self, name):
        s = self.nc.alloc_semaphore(f"{self.name}_{name}")
        self.sems.append(s)
        return s

    def __exit__(self, kind, value, trace):
        self.ctx.close()
        if kind is None:
            self.nc.clear_and_free_semaphores(self.sems)
            self.nc.all_engine_barrier()


def chain(eng, sem, base=0):
    n = [0]

    def link(ins):
        n[0] += 1
        ins.then_inc(sem, 1)
        eng.wait_ge(sem, base + n[0])
    return link


def row_stats(nc, name, X, rstd, shift):
    with Phase(nc, name) as ph:
        parts = ph.sb("parts", [TN, NT, 6])
        a, b, c = (ph.sb(k, [TN, NT]) for k in "abc")
        taken, link_s, var_ready, root_ready = (ph.sem(k) for k in ("taken", "link", "var", "root"))
        with nc.Block() as block:
            @block.vector
            def _(v):
                with v.Fori(0, 5) as i:
                    for s in range(5):
                        v.bn_stats(out=parts[:, i * 5 + s, :], in_=X[:, i * 5 + s, :]).then_inc(taken, 1)
                v.wait_ge(taken, NT)
                link = chain(v, link_s)
                link(v.tensor_tensor(a[:], parts[:, :, 1], parts[:, :, 4], ALU.add))
                link(v.tensor_tensor(b[:], parts[:, :, 1], parts[:, :, 4], ALU.subtract))
                link(v.tensor_tensor(c[:], parts[:, :, 2], parts[:, :, 5], ALU.add))
                link(v.tensor_tensor(b[:], b[:], b[:], ALU.mult))
                link(v.scalar_tensor_tensor(out=b[:], in0=b[:], scalar=D / 4.0, in1=c[:], op0=ALU.mult, op1=ALU.add))
                v.tensor_scalar(c[:], b[:], 1.0 / D, EPS, ALU.mult, ALU.add).then_inc(var_ready, 1)
                v.wait_ge(root_ready, 1)
                link(v.reciprocal(rstd[:], b[:]))
                link(v.scalar_tensor_tensor(out=shift[:], in0=a[:], scalar=-0.5, in1=rstd[:], op0=ALU.mult, op1=ALU.mult))

            @block.scalar
            def _(act):
                act.wait_ge(var_ready, 1)
                nc.scalar.activation(b[:], c[:], ACT.Sqrt).then_inc(root_ready, 1)


def normalise(nc, name, X, rstd, shift, out):
    with Phase(nc, name) as ph:
        done = ph.sem("done")
        with nc.Block() as block:
            @block.vector
            def _(v):
                with v.Fori(0, 5) as i:
                    for s in range(5):
                        t = i * 5 + s
                        v.tensor_scalar(out[:, t, :], X[:, t, :], rstd[:, bass.ds(t, 1)], shift[:, bass.ds(t, 1)],
                                        ALU.mult, ALU.add).then_inc(done, 1)
                v.wait_ge(done, NT)


def project(nc, name, cs, X, rstd, shift, weight, jobs, finish, affine=None, UT=None, rows_out=None):
    J = len(jobs)
    with Phase(nc, name) as ph:
        row = ph.sb("row", [TN, 5, D])
        rowT = ph.sb("rowT", [P, 5, 2, TN])
        tp = [ph.psum(f"tp{s}", [P, 2, TN]) for s in range(2)]
        pj = [ph.psum(f"pj{s}", [TN, 512]) for s in range(5)] if J else []
        W = ph.sb("W", [P, 2, weight.shape[1]]) if J else None
        G = ph.sb("G", [TN, 2, D]) if affine else None
        loaded, row_ready, turned, copied, projected, finished, link_s, passed = (
            ph.sem(k) for k in ("loaded", "row", "turned", "copied", "projected", "finished", "link", "passed"))
        n_links = (2 if affine else 0) * 5
        with nc.Block() as block:
            @block.sync
            def _(sp):
                if J:
                    sp.dma_start(W[:], weight.rearrange("(k p) n -> p k n", p=P)).then_inc(loaded, 16)
                if affine:
                    for k in range(2):
                        sp.dma_start(G[:, k, :], affine[k].partition_broadcast(TN)).then_inc(loaded, 16)

            @block.vector
            def _(v):
                if affine:
                    v.wait_ge(loaded, 16 * (2 + (J > 0)))
                v.sem_inc(finished, 5)
                with v.Fori(0, 5) as i:
                    link = chain(v, link_s, i * n_links)

                    def make_row(s):
                        t = i * 5 + s
                        v.wait_ge(copied, i * 5 + (s + 1))
                        ins = v.tensor_scalar(row[:, s, :], X[:, t, :], rstd[:, bass.ds(t, 1)], shift[:, bass.ds(t, 1)],
                                              ALU.mult, ALU.add)
                        if affine:
                            link(ins)
                            link(v.tensor_tensor(row[:, s, :], row[:, s, :], G[:, 0, :], ALU.mult))
                            ins = v.tensor_tensor(row[:, s, :], row[:, s, :], G[:, 1, :], ALU.add)
                        ins.then_inc(row_ready, 1)

                    def finish_tile(s):
                        for j in range(J):
                            q = s * J + j
                            v.wait_ge(projected, i * (5 * J) + (q + 1))
                            finish(v, j, i * 5 + s, s, pj[q % 5][:, 0:jobs[j][1]]).then_inc(finished, 1)

                    for s in range(5):
                        make_row(s)
                        if s:
                            finish_tile(s - 1)
                    finish_tile(4)
                v.wait_ge(finished, 25 * J + 5)

            @block.tensor
            def _(pe):
                if J:
                    pe.wait_ge(loaded, 16 * (1 + 2 * bool(affine)))
                with pe.Fori(0, 5) as i:
                    def turn(s):
                        pe.wait_ge(row_ready, i * 5 + (s + 1))
                        pe.sem_inc(passed, 1)
                        pe.wait_ge(copied, i * 5 + (s + 4))
                        for k in range(2):
                            ins = pe.transpose(tp[s % 2][:, k, :], row[:, s, k * P:(k + 1) * P], cs.ident[0:TN, 0:TN])
                        ins.then_inc(turned, 1)

                    def products(s):
                        pe.wait_ge(copied, i * 5 + (s + 6))
                        for j, (c0, w) in enumerate(jobs):
                            q = s * J + j
                            pe.wait_ge(finished, i * (5 * J) + (q + 1))
                            for k in range(2):
                                ins = pe.matmul(pj[q % 5][:, 0:w], rowT[:, s, k, :], W[:, k, c0:c0 + w],
                                                start=(k == 0), stop=(k == 1))
                            ins.then_inc(projected, 1)

                    pe.wait_ge(copied, i * 5 + 5)
                    pe.sem_inc(passed, 1)
                    for s in range(5):
                        turn(s)
                        if s:
                            products(s - 1)
                    products(4)

            @block.scalar
            def _(act):
                act.sem_inc(copied, 5)
                with act.Fori(0, 5) as i:
                    for s in range(5):
                        t = i * 5 + s
                        act.wait_ge(turned, i * 5 + (s + 1))
                        act.sem_inc(passed, 1)
                        if rows_out is not None:
                            nc.scalar.copy(rows_out[:, t, :], row[:, s, :])
                        if UT is not None:
                            nc.scalar.copy(UT[:, :, bass.ds(t * TN, TN)], tp[s % 2][:])
                        nc.scalar.copy(rowT[:, s, :, :], tp[s % 2][:]).then_inc(copied, 1)


class Consts:

    def __init__(self, sb):
        self.ident = sb("ident", [P, P])
        self.ones = sb("ones", [P, P])
        self.count_row = sb("count_row", [P, pairs_of(E1)])
        self.count_col = sb("count_col", [P, 1])
        self.neg_col = sb("neg_col", [P, 1])


def pairs_of(edges):
    most = (edges + P - 1) // P + NT - 1
    return (most // 32 + 1) * 32


class Graph:

    def __init__(self, name, sb, dram, consts, edges):
        self.ident, self.ones, self.count_row = consts.ident, consts.ones, consts.count_row
        self.count_col, self.neg_col = consts.count_col, consts.neg_col
        self.name, self.edges, self.pairs = name, edges, pairs_of(edges)
        self.loops = self.pairs // TURN
        self.src_of = sb(f"{name}_src_of", [P, self.pairs], I32)
        self.tile_of = sb(f"{name}_tile_of", [1, self.pairs], I32)
        self.local = sb(f"{name}_local", [P, self.pairs])
        self.neg_local = sb(f"{name}_neg_local", [P, self.pairs])
        self.neg_big = sb(f"{name}_neg_big", [P, self.pairs])
        self.last_of = sb(f"{name}_last_of", [P, self.pairs])
        self.local_rows = dram(f"{name}_local_rows", [self.pairs, P]).ap()
        self.keys_t = dram(f"{name}_keys", [self.pairs * P + 2])
        self.keys = self.keys_t.ap()


def constants(nc, cs):
    with Phase(nc, "const") as ph:
        made = ph.sem("made")
        t32 = ph.sb("t32", [P, cs.count_row.shape[1]], I32)
        p32 = ph.sb("p32", [P, 1], I32)
        with nc.Block() as block:
            @block.gpsimd
            def _(g):
                link = chain(g, made)
                link(g.memset(cs.ident[:], 0.0))
                link(g.affine_select(out=cs.ident[:], in_=cs.ident[:], compare_op=ALU.not_equal, fill=1.0,
                                     base=0, pattern=[[-1, P]], channel_multiplier=1))
                link(g.iota(t32[:], pattern=[[1, cs.count_row.shape[1]]], base=0, channel_multiplier=0))
                link(g.tensor_copy(cs.count_row[:], t32[:]))
                link(g.iota(p32[:], pattern=[[1, 1]], base=0, channel_multiplier=1))
                link(g.tensor_copy(cs.count_col[:], p32[:]))
                link(g.tensor_scalar(cs.neg_col[:], cs.count_col[:], -1.0, None, ALU.mult))
                link(g.memset(cs.ones[:], 1.0))


def index_tables(nc, cs, src=None, dst=None, joined=None):
    PAIRS, E = cs.pairs, cs.edges
    PR = PAIRS // 4
    NB = (PAIRS + P - 1) // P
    count = cs.count_row[:, 0:PAIRS]
    with Phase(nc, cs.name) as ph:
        raw = ph.sb("raw", [P, 2, NB, P] if joined is None else [P, NB, P, 2], I32)
        raw_of = [raw[:, k, :, :] if joined is None else raw[:, :, :, k] for k in range(2)]
        val = ph.sb("val", [P, 2, NB, P])
        W = NT - 1 + NB * P
        lanes = ph.sb("lanes", [P, 2, W])
        less = ph.sb("less", [P, NT - 1])
        junk = ph.sb("junk", [P, NB * P])
        first = ph.sb("first", [P, NT - 1])
        firsti = ph.sb("firsti", [P, NT - 1], I32)
        mask = ph.sb("mask", [P, PAIRS], I32)
        srcx = ph.sb("srcx", [P, PAIRS])
        dstx = ph.sb("dstx", [P, PAIRS])
        tile_f = ph.sb("tile_f", [P, PAIRS])
        valid = ph.sb("valid", [P, PAIRS])
        key = ph.sb("key", [P, PAIRS])
        rows = ph.sb("rows", [PR, 2, 4, P])
        near = ph.sb("near", [PR, 2, 4, P])
        edge1 = ph.sb("edge1", [1, 2])
        pt = [ph.psum(f"pt{b}", [P, NB, P]) for b in range(2)]
        pr = [ph.psum(f"pr{b}", [PR, 4, P]) for b in range(2)]
        pn = ph.psum("pn", [P, NT - 1])
        pe_end = ph.psum("pe", [P, 4, P])
        filled, loaded, cast, turned, summed, tables, rowed, in_rows, written, near_in, ends, ended, v_link = (
            ph.sem(k) for k in ("filled", "loaded", "cast", "turned", "summed", "tables", "rowed", "in_rows", "written",
                                "near_in", "ends", "ended", "link"))
        FB = E // (P * P)
        full = FB * P * P
        rest = (E - full) // P
        tail = E - full - rest * P
        n_loads = 1 if joined is not None else 2 * (1 + (rest > 0) + (tail > 0))
        assert joined is None or full == E
        with nc.Block() as block:
            @block.sync
            def _(sp):
                sp.wait_ge(filled, 2)
                if joined is not None:
                    sp.dma_start(raw[:, 0:FB, :, :], joined.rearrange("(b t l) k -> t b l k", b=FB, l=P)).then_inc(loaded, 16)
                for k, a in enumerate((dst, src) if joined is None else ()):
                    sp.dma_start(raw[:, k, 0:FB, :], a[0:full].rearrange("(b t l) -> t b l", b=FB, l=P)).then_inc(loaded, 16)
                    if rest:
                        sp.dma_start(raw[0:rest, k, FB, :], a[full:full + rest * P].rearrange("(t l) -> t l", l=P)).then_inc(loaded, 16)
                    if tail:
                        sp.dma_start(raw[rest:rest + 1, k, FB, 0:tail], a[E - tail:E].rearrange("(t l) -> t l", t=1)).then_inc(loaded, 16)
                sp.wait_ge(in_rows, 2)
                sp.dma_start(cs.local_rows.rearrange("(b r) l -> r b l", b=4), rows[:, 0, :, :]).then_inc(written, 16)
                body = cs.keys[1:1 + PAIRS * P]
                sp.dma_start(body.rearrange("(b r l) -> r b l", b=4, l=P), rows[:, 1, :, :]).then_inc(written, 16)
                sp.dma_start(cs.keys[0:1].rearrange("(a b) -> a b", a=1), edge1[:, 0:1]).then_inc(written, 16)
                sp.dma_start(cs.keys[1 + PAIRS * P:2 + PAIRS * P].rearrange("(a b) -> a b", a=1), edge1[:, 1:2]).then_inc(written, 16)
                sp.wait_ge(written, 64)
                for k in range(2):
                    sp.dma_start(near[:, k, :, :], cs.keys[1 + k:1 + k + PAIRS * P].rearrange("(b r l) -> r b l", b=4, l=P)).then_inc(near_in, 16)
                sp.wait_ge(near_in, 32)

            @block.vector
            def _(v):
                v.memset(raw_of[0][:, FB, :], int(NO_DST)).then_inc(filled, 1)
                v.memset(raw_of[1][:, FB, :], 0).then_inc(filled, 1)
                link = chain(v, v_link)
                link(v.memset(edge1[:], NO_KEY))
                link(v.memset(lanes[:], 0.0))
                v.wait_ge(loaded, 16 * n_loads)
                v.tensor_copy(val[:, 0, :, :], raw_of[0])
                v.tensor_copy(val[:, 1, :, :], raw_of[1]).then_inc(cast, 1)
                v.wait_ge(cast, 1)
                for j in range(1, NT):
                    link(v.tensor_scalar(junk[:], val[:, 0, :, :].rearrange("p b l -> p (b l)"), float(TN * j), 0.0, ALU.is_lt, ALU.add,
                                         accum_out=less[:, j - 1:j]))
                v.sem_inc(cast, 1)
                v.wait_ge(turned, 2)
                for k in range(2):
                    link(v.tensor_copy(lanes[:, k, NT - 1:NT - 1 + NB * P], pt[k][:].rearrange("p b l -> p (b l)")))
                v.wait_ge(summed, 1)
                link(v.tensor_copy(firsti[:], pn[:]))
                link(v.tensor_scalar(firsti[:], firsti[:], 7, None, ALU.arith_shift_right))
                link(v.tensor_copy(first[:], firsti[:]))
                link(v.scalar_tensor_tensor(out=first[:], in0=first[:], scalar=1.0, in1=cs.count_row[:, 0:NT - 1], op0=ALU.add, op1=ALU.add))
                link(v.memset(tile_f[:], 0.0))
                link(v.tensor_copy(dstx[:], lanes[:, 0, NT - 1:NT - 1 + PAIRS]))
                link(v.tensor_copy(srcx[:], lanes[:, 1, NT - 1:NT - 1 + PAIRS]))
                for j in range(1, NT):
                    at = first[:, j - 1:j]
                    link(v.tensor_scalar(mask[:], count, at, None, ALU.is_ge))
                    link(v.copy_predicated(dstx[:], mask[:], lanes[:, 0, NT - 1 - j:NT - 1 - j + PAIRS]))
                    link(v.copy_predicated(srcx[:], mask[:], lanes[:, 1, NT - 1 - j:NT - 1 - j + PAIRS]))
                    link(v.scalar_tensor_tensor(out=tile_f[:], in0=count, scalar=at, in1=tile_f[:], op0=ALU.is_ge, op1=ALU.add))
                link(v.tensor_copy(cs.src_of[:], srcx[:]))
                link(v.tensor_copy(cs.tile_of[:], tile_f[0:1, :]))
                link(v.scalar_tensor_tensor(out=cs.local[:], in0=tile_f[:], scalar=-float(TN), in1=dstx[:], op0=ALU.mult, op1=ALU.add))
                link(v.tensor_scalar(cs.neg_local[:], cs.local[:], -1.0, None, ALU.mult))
                link(v.tensor_scalar(valid[:], cs.local[:], 0.0, None, ALU.is_ge))
                link(v.scalar_tensor_tensor(out=valid[:], in0=cs.local[:], scalar=float(TN), in1=valid[:], op0=ALU.is_lt, op1=ALU.mult))
                link(v.tensor_scalar(cs.neg_big[:], valid[:], BIG, -BIG, ALU.mult, ALU.add))
                link(v.scalar_tensor_tensor(out=key[:], in0=dstx[:], scalar=1.0, in1=valid[:], op0=ALU.add, op1=ALU.mult))
                link(v.tensor_scalar(key[:], key[:], -1.0, None, ALU.add))
                v.sem_inc(tables, 1)
                for k in range(2):
                    v.wait_ge(rowed, k + 1)
                    v.tensor_copy(rows[:, k, :, :], pr[k][:]).then_inc(in_rows, 1)
                v.wait_ge(near_in, 32)
                v.tensor_tensor(near[:, 0, :, :], near[:, 0, :, :], near[:, 1, :, :], ALU.not_equal).then_inc(ends, 1)
                v.wait_ge(ended, 1)
                link(v.tensor_copy(cs.last_of[:].rearrange("p (b r) -> p b r", b=4), pe_end[:, :, 0:PR]))

            @block.tensor
            def _(pe):
                pe.wait_ge(cast, 1)
                for k in range(2):
                    for b in range(NB):
                        ins = pe.transpose(pt[k][:, b, :], val[:, k, b, :], cs.ident[:])
                    ins.then_inc(turned, 1)
                pe.wait_ge(cast, 2)
                pe.matmul(pn[:], cs.ones[:], less[:], start=True, stop=True).then_inc(summed, 1)
                pe.wait_ge(tables, 1)
                for k, table in enumerate((cs.local, key)):
                    for b in range(4):
                        ins = pe.transpose(pr[k][:, b, :], table[:, b * PR:(b + 1) * PR], cs.ident[:])
                    ins.then_inc(rowed, 1)
                pe.wait_ge(ends, 1)
                for b in range(4):
                    ins = pe.transpose(pe_end[:, b, 0:PR], near[:, 0, b, :], cs.ident[0:PR, 0:PR])
                ins.then_inc(ended, 1)


def sort_edges(nc, cs, edge_index, joined):
    ES = edge_index.shape[1]
    ST = ES // P
    NB = ST // P
    TURNS = ST // TURN
    A = NT
    with Phase(nc, "sort") as ph:
        raw = ph.sb("raw", [P, 2, NB, P], I32)
        val = ph.sb("val", [P, 2, NB, P])
        lanes = ph.sb("lanes", [P, 2, ST])
        pay = ph.sb("pay", [P, ST, 2], I32)
        a_of, b_of = ph.sb("a_of", [P, ST]), ph.sb("b_of", [P, ST])
        earlier = ph.sb("earlier", [P, P])
        upper = ph.sb("upper", [P, A])
        zero = ph.sb("zero", [P, TN], BF16)
        rows = ph.sb("rows", [P, RING, PB * P], I32)
        hotA = ph.sb("hotA", [P, RING, PB, A], BF16)
        hotAf = ph.sb("hotAf", [P, RING, PB, A])
        hotB = ph.sb("hotB", [P, RING, PB, TN], BF16)
        hotT = ph.sb("hotT", [A, RING, PB, P])
        hist, incl, start = (ph.sb(k, [A, TN]) for k in ("hist", "incl", "start"))
        zeros = ph.sb("zeros", [A, TN])
        before = ph.sb("before", [A, 1])
        snap = ph.sb("snap", [A, 2, TN])
        same = ph.sb("same", [P, RING, PB, P])
        pick = ph.sb("pick", [P, RING, PB, TN])
        n_same, n_before = ph.sb("n_same", [P, RING, PB]), ph.sb("n_before", [P, RING, PB])
        pos = ph.sb("pos", [P, RING, PB], I32)
        payload = ph.sb("payload", [P, RING, PB, 2], I32)
        pt = [ph.psum(f"pt{k}", [P, NB, P]) for k in range(2)]
        counts = ph.psum("counts", [A, 512])
        pa = ph.psum("pa", [A, PB, P])
        pr = [ph.psum(f"pr{k}", [P, 512]) for k in range(4)]
        loaded, cast, turned, consts, v_link, g_link, hot1, summed1, hist_out, off, off_in, started = (
            ph.sem(k) for k in ("loaded", "cast", "turned", "consts", "v_link", "g_link", "hot1", "summed1", "hist", "off", "off_in", "started"))
        hots, hot_turned, hot_copied, snapped, grown, looked, placed, rank_on, pe_on, act_on, sp_on, dve_on, pool_on = (
            ph.sem(k) for k in ("hots", "hot_turned", "hot_copied", "snapped", "grown", "looked", "placed", "rank_on", "pe_on", "act_on",
                                "sp_on", "dve_on", "pool_on"))
        rows_in = [ph.sem(f"rows{q}") for q in range(RING)]
        out = [ph.sem(f"out{q}") for q in range(RING)]
        with nc.Block() as block:
            @block.sync
            def _(sp):
                for k in range(2):
                    sp.dma_start(raw[:, k, :, :], edge_index[1 - k].rearrange("(b t l) -> t b l", b=NB, l=P)).then_inc(loaded, 16)
                with sp.Fori(0, TURNS) as i:
                    for q in range(RING):
                        sp.wait_ge(placed, i * RING + (q + 1))
                        sp.sem_inc(sp_on, 1)
                        sp.dma_start(rows[:, q, :], edge_index[1, bass.ds(i * (TURN * P) + q * PB * P, PB * P)].partition_broadcast(P))\
                          .then_inc(rows_in[q], 16)

            @block.gpsimd
            def _(g):
                link = chain(g, g_link)
                link(g.memset(earlier[:], 1.0))
                link(g.memset(upper[:], 1.0))
                link(g.affine_select(out=earlier[:], in_=earlier[:], compare_op=ALU.is_gt, fill=0.0, base=0,
                                     pattern=[[-1, P]], channel_multiplier=1))
                link(g.affine_select(out=upper[:], in_=upper[:], compare_op=ALU.is_gt, fill=0.0, base=0,
                                     pattern=[[1, A]], channel_multiplier=-1))
                g.sem_inc(consts, 1)
                with g.Fori(0, TURNS) as i:
                    for q in range(RING):
                        g.wait_ge(placed, i * RING + (RING + q + 1))
                        g.sem_inc(pool_on, 1)
                        for u in range(PB):
                            g.indirect_dma_start(out=joined, out_offset=bass.IndirectOffsetOnAxis(ap=pos[:, q, u:u + 1], axis=0),
                                                 in_=payload[:, q, u, :], in_offset=None).then_inc(out[q], 16)
                for q in range(RING):
                    g.wait_ge(out[q], 16 * PB * TURNS)

            @block.vector
            def _(v):
                link = chain(v, v_link)
                v.wait_ge(loaded, 32)
                v.tensor_copy(val[:], raw[:]).then_inc(cast, 1)
                link(v.memset(a_of[:], 0.0))
                link(v.memset(zero[:], 0.0))
                link(v.memset(zeros[:], 0.0))
                v.wait_ge(turned, 2)
                for k in range(2):
                    link(v.tensor_copy(lanes[:, k, :], pt[k][:].rearrange("p b l -> p (b l)")))
                    link(v.tensor_copy(pay[:, :, k], lanes[:, k, :]))
                for j in range(1, A):
                    link(v.scalar_tensor_tensor(out=a_of[:], in0=lanes[:, 0, :], scalar=float(TN * j), in1=a_of[:], op0=ALU.is_ge, op1=ALU.add))
                link(v.scalar_tensor_tensor(out=b_of[:], in0=a_of[:], scalar=-float(TN), in1=lanes[:, 0, :], op0=ALU.mult, op1=ALU.add))

                def make_hots(i, q, ready, floats):
                    tiles = bass.ds(i * TURN + q * PB, PB)
                    wide = lambda x, n: x[:, tiles].unsqueeze(2).to_broadcast([P, PB, n])
                    number = lambda n: cs.count_row[:, 0:n].unsqueeze(1).to_broadcast([P, PB, n])
                    v.tensor_tensor(hotA[:, q, :, :], number(A), wide(a_of, A), ALU.is_equal)
                    if floats:
                        v.tensor_tensor(hotAf[:, q, :, :], number(A), wide(a_of, A), ALU.is_equal)
                    v.tensor_tensor(hotB[:, q, :, :], number(TN), wide(b_of, TN), ALU.is_equal).then_inc(ready, 1)

                with v.Fori(0, TURNS) as i:
                    for q in range(RING):
                        v.wait_ge(summed1, i * RING + (q + 1))
                        v.sem_inc(dve_on, 1)
                        make_hots(i, q, hot1, False)
                v.wait_ge(summed1, TURNS * RING + RING)
                v.tensor_copy(hist[:], counts[:, 0:TN]).then_inc(hist_out, 1)
                v.wait_ge(hist_out, 1)
                link(v.tensor_tensor_scan(incl[:], zeros[:], hist[:], 0.0, ALU.add, ALU.add))
                v.sem_inc(off, 1)
                v.wait_ge(off_in, 1)
                link(v.tensor_copy(before[:], pr[0][0:A, 0:1]))
                link(v.tensor_tensor(start[:], incl[:], hist[:], ALU.subtract))
                link(v.tensor_scalar(start[:], start[:], before[:, 0:1], None, ALU.add))
                v.sem_inc(started, 1)
                v.wait_ge(consts, 1)
                v.sem_inc(placed, RING)
                v.sem_inc(looked, 4)
                def place_turn(i, first):
                    for q in range(RING):
                        v.wait_ge(grown, i * TURN + (q * PB + PB))
                        v.sem_inc(dve_on, 1)
                        make_hots(i, q, hots, True)
                        v.wait_ge(rows_in[q], i * 16 + 16)
                        v.sem_inc(dve_on, 1)
                        for u in range(PB):
                            v.scalar_tensor_tensor(out=same[:, q, u, :], in0=rows[:, q, u * P:(u + 1) * P],
                                                   scalar=lanes[:, 0, bass.ds(i * TURN + q * PB + u, 1)], in1=earlier[:],
                                                   op0=ALU.is_equal, op1=ALU.mult, accum_out=n_same[:, q, u:u + 1])
                        for u in range(PB):
                            v.wait_ge(rank_on, i * TURN + (q * PB + u + 3))
                            v.sem_inc(dve_on, 1)
                            v.tensor_tensor_reduce(out=pick[:, q, u, :], in0=pr[u][:, 0:TN], in1=hotB[:, q, u, :], scale=1.0, scalar=0.0,
                                                   op0=ALU.mult, op1=ALU.add, accum_out=n_before[:, q, u:u + 1]).then_inc(looked, 1)
                        v.wait_ge(looked, i * TURN + (q * PB + PB + 4))
                        v.sem_inc(dve_on, 1)
                        if not first:
                            v.wait_ge(out[q], i * (16 * PB))
                            v.sem_inc(dve_on, 1)
                        v.tensor_copy(payload[:, q, :, :], pay[:, bass.ds(i * TURN + q * PB, PB), :])
                        v.tensor_tensor(pos[:, q, :], n_same[:, q, :], n_before[:, q, :], ALU.add).then_inc(placed, 1)

                place_turn(0, True)
                with v.Fori(1, TURNS) as i:
                    place_turn(i, False)

            @block.tensor
            def _(pe):
                pe.wait_ge(cast, 1)
                for k in range(2):
                    for b in range(NB):
                        ins = pe.transpose(pt[k][:, b, :], val[:, k, b, :], cs.ident[:])
                    ins.then_inc(turned, 1)
                pe.sem_inc(summed1, RING)
                pe.wait_ge(hot1, 1)
                pe.matmul(counts[:, 0:TN], zero[:, 0:A], zero[:], start=True, stop=True)
                with pe.Fori(0, TURNS) as i:
                    for q in range(RING):
                        pe.wait_ge(hot1, i * RING + (q + 1))
                        pe.sem_inc(pe_on, 1)
                        for u in range(PB):
                            ins = pe.matmul(counts[:, 0:TN], hotA[:, q, u, :], hotB[:, q, u, :], start=False, stop=True, skip_group_check=True)
                        ins.then_inc(summed1, 1)
                pe.wait_ge(off, 1)
                pe.wait_ge(consts, 1)
                pe.matmul(pr[0][0:A, 0:1], upper[0:A, :], incl[:, TN - 1:TN], start=True, stop=True).then_inc(off_in, 1)
                pe.wait_ge(started, 1)
                pe.matmul(counts[:, 0:TN], cs.ident[0:A, 0:A], start[:], start=True, stop=True).then_inc(grown, 1)
                pe.sem_inc(grown, TURN - 1)
                pe.sem_inc(rank_on, 2)
                with pe.Fori(0, TURNS) as i:
                    for q in range(RING):
                        pe.wait_ge(hots, i * RING + (q + 1))
                        pe.sem_inc(pe_on, 1)
                        pe.wait_ge(hot_copied, i * RING + (q + 1))
                        pe.sem_inc(pe_on, 1)
                        for u in range(PB):
                            ins = pe.transpose(pa[:, u, :], hotAf[:, q, u, :], cs.ident[:])
                        ins.then_inc(hot_turned, 1)
                        pe.wait_ge(hot_copied, i * RING + (q + 2))
                        pe.sem_inc(pe_on, 1)
                        for u in range(PB):
                            n = i * TURN + (q * PB + u + 1)
                            pe.wait_ge(snapped, n)
                            pe.sem_inc(pe_on, 1)
                            pe.matmul(counts[:, 0:TN], hotA[:, q, u, :], hotB[:, q, u, :], start=False, stop=True,
                                      skip_group_check=True).then_inc(grown, 1)
                            pe.wait_ge(looked, n)
                            pe.sem_inc(pe_on, 1)
                            pe.matmul(pr[u][:, 0:TN], hotT[:, q, u, :], snap[:, u % 2, :], start=True, stop=True).then_inc(rank_on, 1)

            @block.scalar
            def _(act):
                act.sem_inc(hot_copied, 1)
                with act.Fori(0, TURNS) as i:
                    for q in range(RING):
                        act.wait_ge(hot_turned, i * RING + (q + 1))
                        act.sem_inc(act_on, 1)
                        nc.scalar.copy(hotT[:, q, :, :], pa[:]).then_inc(hot_copied, 1)
                        for u in range(PB):
                            n = i * TURN + (q * PB + u)
                            act.wait_ge(grown, n + TURN)
                            act.sem_inc(act_on, 1)
                            act.wait_ge(rank_on, n + 1)
                            act.sem_inc(act_on, 1)
                            nc.scalar.copy(snap[:, u % 2, :], counts[:, 0:TN]).then_inc(snapped, 1)


def gather_pairs(g, cs, table, ring, idx, idx_ready, slot_free, got, passed):
    with g.Fori(0, cs.loops) as i:
        for q in range(RING):
            g.wait_ge(slot_free, i * RING + (q + 1))
            g.tensor_copy(idx[:, q, :], cs.src_of[:, bass.ds(i * (TURN) + q * PB, PB)]).then_inc(idx_ready, 1)
            g.wait_ge(idx_ready, i * RING + (q + 1))
            g.sem_inc(passed, 1)
            for u in range(PB):
                g.indirect_dma_start(out=ring[:, q * PB + u, :], out_offset=None, in_=table,
                                     in_offset=bass.IndirectOffsetOnAxis(ap=idx[:, q, u:u + 1], axis=0)).then_inc(got[q], 16)


def load_local_rows(sp, cs, Lb, lb_got, hot_ready, passed):
    with sp.Fori(0, cs.loops) as i:
        for q in range(RING):
            sp.wait_ge(hot_ready, i * RING + (q + 1))
            sp.sem_inc(passed, 1)
            rows = cs.local_rows[bass.ds(i * (TURN) + q * PB, PB), :].rearrange("r l -> (r l)")
            sp.dma_start(Lb[:, q, :], rows.partition_broadcast(TN)).then_inc(lb_got[q], 16)


def node_hots(nc, act, cs, Lb, hotT, dist, lb_got, hot_ready, dist_ready, i, q):
    act.wait_ge(lb_got[q], i * 16 + 16)
    act.sem_inc(dist_ready[1], 1)
    nc.scalar.activation(dist[:, q, :], Lb[:, q, :], ACT.Abs, bias=cs.neg_col[0:TN, :]).then_inc(dist_ready[0], 1)
    act.wait_ge(dist_ready[0], i * RING + (q + 1))
    nc.scalar.activation(hotT[:, q, :], dist[:, q, :], ACT.Relu, scale=-1.0, bias=1.0).then_inc(hot_ready, 1)


def edge_scores(nc, cs, q_dram, K, S):
    with Phase(nc, "score") as ph:
        ring = ph.sb("ring", [P, TURN, D])
        idx = ph.sb("idx", [P, RING, PB], I32)
        Lb = ph.sb("Lb", [TN, RING, PB * P])
        hotT = ph.sb("hotT", [TN, RING, PB * P])
        dist = ph.sb("dist", [TN, RING, PB * P])
        prod = ph.sb("prod", [P, 2, PB * D])
        kd = [ph.psum(f"kd{q}", [P, PB * D]) for q in range(RING)]
        idx_ready, hot_ready, kd_ready, multiplied, reduced, dist_ready, pool_on, sp_on, act_on, pe_on, dve_on = (
            ph.sem(k) for k in ("idx", "hot", "kd", "multiplied", "reduced", "dist", "pool_on", "sp_on", "act_on", "pe_on", "dve_on"))
        got = [ph.sem(f"got{q}") for q in range(RING)]
        lb_got = [ph.sem(f"lb{q}") for q in range(RING)]
        with nc.Block() as block:
            @block.gpsimd
            def _(g):
                gather_pairs(g, cs, q_dram, ring, idx, idx_ready, multiplied, got, pool_on)

            @block.sync
            def _(sp):
                load_local_rows(sp, cs, Lb, lb_got, hot_ready, sp_on)

            @block.scalar
            def _(act):
                act.sem_inc(hot_ready, RING)
                with act.Fori(0, cs.loops) as i:
                    for q in range(RING):
                        act.wait_ge(kd_ready, i * RING + (q + 1))
                        act.sem_inc(act_on, 1)
                        node_hots(nc, act, cs, Lb, hotT, dist, lb_got, hot_ready, (dist_ready, act_on), i, q)

            @block.tensor
            def _(pe):
                pe.sem_inc(kd_ready, RING)
                with pe.Fori(0, cs.loops) as i:
                    for q in range(RING):
                        pe.wait_ge(hot_ready, i * RING + (RING + q + 1))
                        pe.sem_inc(pe_on, 1)
                        pe.wait_ge(multiplied, i * RING + (q + 1))
                        pe.sem_inc(pe_on, 1)
                        for u in range(PB):
                            tile = pe.value_load(cs.tile_of[0:1, bass.ds(i * (TURN) + (q * PB + u), 1)], min_val=0, max_val=NT - 1)
                            ins = pe.matmul(kd[q][:, u * D:(u + 1) * D], hotT[:, q, u * P:(u + 1) * P], K[:, tile, :], start=True, stop=True)
                        ins.then_inc(kd_ready, 1)

            @block.vector
            def _(v):
                v.sem_inc(multiplied, RING)
                v.sem_inc(reduced, 2)
                with v.Fori(0, cs.loops) as i:
                    for q in range(RING):
                        v.wait_ge(got[q], i * (16 * PB) + 16 * PB)
                        v.sem_inc(dve_on, 1)
                        v.wait_ge(reduced, i * RING + (q + 1))
                        v.sem_inc(dve_on, 1)
                        v.wait_ge(kd_ready, i * RING + (RING + q + 1))
                        v.tensor_tensor(prod[:, q % 2, :], kd[q][:], ring[:, q * PB:(q + 1) * PB, :].rearrange("p u d -> p (u d)"),
                                        ALU.mult).then_inc(multiplied, 1)
                        v.wait_ge(multiplied, i * RING + (RING + q + 1))
                        v.sem_inc(dve_on, 1)
                        v.tensor_reduce(S[:, bass.ds(i * (TURN) + q * PB, PB), :].rearrange("p u h -> p (u h)"),
                                        prod[:, q % 2, :].rearrange("p (g d) -> p g d", d=D // H), AX.X, ALU.add).then_inc(reduced, 1)
                v.wait_ge(reduced, cs.loops * RING + 2)


def segment_max(nc, cs, name, S, heads, M, carry_dram):
    B = P // heads
    NB = cs.pairs // B
    R = cs.pairs * heads
    with Phase(nc, name) as ph:
        T = ph.sb("T", [P, NB, P])
        fwd = ph.sb("fwd", [P, NB, P])
        bwd = ph.sb("bwd", [P, NB, P])
        n_start = ph.sb("n_start", [P, NB, P])
        n_end = ph.sb("n_end", [P, NB, P])
        side = ph.sb("side", [P, 4, NB])
        lane0 = ph.sb("lane0", [P, NB])
        lane127 = ph.sb("lane127", [P, NB])
        sideT = ph.sb("sideT", [4 * NB, P])
        line = ph.sb("line", [1, 2, R + 2 * heads])
        cinT = ph.sb("cinT", [2 * NB, P])
        pt = [ph.psum(f"pt{b}", [P, P]) for b in range(4)]
        pc = ph.psum("pc", [P, P])
        keys_in, masked, turned, copied, sides, sideturned, side_out, side_stored, line_in, carried, cin_stored, cin_in, cinturned, joined, back, used, v_link = (
            ph.sem(k) for k in ("keys", "masked", "turned", "copied", "sides", "sideturned", "side_out", "side_stored", "line", "carried",
                                "cin_stored", "cin_in", "cinturned", "joined", "back", "used", "link"))

        def key_view(k):
            return bass.AP(cs.keys_t, k, [[P, B], [0, heads], [B * P, NB], [1, P]])

        flat = "p b l -> p (b l)"
        side_d, cin_d = carry_dram
        with nc.Block() as block:
            @block.sync
            def _(sp):
                for k, dest in enumerate((n_start, fwd, n_end)):
                    for b in range(NB):
                        sp.dma_start(dest[:, b, :], bass.AP(cs.keys_t, k + b * B * P, [[P, B], [0, heads], [1, P]])).then_inc(keys_in, 16)
                sp.wait_ge(side_out, 1)
                sp.dma_start(side_d, sideT[:]).then_inc(side_stored, 16)
                sp.wait_ge(side_stored, 16)
                sp.wait_ge(carried, 1)
                for k in range(2):
                    sp.dma_start(line[:, :, heads:R + heads],
                                 side_d[k * 2 * NB:(k + 1) * 2 * NB, :].rearrange("(a s b) r -> a s (b r)", a=1, s=2)).then_inc(line_in, 16)
                    sp.wait_ge(carried, k + 2)
                    sp.dma_start(cin_d[k * NB:(k + 1) * NB, :].rearrange("(a b) r -> a (b r)", a=1),
                                 line[:, 0, 2 * k * heads:2 * k * heads + R]).then_inc(cin_stored, 16)
                    sp.wait_ge(cin_stored, 16 * (k + 1))
                sp.wait_ge(cin_stored, 32)
                sp.dma_start(cinT[:], cin_d).then_inc(cin_in, 16)

            @block.tensor
            def _(pe):
                pe.wait_ge(masked, 1)
                for b in range(NB):
                    if b >= 4:
                        pe.wait_ge(copied, b - 3)
                    pe.transpose(pt[b % 4][:], S[:, b * B:(b + 1) * B, :].rearrange("p a h -> p (a h)"), cs.ident[:]).then_inc(turned, 1)
                pe.wait_ge(sides, 1)
                pe.transpose(pc[0:4 * NB, :], side[:].rearrange("p s b -> p (s b)"), cs.ident[:]).then_inc(sideturned, 1)
                pe.wait_ge(cin_in, 16)
                pe.wait_ge(side_out, 1)
                pe.transpose(pc[:, 0:2 * NB], cinT[:], cs.ident[0:2 * NB, 0:2 * NB]).then_inc(cinturned, 1)
                pe.wait_ge(joined, 1)
                pe.wait_ge(copied, NB)
                for b in range(NB):
                    if b >= 4:
                        pe.wait_ge(used, b - 3)
                    pe.transpose(pt[b % 4][:], fwd[:, b, :], cs.ident[:]).then_inc(back, 1)

            @block.scalar
            def _(act):
                for b in range(NB):
                    act.wait_ge(turned, b + 1)
                    nc.scalar.copy(T[:, b, :], pt[b % 4][:]).then_inc(copied, 1)
                act.wait_ge(sideturned, 1)
                nc.scalar.copy(sideT[:], pc[0:4 * NB, :]).then_inc(side_out, 1)
                for b in range(NB):
                    act.wait_ge(back, b + 1)
                    nc.scalar.copy(M[:, b * B:(b + 1) * B, :].rearrange("p a h -> p (a h)"), pt[b % 4][:]).then_inc(used, 1)
                act.wait_ge(used, NB)

            @block.vector
            def _(v):
                v.tensor_tensor(S[:], S[:], cs.neg_big[:].unsqueeze(2).to_broadcast([P, cs.pairs, heads]), ALU.add).then_inc(masked, 1)
                link = chain(v, v_link)
                v.wait_ge(keys_in, 48 * NB)
                link(v.tensor_tensor(n_start[:], n_start[:], fwd[:], ALU.not_equal))
                link(v.tensor_tensor(n_end[:], n_end[:], fwd[:], ALU.not_equal))
                link(v.tensor_scalar(n_start[:], n_start[:], -BIG, None, ALU.mult))
                link(v.tensor_scalar(n_end[:], n_end[:], -BIG, None, ALU.mult))
                link(v.tensor_copy(lane0[:], n_start[:, :, 0]))
                link(v.tensor_copy(lane127[:], n_end[:, :, P - 1]))
                link(v.tensor_reduce(side[:, 1, :], n_start[:], AX.X, ALU.min))
                link(v.tensor_reduce(side[:, 3, :], n_end[:], AX.X, ALU.min))
                link(v.memset(n_start[:, :, 0], -BIG))
                link(v.memset(n_end[:, :, P - 1], -BIG))
                v.wait_ge(copied, NB)

                def scans():
                    link(v.tensor_tensor_scan(fwd[:].rearrange(flat), n_start[:].rearrange(flat), T[:].rearrange(flat),
                                              -BIG, ALU.add, ALU.max))
                    link(v.tensor_tensor_scan(bwd[:].rearrange(flat)[:, ::-1], n_end[:].rearrange(flat)[:, ::-1], T[:].rearrange(flat)[:, ::-1],
                                              -BIG, ALU.add, ALU.max))
                scans()
                link(v.tensor_copy(side[:, 0, :], fwd[:, :, P - 1]))
                v.tensor_copy(side[:, 2, :], bwd[:, :, 0]).then_inc(sides, 1)
                link(v.memset(line[:], -BIG))
                v.sem_inc(carried, 1)
                for k in range(2):
                    v.wait_ge(line_in, 16 * (k + 1))
                    way = 1 - 2 * k
                    for h in range(heads):
                        of = lambda r: line[:, r, heads:R + heads].rearrange("a (r h) -> a h r", h=heads)[:, h, ::way]
                        link(v.tensor_tensor_scan(of(0), of(1), of(0), -BIG, ALU.add, ALU.max))
                    v.sem_inc(carried, 1)
                v.wait_ge(cinturned, 1)
                link(v.tensor_tensor(lane0[:], lane0[:], pc[:, 0:NB], ALU.add))
                link(v.tensor_tensor(lane127[:], lane127[:], pc[:, NB:2 * NB], ALU.add))
                link(v.tensor_tensor(T[:, :, 0], T[:, :, 0], lane0[:], ALU.max))
                link(v.tensor_tensor(T[:, :, P - 1], T[:, :, P - 1], lane127[:], ALU.max))
                scans()
                v.tensor_tensor(fwd[:], fwd[:], bwd[:], ALU.max).then_inc(joined, 1)


def edge_weights(nc, name, S, M, Wt):
    with Phase(nc, name) as ph:
        shifted = ph.sem("shifted")
        raised = ph.sem("raised")
        with nc.Block() as block:
            @block.vector
            def _(v):
                v.tensor_tensor(S[:], S[:], M[:], ALU.subtract).then_inc(shifted, 1)

            @block.scalar
            def _(act):
                act.wait_ge(shifted, 1)
                nc.scalar.activation(Wt, S[:], ACT.Exp).then_inc(raised, 1)
                act.wait_ge(raised, 1)


def lane_hots(nc, act, cs, hot, dist, hot_free, hot_ready, dist_ready, act_on):
    with act.Fori(0, cs.loops) as i:
        for q in range(RING):
            act.wait_ge(hot_free, i * RING + (q + 1))
            act.sem_inc(act_on, 1)
            for u in range(PB):
                p = i * (TURN) + (q * PB + u)
                ins = nc.scalar.activation(dist[:, q, u, :], cs.count_row[:, 0:TN], ACT.Abs, bias=cs.neg_local[:, bass.ds(p, 1)])
            ins.then_inc(dist_ready, 1)
            act.wait_ge(dist_ready, i * RING + (q + 1))
            nc.scalar.activation(hot[:, q, :, :], dist[:, q, :, :], ACT.Relu, scale=-1.0, bias=1.0).then_inc(hot_ready, 1)


def weigh_values(nc, cs, v_dram, Wt, acc):
    C = D + H + 1
    with Phase(nc, "value") as ph:
        ring = ph.sb("ring", [P, TURN, D])
        idx = ph.sb("idx", [P, RING, PB], I32)
        hot = ph.sb("hot", [P, RING, PB, TN])
        dist = ph.sb("dist", [P, RING, PB, TN])
        wv = ph.sb("wv", [P, RING, PB, D])
        part = [ph.psum(f"part{u}", [TN, 512]) for u in range(2 * PB)]
        idx_ready, hot_ready, weighed, summed, added, dist_ready, pool_on, act_on, pe_on, dve_on = (
            ph.sem(k) for k in ("idx", "hot", "weighed", "summed", "added", "dist", "pool_on", "act_on", "pe_on", "dve_on"))
        cleared = ph.sem("cleared")
        got = [ph.sem(f"got{q}") for q in range(RING)]
        HB = PB // 2
        with nc.Block() as block:
            @block.gpsimd
            def _(g):
                gather_pairs(g, cs, v_dram, ring, idx, idx_ready, weighed, got, pool_on)

            @block.scalar
            def _(act):
                lane_hots(nc, act, cs, hot, dist, summed, hot_ready, dist_ready, act_on)

            @block.vector
            def _(v):
                v.memset(acc[:], 0.0).then_inc(cleared, 1)
                v.wait_ge(cleared, 1)
                v.sem_inc(weighed, RING)
                v.sem_inc(added, 2 * PB)
                with v.Fori(0, cs.loops) as i:
                    for q in range(RING):
                        v.wait_ge(got[q], i * (16 * PB) + 16 * PB)
                        v.sem_inc(dve_on, 1)
                        v.wait_ge(summed, i * RING + (q + 1))
                        v.sem_inc(dve_on, 1)
                        w = Wt[:, bass.ds(i * (TURN) + q * PB, PB), 0:H]
                        v.tensor_tensor(wv[:, q, :, :].rearrange("p u (h d) -> p u h d", h=H),
                                        ring[:, q * PB:(q + 1) * PB, :].rearrange("p u (h d) -> p u h d", h=H),
                                        w.unsqueeze(3).to_broadcast([P, PB, H, D // H]), ALU.mult).then_inc(weighed, 1)
                        for u in range(PB):
                            pp = i * (TURN) + (q * PB + u)
                            tile = v.value_load(cs.tile_of[0:1, bass.ds(pp, 1)], min_val=0, max_val=NT - 1)
                            v.wait_ge(added, pp + 2 * PB)
                            v.sem_inc(dve_on, 1)
                            if u == 0:
                                v.wait_ge(summed, i * RING + (RING + q + 1))
                                v.sem_inc(dve_on, 1)
                            v.tensor_tensor(acc[:, tile, :], acc[:, tile, :], part[(q % 2) * PB + u][:, 0:C], ALU.add).then_inc(added, 1)
                v.wait_ge(added, cs.pairs + 2 * PB)

            @block.tensor
            def _(pe):
                pe.sem_inc(summed, RING)
                with pe.Fori(0, cs.loops) as i:
                    for q in range(RING):
                        pe.wait_ge(hot_ready, i * RING + (q + 1))
                        pe.sem_inc(pe_on, 1)
                        pe.wait_ge(weighed, i * RING + (RING + q + 1))
                        pe.sem_inc(pe_on, 1)
                        pe.wait_ge(added, i * (TURN) + (q * PB + PB))
                        pe.sem_inc(pe_on, 1)
                        for u in range(PB):
                            p = i * (TURN) + (q * PB + u)
                            out = part[(q % 2) * PB + u]
                            pe.matmul(out[:, 0:D], hot[:, q, u, :], wv[:, q, u, :], start=True, stop=True)
                            ins = pe.matmul(out[:, D:C], hot[:, q, u, :], Wt[:, p, :], start=True, stop=True)
                        ins.then_inc(summed, 1)


def neighbour_sums(nc, name, cs, table, width, acc, bias_rows=None):
    per_bank = 512 // width
    with Phase(nc, name) as ph:
        ring = ph.sb("ring", [P, TURN, width])
        idx = ph.sb("idx", [P, RING, PB], I32)
        hot = ph.sb("hot", [P, RING, PB, TN])
        dist = ph.sb("dist", [P, RING, PB, TN])
        zero = ph.sb("zero", [1, 512])
        idx_ready, hot_ready, summed, dist_ready, zeroed, pool_on, act_on, pe_on = (
            ph.sem(k) for k in ("idx", "hot", "summed", "dist", "zeroed", "pool_on", "act_on", "pe_on"))
        got = [ph.sem(f"got{q}") for q in range(RING)]
        with nc.Block() as block:
            @block.vector
            def _(v):
                v.memset(zero[:], 0.0).then_inc(zeroed, 1)

            @block.gpsimd
            def _(g):
                gather_pairs(g, cs, table, ring, idx, idx_ready, summed, got, pool_on)

            @block.scalar
            def _(act):
                lane_hots(nc, act, cs, hot, dist, summed, hot_ready, dist_ready, act_on)

            @block.tensor
            def _(pe):
                pe.wait_ge(zeroed, 1)
                for b in range((NT + per_bank - 1) // per_bank):
                    pe.matmul(acc[:, b * 512:(b + 1) * 512], zero[:, 0:TN], zero[:], start=True, stop=True)
                pe.sem_inc(summed, RING)
                with pe.Fori(0, cs.loops) as i:
                    for q in range(RING):
                        pe.wait_ge(hot_ready, i * RING + (q + 1))
                        pe.sem_inc(pe_on, 1)
                        pe.wait_ge(got[q], i * (16 * PB) + 16 * PB)
                        pe.sem_inc(pe_on, 1)
                        for u in range(PB):
                            p = i * (TURN) + (q * PB + u)
                            tile = pe.value_load(cs.tile_of[0:1, bass.ds(p, 1)], min_val=0, max_val=NT - 1)
                            ins = pe.matmul(acc[:, bass.ds(tile * width, width)], hot[:, q, u, :], ring[:, q * PB + u, :],
                                            start=False, stop=True, skip_group_check=True)
                        ins.then_inc(summed, 1)
                pe.wait_ge(summed, cs.loops * RING + RING)


def experts(nc, name, cs, UT, Y, gates, w1, b1, w2, b2, n_experts, func):
    F = 512
    FT = F // P
    CT = 5
    CW = CT * TN
    halves = [(0, 313), (313, CW)]
    with Phase(nc, name) as ph:
        W1 = ph.sb("W1", [P, 2, 2, F])
        W2 = ph.sb("W2", [P, 2, FT, D])
        B2 = ph.sb("B2", [TN, 2, D])
        brow = ph.sb("brow", [n_experts * FT, P])
        bcol = ph.sb("bcol", [P, n_experts * FT])
        hidden = ph.sb("hidden", [P, 2, FT, CW])
        plus = ph.sb("plus", [TN, 2, D])
        hp = [ph.psum(f"hp{k}", [P, 2, 512]) for k in range(2)]
        yp = [ph.psum(f"yp{k}", [TN, D]) for k in range(2)]
        bp = ph.psum("bp", [P, n_experts * FT])
        b_in, b_turned, b_ready, up, acted, down, added, biased, act_on, sp_on, dve_on = (
            ph.sem(k) for k in ("b_in", "b_turned", "b_ready", "up", "acted", "down", "added", "biased", "act_on", "sp_on", "dve_on"))
        w_in = [ph.sem(f"w_in{k}") for k in range(2)]
        NW = 3 if b2 is not None else 2
        C = 50
        with nc.Block() as block:
            @block.sync
            def _(sp):
                sp.dma_start(brow[:], b1.rearrange("e (f p) -> (e f) p", p=P)).then_inc(b_in, 16)
                with sp.Fori(0, n_experts // 2) as i:
                    for k in range(2):
                        sp.wait_ge(down, i * 50 + (25 * k + 25))
                        sp.sem_inc(sp_on, 1)
                        if b2 is not None:
                            sp.wait_ge(biased, i * 50 + (25 * k + 25))
                            sp.sem_inc(sp_on, 1)
                        e = i * 2 + k
                        sp.dma_start(W1[:, k, :, :], w1[bass.ds(e, 1), :, :].rearrange("e (c p) f -> p (e c) f", p=P)).then_inc(w_in[k], 16)
                        sp.dma_start(W2[:, k, :, :], w2[bass.ds(e, 1), :, :].rearrange("e (c p) d -> p (e c) d", p=P)).then_inc(w_in[k], 16)
                        if b2 is not None:
                            sp.dma_start(B2[:, k, :], b2[bass.ds(e, 1), :].rearrange("e d -> (e d)").partition_broadcast(TN)).then_inc(w_in[k], 16)

            @block.tensor
            def _(pe):
                pe.wait_ge(b_in, 16)
                pe.transpose(bp[:], brow[:], cs.ident[0:n_experts * FT, 0:n_experts * FT]).then_inc(b_turned, 1)
                pe.sem_inc(down, C)
                with pe.Fori(0, n_experts // 2) as i:
                    for k in range(2):
                        pe.wait_ge(w_in[k], i * (16 * NW) + 16 * NW)
                        pe.sem_inc(sp_on, 1)
                        for c in range(5):
                            n = 5 * k + c
                            for f in range(FT):
                                pe.wait_ge(acted, i * 40 + (n * FT + f + 1))
                                for (lo, hi) in halves:
                                    for kk in range(2):
                                        ins = pe.matmul(hp[f % 2][:, lo // 313, 0:hi - lo], W1[:, k, kk, f * P:(f + 1) * P],
                                                        UT[:, kk, c * CW + lo:c * CW + hi], start=(kk == 0), stop=(kk == 1))
                                ins.then_inc(up, 1)
                            pe.wait_ge(acted, i * 40 + (n * FT + FT + 2))
                            for t in range(CT):
                                m = n * CT + t
                                pe.wait_ge(added, i * 50 + (m + 1))
                                for f in range(FT):
                                    ins = pe.matmul(yp[m % 2][:], hidden[:, n % 2, f, t * TN:(t + 1) * TN], W2[:, k, f, :],
                                                    start=(f == 0), stop=(f == FT - 1))
                                ins.then_inc(down, 1)

            @block.scalar
            def _(act):
                act.sem_inc(acted, 2)
                with act.Fori(0, n_experts // 2) as i:
                    for n in range(10):
                        act.wait_ge(down, i * 50 + (5 * n + C - 5))
                        act.sem_inc(act_on, 1)
                        if n == 0:
                            act.wait_ge(b_ready, 1)
                        for f in range(FT):
                            act.wait_ge(up, i * 40 + (n * FT + f + 1))
                            act.sem_inc(act_on, 1)
                            bias = bcol[:, bass.ds(i * (2 * FT) + ((n // 5) * FT + f), 1)]
                            for (lo, hi) in halves:
                                ins = nc.scalar.activation(hidden[:, n % 2, f, lo:hi], hp[f % 2][:, lo // 313, 0:hi - lo], func, bias=bias)
                            ins.then_inc(acted, 1)

            @block.vector
            def _(v):
                v.wait_ge(b_turned, 1)
                v.tensor_copy(bcol[:], bp[:]).then_inc(b_ready, 1)
                v.sem_inc(added, 2)
                v.sem_inc(biased, C)
                with v.Fori(0, n_experts // 2) as i:
                    for m in range(50):
                        v.wait_ge(down, i * 50 + (m + 1 + C))
                        k, t = m // 25, m % 25
                        y = yp[m % 2][:]
                        if b2 is not None:
                            v.tensor_tensor(plus[:, m % 2, :], y, B2[:, k, :], ALU.add).then_inc(biased, 1)
                            v.wait_ge(biased, i * 50 + (m + 1 + C))
                            y = plus[:, m % 2, :]
                        v.sem_inc(dve_on, 1)
                        v.scalar_tensor_tensor(out=Y[:, t, :], in0=y, scalar=gates[:, t, bass.ds(i * 2 + k, 1)], in1=Y[:, t, :],
                                               op0=ALU.mult, op1=ALU.add).then_inc(added, 1)
                v.wait_ge(added, n_experts * 25 + 2)


def table_rows(table):
    return table.rearrange("(t p) w -> p t w", p=TN)


def move(nc, name, pairs):
    with Phase(nc, name) as ph:
        moved = ph.sem("moved")
        with nc.Block() as block:
            @block.sync
            def _(sp):
                for to, of in pairs:
                    sp.dma_start(to, of).then_inc(moved, 16)
                sp.wait_ge(moved, 16 * len(pairs))


def vector_steps(nc, name, steps, loads=()):
    with Phase(nc, name) as ph:
        link_s, asked, answered, loaded = (ph.sem(k) for k in ("link", "asked", "answered", "loaded"))
        asks = []
        with nc.Block() as block:
            @block.sync
            def _(sp):
                for to, of in loads:
                    sp.dma_start(to, of).then_inc(loaded, 16)
                if loads:
                    sp.wait_ge(loaded, 16 * len(loads))

            @block.vector
            def _(v):
                if loads:
                    v.wait_ge(loaded, 16 * len(loads))

                def act_do(*a):
                    asks.append(a)
                    v.sem_inc(asked, 1)
                    v.wait_ge(answered, len(asks))
                steps(v, chain(v, link_s), act_do)

            @block.scalar
            def _(act):
                for n, (out, in_, func) in enumerate(asks):
                    act.wait_ge(asked, n + 1)
                    nc.scalar.activation(out, in_, func).then_inc(answered, 1)


def top2_gates(nc, name, cs, scores, n, gates):
    W = scores.shape[2]
    with Phase(nc, name + "_b") as ph:
        best = ph.sb("best", [TN, NT, 8])
        at_i = ph.sb("at_i", [TN, NT, 8], U32)
        at = ph.sb("at", [TN, NT, 8])
        diff, rest = (ph.sb(k, [TN, NT]) for k in ("diff", "rest"))
        hot = ph.sb("hot", [TN, NT, n])

        def steps(v, link, act_do):
            for t in range(NT):
                link(v.max(best[:, t, :], scores[:, t, :]))
                link(v.max_index(at_i[:, t, :], best[:, t, :], scores[:, t, :]))
            link(v.tensor_copy(at[:], at_i[:]))
            link(v.tensor_tensor(diff[:], best[:, :, 1], best[:, :, 0], ALU.subtract))
            act_do(diff[:], diff[:], ACT.Exp)
            link(v.tensor_scalar(rest[:], diff[:], 1.0, None, ALU.add))
            link(v.reciprocal(rest[:], rest[:]))
            link(v.tensor_tensor(diff[:], diff[:], rest[:], ALU.mult))
            number = cs.count_row[0:TN, 0:n].unsqueeze(1).to_broadcast([TN, NT, n])
            wide = lambda a: a.unsqueeze(2).to_broadcast([TN, NT, n])
            link(v.tensor_tensor(hot[:], number, wide(at[:, :, 0]), ALU.is_equal))
            link(v.tensor_tensor(gates[:], hot[:], wide(rest[:]), ALU.mult))
            link(v.tensor_tensor(hot[:], number, wide(at[:, :, 1]), ALU.is_equal))
            link(v.tensor_tensor(hot[:], hot[:], wide(diff[:]), ALU.mult))
            link(v.tensor_tensor(gates[:], gates[:], hot[:], ALU.add))
        vector_steps(nc, name, steps)


def take_sums(nc, name, acc, rows, dinv, width):
    def steps(v, link, act_do):
        link(v.tensor_tensor(rows[:], acc[:, 0:NT * width].rearrange("p (t w) -> p t w", w=width), rows[:], ALU.add))
        link(v.tensor_tensor(rows[:], rows[:], dinv[:].unsqueeze(2).to_broadcast([TN, NT, width]), ALU.mult))
    vector_steps(nc, name, steps)


def batch_norm(nc, name, cs, rows, bias, gamma, beta, width, XT):
    with Phase(nc, name) as ph:
        cols = ph.sb("cols", [width, 3])
        parts = ph.sb("parts", [width, 7, 6])
        ms = ph.sb("ms", [width, 2])
        scale, move_ = ph.sb("scale", [width, 1]), ph.sb("shift", [width, 1])
        tp = [ph.psum(f"tp{k}", [width, TN]) for k in range(4)]
        loaded, turned, copied, link_s, asked, answered, relu = (
            ph.sem(k) for k in ("loaded", "turned", "copied", "link", "asked", "answered", "relu"))
        with nc.Block() as block:
            @block.sync
            def _(sp):
                for k, a in enumerate((bias, gamma, beta)):
                    sp.dma_start(cols[:, k:k + 1], a.rearrange("(p a) -> p a", a=1)).then_inc(loaded, 16)
                sp.wait_ge(loaded, 48)

            @block.vector
            def _(v):
                v.wait_ge(loaded, 48)
                v.wait_ge(copied, NT)
                link = chain(v, link_s)
                for k in range(7):
                    lo, hi = k * 500, min(N, k * 500 + 500)
                    link(v.bn_stats(out=parts[:, k, :], in_=XT[:, lo:hi]))
                link(v.bn_aggr(out=ms[:], in_=parts[:].rearrange("p k s -> p (k s)")))
                link(v.tensor_scalar(ms[:, 1:2], ms[:, 1:2], EPS, None, ALU.add))
                v.sem_inc(asked, 1)
                v.wait_ge(answered, 1)
                link(v.reciprocal(scale[:], ms[:, 1:2]))
                link(v.tensor_tensor(scale[:], scale[:], cols[:, 1:2], ALU.mult))
                link(v.scalar_tensor_tensor(out=move_[:], in0=scale[:], scalar=ms[:, 0:1], in1=cols[:, 2:3], op0=ALU.mult, op1=ALU.subtract))
                link(v.tensor_scalar(move_[:], move_[:], -1.0, None, ALU.mult))
                v.sem_inc(asked, 1)

            @block.tensor
            def _(pe):
                for t in range(NT):
                    if t >= 4:
                        pe.wait_ge(copied, t - 3)
                    pe.transpose(tp[t % 4][:], rows[:, t, :], cs.ident[0:TN, 0:TN]).then_inc(turned, 1)

            @block.scalar
            def _(act):
                act.wait_ge(loaded, 48)
                for t in range(NT):
                    act.wait_ge(turned, t + 1)
                    nc.scalar.activation(XT[:, t * TN:(t + 1) * TN], tp[t % 4][:], ACT.Identity, bias=cols[:, 0:1]).then_inc(copied, 1)
                act.wait_ge(asked, 1)
                nc.scalar.activation(ms[:, 1:2], ms[:, 1:2], ACT.Sqrt).then_inc(answered, 1)
                act.wait_ge(asked, 2)
                nc.scalar.activation(XT[:], XT[:], ACT.Relu, scale=scale[:], bias=move_[:]).then_inc(relu, 1)
                act.wait_ge(relu, 1)


def from_features(nc, name, groups, cols, finish, loads):
    with Phase(nc, name) as ph:
        ps = [ph.psum(f"ps{k}", [TN, 512]) for k in range(4)]
        loaded, summed, finished, link_s = (ph.sem(k) for k in ("loaded", "summed", "finished", "link"))
        with nc.Block() as block:
            @block.sync
            def _(sp):
                for to, of in loads:
                    sp.dma_start(to, of).then_inc(loaded, 16)
                sp.wait_ge(loaded, 16 * len(loads))

            @block.tensor
            def _(pe):
                pe.wait_ge(loaded, 16 * len(loads))
                for t in range(NT):
                    if t >= 4:
                        pe.wait_ge(finished, t - 3)
                    for k, (XT, W) in enumerate(groups):
                        ins = pe.matmul(ps[t % 4][:, 0:cols], XT[:, t * TN:(t + 1) * TN], W, start=(k == 0), stop=(k == len(groups) - 1))
                    ins.then_inc(summed, 1)

            @block.vector
            def _(v):
                v.wait_ge(loaded, 16 * len(loads))
                link = chain(v, link_s)
                for t in range(NT):
                    v.wait_ge(summed, t + 1)
                    finish(v, link, t, ps[t % 4][:, 0:cols]).then_inc(finished, 1)
                v.wait_ge(finished, NT)


def gat_scores(nc, cs, table, AD, GT, S):
    C = GH * GE + GH
    with Phase(nc, "gscore") as ph:
        ring = ph.sb("ring", [P, TURN, C])
        idx = ph.sb("idx", [P, RING, PB], I32)
        Lb = ph.sb("Lb", [TN, RING, PB * P])
        hotT = ph.sb("hotT", [TN, RING, PB * P])
        dist = ph.sb("dist", [TN, RING, PB * P])
        ad = [ph.psum(f"ad{q}", [P, PB, GH]) for q in range(RING)]
        idx_ready, hot_ready, ad_ready, taken, dist_ready, pool_on, sp_on, act_on, pe_on, dve_on, leaked = (
            ph.sem(k) for k in ("idx", "hot", "ad", "taken", "dist", "pool_on", "sp_on", "act_on", "pe_on", "dve_on", "leaked"))
        got = [ph.sem(f"got{q}") for q in range(RING)]
        lb_got = [ph.sem(f"lb{q}") for q in range(RING)]
        with nc.Block() as block:
            @block.gpsimd
            def _(g):
                gather_pairs(g, cs, table, ring, idx, idx_ready, taken, got, pool_on)

            @block.sync
            def _(sp):
                load_local_rows(sp, cs, Lb, lb_got, hot_ready, sp_on)

            @block.scalar
            def _(act):
                act.sem_inc(hot_ready, RING)
                with act.Fori(0, cs.loops) as i:
                    for q in range(RING):
                        act.wait_ge(ad_ready, i * RING + (q + 1))
                        act.sem_inc(act_on, 1)
                        node_hots(nc, act, cs, Lb, hotT, dist, lb_got, hot_ready, (dist_ready, act_on), i, q)

            @block.tensor
            def _(pe):
                pe.sem_inc(ad_ready, RING)
                with pe.Fori(0, cs.loops) as i:
                    for q in range(RING):
                        pe.wait_ge(hot_ready, i * RING + (RING + q + 1))
                        pe.sem_inc(pe_on, 1)
                        pe.wait_ge(taken, i * RING + (q + 1))
                        pe.sem_inc(pe_on, 1)
                        for u in range(PB):
                            tile = pe.value_load(cs.tile_of[0:1, bass.ds(i * (TURN) + (q * PB + u), 1)], min_val=0, max_val=NT - 1)
                            ins = pe.matmul(ad[q][:, u, :], hotT[:, q, u * P:(u + 1) * P], AD[:, tile, :], start=True, stop=True)
                        ins.then_inc(ad_ready, 1)

            @block.vector
            def _(v):
                v.sem_inc(taken, RING)
                with v.Fori(0, cs.loops) as i:
                    for q in range(RING):
                        v.wait_ge(got[q], i * (16 * PB) + 16 * PB)
                        v.sem_inc(dve_on, 1)
                        batch = bass.ds(i * (TURN) + q * PB, PB)
                        part = ring[:, q * PB:(q + 1) * PB, :]
                        v.tensor_copy(GT[:, batch, :], part)
                        v.wait_ge(ad_ready, i * RING + (RING + q + 1))
                        v.sem_inc(dve_on, 1)
                        v.tensor_tensor(S[:, batch, :], ad[q][:], part[:, :, GH * GE:C], ALU.add).then_inc(taken, 1)
                v.wait_ge(taken, cs.loops * RING + RING)
                v.scalar_tensor_tensor(out=S[:], in0=S[:], scalar=0.2, in1=S[:], op0=ALU.mult, op1=ALU.max).then_inc(leaked, 1)
                v.wait_ge(leaked, 1)


def gat_sums(nc, cs, RW, acc):
    C = RW.shape[2]
    with Phase(nc, "gsum") as ph:
        hot = ph.sb("hot", [P, RING, PB, TN])
        zero = ph.sb("zero", [1, 512])
        hot_ready, summed, zeroed, pe_on, dve_on = (ph.sem(k) for k in ("hot", "summed", "zeroed", "pe_on", "dve_on"))
        with nc.Block() as block:
            @block.vector
            def _(v):
                v.memset(zero[:], 0.0).then_inc(zeroed, 1)
                with v.Fori(0, cs.loops) as i:
                    for q in range(RING):
                        v.wait_ge(summed, i * RING + (q + 1))
                        v.sem_inc(dve_on, 1)
                        own = cs.local[:, bass.ds(i * (TURN) + q * PB, PB)]
                        v.tensor_tensor(hot[:, q, :, :], cs.count_row[:, 0:TN].unsqueeze(1).to_broadcast([P, PB, TN]),
                                        own.unsqueeze(2).to_broadcast([P, PB, TN]), ALU.is_equal).then_inc(hot_ready, 1)

            @block.tensor
            def _(pe):
                pe.wait_ge(zeroed, 1)
                for b in range(2):
                    pe.matmul(acc[:, b * 512:(b + 1) * 512], zero[:, 0:TN], zero[:], start=True, stop=True)
                pe.sem_inc(summed, RING)
                with pe.Fori(0, cs.loops) as i:
                    for q in range(RING):
                        pe.wait_ge(hot_ready, i * RING + (q + 1))
                        pe.sem_inc(pe_on, 1)
                        for u in range(PB):
                            p = i * (TURN) + (q * PB + u)
                            tile = pe.value_load(cs.tile_of[0:1, bass.ds(p, 1)], min_val=0, max_val=NT - 1)
                            ins = pe.matmul(acc[:, bass.ds(tile * 32, C)], hot[:, q, u, :], RW[:, p, :],
                                            start=False, stop=True, skip_group_check=True)
                        ins.then_inc(summed, 1)
                pe.wait_ge(summed, cs.loops * RING + RING)


def build(nc, a, out):
    with ExitStack() as ctx:
        def sb(name, shape, dt=F32, c=ctx):
            return c.enter_context(nc.sbuf_tensor(name, shape, dt))

        def dram(name, shape):
            return nc.dram_tensor(name, shape, F32)

        cs = Consts(sb)
        g1 = Graph("g1", sb, dram, cs, E1)
        g2 = Graph("g2", sb, dram, cs, E2)
        sorted_edges = nc.dram_tensor("sorted_edges", [E2, 2], I32).ap()
        q_dram, v_dram, h1_dram, h2_dram, g_dram = (dram(k, [N, w]).ap() for k, w in (
            ("q_rows", D), ("v_rows", D), ("h1_rows", 128), ("h2_rows", 64), ("g_rows", GH * GE + GH)))
        carries = {h: (dram(f"side{h}", [4 * pairs * h // P, P]).ap(), dram(f"cin{h}", [2 * pairs * h // P, P]).ap())
                   for h, pairs in ((H, g1.pairs), (GH, g2.pairs))}

        X = sb("X", [TN, NT, D])
        rstd, shift = sb("rstd", [TN, NT]), sb("shift", [TN, NT])
        dinv = sb("dinv", [TN, NT])

        constants(nc, cs)
        index_tables(nc, g1, a["src"], a["dst"])
        sort_edges(nc, cs, a["L1_ffn_edge_index"], sorted_edges)
        index_tables(nc, g2, joined=sorted_edges)
        move(nc, "in", [(X[:], table_rows(a["x"]))])

        with ExitStack() as l1:
            T = sb("T", [TN, NT, D], c=l1)
            with ExitStack() as att:
                S = sb("S", [P, g1.pairs, H], c=att)
                row_stats(nc, "st0", X, rstd, shift)
                normalise(nc, "nm0", X, rstd, shift, T)
                row_stats(nc, "st1", T, rstd, shift)
                with ExitStack() as kq:
                    K = sb("K", [TN, NT, D], c=kq)
                    with ExitStack() as qv:
                        Q, V = sb("Q", [TN, NT, D], c=qv), sb("V", [TN, NT, D], c=qv)
                        BQ = sb("BQ", [TN, 3 * D], c=qv)
                        SCALE = D ** -0.5

                        def scale_bq(v, link, act_do):
                            link(v.tensor_scalar(BQ[:, 0:D], BQ[:, 0:D], SCALE, None, ALU.mult))
                        vector_steps(nc, "bq", scale_bq, [(BQ[:], a["L0_gnn_bqkv"].partition_broadcast(TN))])

                        def finish(v, j, tile, s, ps):
                            if j == 0:
                                v.scalar_tensor_tensor(out=Q[:, tile, :], in0=ps[:, 0:D], scalar=SCALE, in1=BQ[:, 0:D], op0=ALU.mult, op1=ALU.add)
                                return v.tensor_tensor(K[:, tile, :], ps[:, D:2 * D], BQ[:, D:2 * D], ALU.add)
                            return v.tensor_tensor(V[:, tile, :], ps, BQ[:, 2 * D:3 * D], ALU.add)
                        project(nc, "qkv", cs, T, rstd, shift, a["L0_gnn_Wqkv"], [(0, 512), (512, 256)], finish,
                                affine=(a["L0_gnn_ln_attn_g"], a["L0_gnn_ln_attn_b"]))
                        move(nc, "qv", [(table_rows(q_dram), Q[:]), (table_rows(v_dram), V[:])])
                    edge_scores(nc, g1, q_dram, K, S)
                with ExitStack() as mw:
                    M = sb("M", [P, g1.pairs, H], c=mw)
                    segment_max(nc, g1, "max8", S, H, M, carries[H])
                    Wt = sb("Wt", [P, g1.pairs, H + 1], c=mw)
                    edge_weights(nc, "w8", S, M, Wt[:, :, 0:H])

                    def one_column(v, link, act_do):
                        link(v.memset(Wt[:, :, H], 1.0))
                    vector_steps(nc, "one", one_column)
                    acc = sb("acc", [TN, NT, D + H + 1], c=mw)
                    weigh_values(nc, g1, v_dram, Wt, acc)

                    def combine(v, link, act_do):
                        w = acc[:, :, D:D + H]
                        link(v.tensor_scalar(w, w, 0.5, None, ALU.max))
                        link(v.reciprocal(w, w))
                        val = acc[:, :, 0:D].rearrange("p t (h d) -> p t h d", h=H)
                        link(v.tensor_tensor(val, val, w.unsqueeze(3).to_broadcast([TN, NT, H, D // H]), ALU.mult))
                        link(v.tensor_tensor(T[:], T[:], acc[:, :, 0:D], ALU.add))
                        link(v.tensor_scalar(dinv[:], acc[:, :, D + H], 1.0, None, ALU.add))
                        act_do(dinv[:], dinv[:], ACT.Sqrt)
                        link(v.reciprocal(dinv[:], dinv[:]))
                    vector_steps(nc, "comb", combine)
            with ExitStack() as ff:
                UT = sb("UT0", [P, 2, N], c=ff)
                bo = sb("bo", [TN, D], c=ff)
                gate1 = sb("gate1", [TN, NT, 2], c=ff)
                row_stats(nc, "st2", T, rstd, shift)
                project(nc, "ln2", cs, T, rstd, shift, None, [], None,
                        affine=(a["L0_gnn_ln_res_g"], a["L0_gnn_ln_res_b"]), UT=UT)

                def start(v, link, act_do):
                    link(v.memset(gate1[:], 1.0))
                    link(v.tensor_tensor(X[:], X[:], T[:], ALU.add))
                    link(v.tensor_tensor(X[:], X[:], bo[:].unsqueeze(1).to_broadcast([TN, NT, D]), ALU.add))
                vector_steps(nc, "y0", start, [(bo[:], a["L0_gnn_b_out"].partition_broadcast(TN))])
                w_in = a["L0_gnn_W_in"].rearrange("d (e f) -> e d f", e=2)
                experts(nc, "ff0", cs, UT, X, gate1, w_in, a["L0_gnn_b_in"].rearrange("(e f) -> e f", e=2),
                        a["L0_gnn_W_out"].rearrange("(e f) d -> e f d", e=2), None, 2, ACT.Gelu)
        with ExitStack() as moe:
            UT = sb("UT1", [P, 2, N], c=moe)
            Y = sb("Y1", [TN, NT, D], c=moe)
            logits, gates = sb("logits", [TN, NT, 16], c=moe), sb("gates", [TN, NT, 16], c=moe)
            gb = sb("gb", [TN, 3 * D], c=moe)
            row_stats(nc, "st3", X, rstd, shift)
            move(nc, "gb", [(gb[:, 0:16], a["L0_ffn_gate_b"].partition_broadcast(TN)),
                            (gb[:, D:2 * D], a["L0_ffn_gamma"].partition_broadcast(TN)),
                            (gb[:, 2 * D:3 * D], a["L0_ffn_beta"].partition_broadcast(TN))])
            project(nc, "gate", cs, X, rstd, shift, a["L0_ffn_gate_w"], [(0, 16)],
                    lambda v, j, tile, s, ps: v.tensor_tensor(logits[:, tile, :], ps, gb[:, 0:16], ALU.add),
                    UT=UT, rows_out=Y)
            top2_gates(nc, "top16", cs, logits, 16, gates)
            experts(nc, "moe", cs, UT, Y, gates, a["L0_ffn_w1"], a["L0_ffn_b1"], a["L0_ffn_w2"], a["L0_ffn_b2"], 16, ACT.Relu)
            row_stats(nc, "st4", Y, rstd, shift)
            normalise(nc, "nm4", Y, rstd, shift, Y)

            def add_moe(v, link, act_do):
                wide = lambda k: gb[:, k * D:(k + 1) * D].unsqueeze(1).to_broadcast([TN, NT, D])
                link(v.tensor_tensor(Y[:], Y[:], wide(1), ALU.mult))
                link(v.tensor_tensor(Y[:], Y[:], wide(2), ALU.add))
                link(v.tensor_tensor(X[:], X[:], Y[:], ALU.add))
            vector_steps(nc, "addm", add_moe)
        with ExitStack() as gcn:
            UT = sb("UT2", [P, 2, N], c=gcn)
            H1 = sb("H1", [TN, NT, 128], c=gcn)
            H2 = sb("H2", [TN, NT, 64], c=gcn)
            XT1 = sb("XT1", [128, N], c=gcn)
            XT2 = sb("XT2", [64, N], c=gcn)
            W2, Wfc, Wfc2 = sb("gW2", [128, 64], c=gcn), sb("Wfc", [P, 3, D], c=gcn), sb("Wfc2", [64, D], c=gcn)
            bfc = sb("bfc", [TN, D], c=gcn)
            relu = sb("relu", [TN, 4, D], c=gcn)
            row_stats(nc, "st5", X, rstd, shift)
            project(nc, "gc1", cs, X, rstd, shift, a["L1_gnn_W1"], [(0, 128)],
                    lambda v, j, tile, s, ps: v.tensor_scalar(H1[:, tile, :], ps, dinv[:, bass.ds(tile, 1)], None, ALU.mult),
                    UT=UT)
            move(nc, "h1", [(table_rows(h1_dram), H1[:])])
            with nc.psum_tensor("acc1", [TN, 7 * 512], F32) as acc1:
                neighbour_sums(nc, "sum1", g1, h1_dram, 128, acc1)
                take_sums(nc, "take1", acc1, H1, dinv, 128)
            batch_norm(nc, "bn1", cs, H1, a["L1_gnn_b1"], a["L1_gnn_g1"], a["L1_gnn_be1"], 128, XT1)
            from_features(nc, "gc2", [(XT1, W2[:])], 64,
                          lambda v, link, t, ps: v.tensor_scalar(H2[:, t, :], ps, dinv[:, t:t + 1], None, ALU.mult),
                          [(W2[:], a["L1_gnn_W2"])])
            move(nc, "h2", [(table_rows(h2_dram), H2[:])])
            with nc.psum_tensor("acc2", [TN, 4 * 512], F32) as acc2:
                neighbour_sums(nc, "sum2", g1, h2_dram, 64, acc2)
                take_sums(nc, "take2", acc2, H2, dinv, 64)
            batch_norm(nc, "bn2", cs, H2, a["L1_gnn_b2"], a["L1_gnn_g2"], a["L1_gnn_be2"], 64, XT2)

            def add_fc(v, link, t, ps):
                r = relu[:, t % 4, :]
                link(v.tensor_tensor(r, ps, bfc[:], ALU.add))
                return v.scalar_tensor_tensor(out=X[:, t, :], in0=r, scalar=0.0, in1=X[:, t, :], op0=ALU.max, op1=ALU.add)
            from_features(nc, "fc", [(UT[:, 0, :], Wfc[:, 0, :]), (UT[:, 1, :], Wfc[:, 1, :]), (XT1, Wfc[:, 2, :]), (XT2, Wfc2[:])],
                          D, add_fc, [(Wfc[:], a["L1_gnn_Wfc"][0:384, :].rearrange("(k p) n -> p k n", p=P)),
                                      (Wfc2[:], a["L1_gnn_Wfc"][384:448, :]),
                                      (bfc[:], a["L1_gnn_bfc"].partition_broadcast(TN))])
        with ExitStack() as gat:
            UT = sb("UT3", [P, 2, N], c=gat)
            gates = sb("gates4", [TN, NT, 4], c=gat)
            HG = sb("HG", [TN, NT, 20], c=gat)
            AD = sb("AD", [TN, NT, 4], c=gat)
            tmp = sb("tmpg", [TN, NT, 16], c=gat)
            vec = sb("vecg", [TN, 5, 16], c=gat)
            row_stats(nc, "st6", X, rstd, shift)
            project(nc, "gat", cs, X, rstd, shift, a["L1_ffn_W_gat"], [(0, 16)],
                    lambda v, j, tile, s, ps: v.tensor_copy(HG[:, tile, 0:16], ps), UT=UT)
            wide16 = lambda k: vec[:, k, :].unsqueeze(1).to_broadcast([TN, NT, 16])

            def attend(v, link, act_do):
                for k, dest in ((0, HG[:, :, 16:20]), (1, AD[:])):
                    link(v.tensor_tensor(tmp[:], HG[:, :, 0:16], wide16(k), ALU.mult))
                    link(v.tensor_reduce(dest, tmp[:].rearrange("p t (h e) -> p t h e", h=GH), AX.X, ALU.add))
            vector_steps(nc, "att", attend, [(vec[:, k, :], v.partition_broadcast(TN)) for k, v in enumerate(
                (a["L1_ffn_att_src"].rearrange("h e -> (h e)"), a["L1_ffn_att_dst"].rearrange("h e -> (h e)"),
                 a["L1_ffn_b_gat"], a["L1_ffn_ln_gamma"], a["L1_ffn_ln_beta"]))])
            move(nc, "g", [(table_rows(g_dram), HG[:])])
            accs = sb("accs", [TN, NT, 25], c=gat)
            with ExitStack() as edges:
                S = sb("Sg", [P, g2.pairs, GH], c=edges)
                M = sb("Mg", [P, g2.pairs, GH], c=edges)
                RW = sb("RW", [P, g2.pairs, 25], c=edges)
                with ExitStack() as gt:
                    GT = sb("GT", [P, g2.pairs, 20], c=gt)
                    gat_scores(nc, g2, g_dram, AD, GT, S)
                    segment_max(nc, g2, "max4", S, GH, M, carries[GH])
                    edge_weights(nc, "w4", S, M, RW[:, :, 16:20])

                    def rows25(v, link, act_do):
                        w = RW[:, :, 16:20].unsqueeze(3).to_broadcast([P, g2.pairs, GH, GE])
                        link(v.tensor_tensor(RW[:, :, 0:16].rearrange("p t (h e) -> p t h e", h=GH),
                                             GT[:, :, 0:16].rearrange("p t (h e) -> p t h e", h=GH), w, ALU.mult))
                        link(v.tensor_tensor(RW[:, :, 20:24], M[:], g2.last_of[:].unsqueeze(2).to_broadcast([P, g2.pairs, GH]), ALU.mult))
                        link(v.tensor_copy(RW[:, :, 24], g2.last_of[:]))
                    vector_steps(nc, "rw", rows25)
                with nc.psum_tensor("acc3", [TN, 1024], F32) as acc3:
                    gat_sums(nc, g2, RW, acc3)

                    def keep(v, link, act_do):
                        link(v.tensor_copy(accs[:], acc3[:, 0:800].rearrange("p (t c) -> p t c", c=32)[:, :, 0:25]))
                    vector_steps(nc, "keep", keep)
            with ExitStack() as node:
                m1, own, m = (sb(k, [TN, NT, GH], c=node) for k in ("m1", "own", "mx"))
                agg, sq = sb("agg", [TN, NT, 16], c=node), sb("sq", [TN, NT, 16], c=node)
                mean, var = sb("mean", [TN, NT], c=node), sb("var", [TN, NT], c=node)
                sc8 = sb("sc8", [TN, NT, 8], c=node)

                def finish_gat(v, link, act_do):
                    four = lambda x: x.unsqueeze(3).to_broadcast([TN, NT, GH, GE])
                    heads = lambda x: x.rearrange("p t (h e) -> p t h e", h=GH)
                    link(v.tensor_scalar(mean[:], accs[:, :, 24], -1.0, BIG, ALU.add, ALU.mult))
                    link(v.tensor_tensor(m1[:], accs[:, :, 20:24], mean[:].unsqueeze(2).to_broadcast([TN, NT, GH]), ALU.add))
                    link(v.tensor_tensor(own[:], HG[:, :, 16:20], AD[:], ALU.add))
                    link(v.scalar_tensor_tensor(out=own[:], in0=own[:], scalar=0.2, in1=own[:], op0=ALU.mult, op1=ALU.max))
                    link(v.tensor_tensor(m[:], m1[:], own[:], ALU.max))
                    link(v.tensor_tensor(m1[:], m1[:], m[:], ALU.subtract))
                    link(v.tensor_tensor(own[:], own[:], m[:], ALU.subtract))
                    act_do(m1[:], m1[:], ACT.Exp)
                    act_do(own[:], own[:], ACT.Exp)
                    link(v.tensor_tensor(m[:], accs[:, :, 16:20], m1[:], ALU.mult))
                    link(v.tensor_tensor(m[:], m[:], own[:], ALU.add))
                    link(v.tensor_scalar(m[:], m[:], 1e-16, None, ALU.add))
                    link(v.reciprocal(m[:], m[:]))
                    link(v.tensor_tensor(heads(agg[:]), heads(accs[:, :, 0:16]), four(m1[:]), ALU.mult))
                    link(v.tensor_tensor(heads(sq[:]), heads(HG[:, :, 0:16]), four(own[:]), ALU.mult))
                    link(v.tensor_tensor(agg[:], agg[:], sq[:], ALU.add))
                    link(v.tensor_tensor(heads(agg[:]), heads(agg[:]), four(m[:]), ALU.mult))
                    link(v.tensor_tensor(agg[:], agg[:], wide16(2), ALU.add))
                    w16 = lambda x: x.unsqueeze(2).to_broadcast([TN, NT, 16])
                    link(v.tensor_reduce(mean[:], agg[:], AX.X, ALU.add))
                    link(v.tensor_scalar(mean[:], mean[:], 1.0 / 16, None, ALU.mult))
                    link(v.tensor_tensor(agg[:], agg[:], w16(mean[:]), ALU.subtract))
                    link(v.tensor_tensor(sq[:], agg[:], agg[:], ALU.mult))
                    link(v.tensor_reduce(var[:], sq[:], AX.X, ALU.add))
                    link(v.tensor_scalar(var[:], var[:], 1.0 / 16, EPS, ALU.mult, ALU.add))
                    act_do(var[:], var[:], ACT.Sqrt)
                    link(v.reciprocal(var[:], var[:]))
                    link(v.tensor_tensor(agg[:], agg[:], w16(var[:]), ALU.mult))
                    link(v.tensor_tensor(agg[:], agg[:], wide16(3), ALU.mult))
                    link(v.tensor_tensor(agg[:], agg[:], wide16(4), ALU.add))
                    link(v.memset(sc8[:], -BIG))
                    link(v.tensor_reduce(sc8[:, :, 0:4], agg[:].rearrange("p t (h e) -> p t e h", h=GH), AX.X, ALU.add))
                    link(v.tensor_scalar(sc8[:, :, 0:4], sc8[:, :, 0:4], 0.25, None, ALU.mult))
                vector_steps(nc, "fin", finish_gat)
                top2_gates(nc, "top4", cs, sc8, 4, gates)
            experts(nc, "ff1", cs, UT, X, gates, a["L1_ffn_W1"], a["L1_ffn_b1"], a["L1_ffn_W2"], a["L1_ffn_b2"], 4, ACT.Gelu)
        move(nc, "out", [(table_rows(out), X[:])])


NAMES = ['x', 'src', 'dst', 'L0_gnn_Wqkv', 'L0_gnn_bqkv', 'L0_gnn_ln_attn_g', 'L0_gnn_ln_attn_b', 'L0_gnn_ln_res_g',
         'L0_gnn_ln_res_b', 'L0_gnn_W_in', 'L0_gnn_b_in', 'L0_gnn_W_out', 'L0_gnn_b_out', 'L0_ffn_gate_w', 'L0_ffn_gate_b',
         'L0_ffn_w1', 'L0_ffn_b1', 'L0_ffn_w2', 'L0_ffn_b2', 'L0_ffn_gamma', 'L0_ffn_beta', 'L1_gnn_W1', 'L1_gnn_b1',
         'L1_gnn_g1', 'L1_gnn_be1', 'L1_gnn_W2', 'L1_gnn_b2', 'L1_gnn_g2', 'L1_gnn_be2', 'L1_gnn_Wfc', 'L1_gnn_bfc',
         'L1_ffn_W_gat', 'L1_ffn_att_src', 'L1_ffn_att_dst', 'L1_ffn_b_gat', 'L1_ffn_ln_gamma', 'L1_ffn_ln_beta',
         'L1_ffn_W1', 'L1_ffn_b1', 'L1_ffn_W2', 'L1_ffn_b2',
         'L1_ffn_edge_index']


def kernel(**inputs):
    import concourse.bacc as bacc
    from concourse.bass_utils import run_bass_kernel_spmd

    nc = bacc.Bacc("TRN2", target_bir_lowering=False, num_devices=1)
    arrays, aps = {}, {}
    for name in NAMES:
        arrays[f"in_{name}"] = np.ascontiguousarray(inputs[name])
        aps[name] = nc.dram_tensor(f"in_{name}", arrays[f"in_{name}"].shape, mybir.dt.from_np(arrays[f"in_{name}"].dtype),
                                   kind="ExternalInput").ap()
    out = nc.dram_tensor("out_x", (N, D), F32, kind="ExternalOutput").ap()
    build(nc, aps, out)
    got = run_bass_kernel_spmd(nc, [arrays], core_ids=[0])
    return got.results[0]["out_x"]
```

```python
from contextlib import ExitStack

import numpy as np
import concourse.bass as bass
from concourse import mybir

F32 = mybir.dt.float32
BF16 = mybir.dt.bfloat16
I32 = mybir.dt.int32
U32 = mybir.dt.uint32
ALU = mybir.AluOpType
ACT = mybir.ActivationFunctionType
AX = mybir.AxisListType

P = 128
N, D = 3125, 256
TN, NT = 125, 25
E1, E2 = 50000, 32768
PB, RING = 4, 4
TURN = PB * RING
H = 8
GH, GE = 4, 4
BIG = 1e30
NO_DST, NO_KEY = 8191.0, -7.0
EPS = 1e-5


class Phase:

    def __init__(self, nc, name):
        self.nc, self.name = nc, name

    def __enter__(self):
        self.ctx, self.sems = ExitStack(), []
        return self

    def sb(self, name, shape, dt=F32):
        return self.ctx.enter_context(self.nc.sbuf_tensor(f"{self.name}_{name}", shape, dt))

    def psum(self, name, shape, dt=F32):
        return self.ctx.enter_context(self.nc.psum_tensor(f"{self.name}_{name}", shape, dt))

    def sem(self, name):
        s = self.nc.alloc_semaphore(f"{self.name}_{name}")
        self.sems.append(s)
        return s

    def __exit__(self, kind, value, trace):
        self.ctx.close()
        if kind is None:
            self.nc.clear_and_free_semaphores(self.sems)
            self.nc.all_engine_barrier()


def chain(eng, sem, base=0):
    n = [0]

    def link(ins):
        n[0] += 1
        ins.then_inc(sem, 1)
        eng.wait_ge(sem, base + n[0])
    return link


def row_stats(nc, name, X, rstd, shift):
    with Phase(nc, name) as ph:
        parts = ph.sb("parts", [TN, NT, 6])
        a, b, c = (ph.sb(k, [TN, NT]) for k in "abc")
        taken, link_s, var_ready, root_ready = (ph.sem(k) for k in ("taken", "link", "var", "root"))
        with nc.Block() as block:
            @block.vector
            def _(v):
                with v.Fori(0, 5) as i:
                    for s in range(5):
                        v.bn_stats(out=parts[:, i * 5 + s, :], in_=X[:, i * 5 + s, :]).then_inc(taken, 1)
                v.wait_ge(taken, NT)
                link = chain(v, link_s)
                link(v.tensor_tensor(a[:], parts[:, :, 1], parts[:, :, 4], ALU.add))
                link(v.tensor_tensor(b[:], parts[:, :, 1], parts[:, :, 4], ALU.subtract))
                link(v.tensor_tensor(c[:], parts[:, :, 2], parts[:, :, 5], ALU.add))
                link(v.tensor_tensor(b[:], b[:], b[:], ALU.mult))
                link(v.scalar_tensor_tensor(out=b[:], in0=b[:], scalar=D / 4.0, in1=c[:], op0=ALU.mult, op1=ALU.add))
                v.tensor_scalar(c[:], b[:], 1.0 / D, EPS, ALU.mult, ALU.add).then_inc(var_ready, 1)
                v.wait_ge(root_ready, 1)
                link(v.reciprocal(rstd[:], b[:]))
                link(v.scalar_tensor_tensor(out=shift[:], in0=a[:], scalar=-0.5, in1=rstd[:], op0=ALU.mult, op1=ALU.mult))

            @block.scalar
            def _(act):
                act.wait_ge(var_ready, 1)
                nc.scalar.activation(b[:], c[:], ACT.Sqrt).then_inc(root_ready, 1)


def normalise(nc, name, X, rstd, shift, out):
    with Phase(nc, name) as ph:
        done = ph.sem("done")
        with nc.Block() as block:
            @block.vector
            def _(v):
                with v.Fori(0, 5) as i:
                    for s in range(5):
                        t = i * 5 + s
                        v.tensor_scalar(out[:, t, :], X[:, t, :], rstd[:, bass.ds(t, 1)], shift[:, bass.ds(t, 1)],
                                        ALU.mult, ALU.add).then_inc(done, 1)
                v.wait_ge(done, NT)


def project(nc, name, cs, X, rstd, shift, weight, jobs, finish, affine=None, UT=None, rows_out=None):
    J = len(jobs)
    with Phase(nc, name) as ph:
        row = ph.sb("row", [TN, 5, D])
        rowT = ph.sb("rowT", [P, 5, 2, TN])
        tp = [ph.psum(f"tp{s}", [P, 2, TN]) for s in range(2)]
        pj = [ph.psum(f"pj{s}", [TN, 512]) for s in range(5)] if J else []
        W = ph.sb("W", [P, 2, weight.shape[1]]) if J else None
        G = ph.sb("G", [TN, 2, D]) if affine else None
        loaded, row_ready, turned, copied, projected, finished, link_s, passed = (
            ph.sem(k) for k in ("loaded", "row", "turned", "copied", "projected", "finished", "link", "passed"))
        n_links = (2 if affine else 0) * 5
        with nc.Block() as block:
            @block.sync
            def _(sp):
                if J:
                    sp.dma_start(W[:], weight.rearrange("(k p) n -> p k n", p=P)).then_inc(loaded, 16)
                if affine:
                    for k in range(2):
                        sp.dma_start(G[:, k, :], affine[k].partition_broadcast(TN)).then_inc(loaded, 16)

            @block.vector
            def _(v):
                if affine:
                    v.wait_ge(loaded, 16 * (2 + (J > 0)))
                v.sem_inc(finished, 5)
                with v.Fori(0, 5) as i:
                    link = chain(v, link_s, i * n_links)

                    def make_row(s):
                        t = i * 5 + s
                        v.wait_ge(copied, i * 5 + (s + 1))
                        ins = v.tensor_scalar(row[:, s, :], X[:, t, :], rstd[:, bass.ds(t, 1)], shift[:, bass.ds(t, 1)],
                                              ALU.mult, ALU.add)
                        if affine:
                            link(ins)
                            link(v.tensor_tensor(row[:, s, :], row[:, s, :], G[:, 0, :], ALU.mult))
                            ins = v.tensor_tensor(row[:, s, :], row[:, s, :], G[:, 1, :], ALU.add)
                        ins.then_inc(row_ready, 1)

                    def finish_tile(s):
                        for j in range(J):
                            q = s * J + j
                            v.wait_ge(projected, i * (5 * J) + (q + 1))
                            finish(v, j, i * 5 + s, s, pj[q % 5][:, 0:jobs[j][1]]).then_inc(finished, 1)

                    for s in range(5):
                        make_row(s)
                        if s:
                            finish_tile(s - 1)
                    finish_tile(4)
                v.wait_ge(finished, 25 * J + 5)

            @block.tensor
            def _(pe):
                if J:
                    pe.wait_ge(loaded, 16 * (1 + 2 * bool(affine)))
                with pe.Fori(0, 5) as i:
                    def turn(s):
                        pe.wait_ge(row_ready, i * 5 + (s + 1))
                        pe.sem_inc(passed, 1)
                        pe.wait_ge(copied, i * 5 + (s + 4))
                        for k in range(2):
                            ins = pe.transpose(tp[s % 2][:, k, :], row[:, s, k * P:(k + 1) * P], cs.ident[0:TN, 0:TN])
                        ins.then_inc(turned, 1)

                    def products(s):
                        pe.wait_ge(copied, i * 5 + (s + 6))
                        for j, (c0, w) in enumerate(jobs):
                            q = s * J + j
                            pe.wait_ge(finished, i * (5 * J) + (q + 1))
                            for k in range(2):
                                ins = pe.matmul(pj[q % 5][:, 0:w], rowT[:, s, k, :], W[:, k, c0:c0 + w],
                                                start=(k == 0), stop=(k == 1))
                            ins.then_inc(projected, 1)

                    pe.wait_ge(copied, i * 5 + 5)
                    pe.sem_inc(passed, 1)
                    for s in range(5):
                        turn(s)
                        if s:
                            products(s - 1)
                    products(4)

            @block.scalar
            def _(act):
                act.sem_inc(copied, 5)
                with act.Fori(0, 5) as i:
                    for s in range(5):
                        t = i * 5 + s
                        act.wait_ge(turned, i * 5 + (s + 1))
                        act.sem_inc(passed, 1)
                        if rows_out is not None:
                            nc.scalar.copy(rows_out[:, t, :], row[:, s, :])
                        if UT is not None:
                            nc.scalar.copy(UT[:, :, bass.ds(t * TN, TN)], tp[s % 2][:])
                        nc.scalar.copy(rowT[:, s, :, :], tp[s % 2][:]).then_inc(copied, 1)


class Consts:

    def __init__(self, sb):
        self.ident = sb("ident", [P, P])
        self.ones = sb("ones", [P, P])
        self.count_row = sb("count_row", [P, pairs_of(E1)])
        self.count_col = sb("count_col", [P, 1])
        self.neg_col = sb("neg_col", [P, 1])


def pairs_of(edges):
    most = (edges + P - 1) // P + NT - 1
    return (most // 32 + 1) * 32


class Graph:

    def __init__(self, name, sb, dram, consts, edges):
        self.ident, self.ones, self.count_row = consts.ident, consts.ones, consts.count_row
        self.count_col, self.neg_col = consts.count_col, consts.neg_col
        self.name, self.edges, self.pairs = name, edges, pairs_of(edges)
        self.loops = self.pairs // TURN
        self.src_of = sb(f"{name}_src_of", [P, self.pairs], I32)
        self.tile_of = sb(f"{name}_tile_of", [1, self.pairs], I32)
        self.local = sb(f"{name}_local", [P, self.pairs])
        self.neg_local = sb(f"{name}_neg_local", [P, self.pairs])
        self.neg_big = sb(f"{name}_neg_big", [P, self.pairs])
        self.last_of = sb(f"{name}_last_of", [P, self.pairs])
        self.local_rows = dram(f"{name}_local_rows", [self.pairs, P]).ap()
        self.keys_t = dram(f"{name}_keys", [self.pairs * P + 2])
        self.keys = self.keys_t.ap()


def constants(nc, cs):
    with Phase(nc, "const") as ph:
        made = ph.sem("made")
        t32 = ph.sb("t32", [P, cs.count_row.shape[1]], I32)
        p32 = ph.sb("p32", [P, 1], I32)
        with nc.Block() as block:
            @block.gpsimd
            def _(g):
                link = chain(g, made)
                link(g.memset(cs.ident[:], 0.0))
                link(g.affine_select(out=cs.ident[:], in_=cs.ident[:], compare_op=ALU.not_equal, fill=1.0,
                                     base=0, pattern=[[-1, P]], channel_multiplier=1))
                link(g.iota(t32[:], pattern=[[1, cs.count_row.shape[1]]], base=0, channel_multiplier=0))
                link(g.tensor_copy(cs.count_row[:], t32[:]))
                link(g.iota(p32[:], pattern=[[1, 1]], base=0, channel_multiplier=1))
                link(g.tensor_copy(cs.count_col[:], p32[:]))
                link(g.tensor_scalar(cs.neg_col[:], cs.count_col[:], -1.0, None, ALU.mult))
                link(g.memset(cs.ones[:], 1.0))


def index_tables(nc, cs, src=None, dst=None, joined=None):
    PAIRS, E = cs.pairs, cs.edges
    PR = PAIRS // 4
    NB = (PAIRS + P - 1) // P
    count = cs.count_row[:, 0:PAIRS]
    with Phase(nc, cs.name) as ph:
        raw = ph.sb("raw", [P, 2, NB, P] if joined is None else [P, NB, P, 2], I32)
        raw_of = [raw[:, k, :, :] if joined is None else raw[:, :, :, k] for k in range(2)]
        val = ph.sb("val", [P, 2, NB, P])
        W = NT - 1 + NB * P
        lanes = ph.sb("lanes", [P, 2, W])
        less = ph.sb("less", [P, NT - 1])
        junk = ph.sb("junk", [P, NB * P])
        first = ph.sb("first", [P, NT - 1])
        firsti = ph.sb("firsti", [P, NT - 1], I32)
        mask = ph.sb("mask", [P, PAIRS], I32)
        srcx = ph.sb("srcx", [P, PAIRS])
        dstx = ph.sb("dstx", [P, PAIRS])
        tile_f = ph.sb("tile_f", [P, PAIRS])
        valid = ph.sb("valid", [P, PAIRS])
        key = ph.sb("key", [P, PAIRS])
        rows = ph.sb("rows", [PR, 2, 4, P])
        near = ph.sb("near", [PR, 2, 4, P])
        edge1 = ph.sb("edge1", [1, 2])
        pt = [ph.psum(f"pt{b}", [P, NB, P]) for b in range(2)]
        pr = [ph.psum(f"pr{b}", [PR, 4, P]) for b in range(2)]
        pn = ph.psum("pn", [P, NT - 1])
        pe_end = ph.psum("pe", [P, 4, P])
        filled, loaded, cast, turned, summed, tables, rowed, in_rows, written, near_in, ends, ended, v_link = (
            ph.sem(k) for k in ("filled", "loaded", "cast", "turned", "summed", "tables", "rowed", "in_rows", "written",
                                "near_in", "ends", "ended", "link"))
        FB = E // (P * P)
        full = FB * P * P
        rest = (E - full) // P
        tail = E - full - rest * P
        n_loads = 1 if joined is not None else 2 * (1 + (rest > 0) + (tail > 0))
        assert joined is None or full == E
        with nc.Block() as block:
            @block.sync
            def _(sp):
                sp.wait_ge(filled, 2)
                if joined is not None:
                    sp.dma_start(raw[:, 0:FB, :, :], joined.rearrange("(b t l) k -> t b l k", b=FB, l=P)).then_inc(loaded, 16)
                for k, a in enumerate((dst, src) if joined is None else ()):
                    sp.dma_start(raw[:, k, 0:FB, :], a[0:full].rearrange("(b t l) -> t b l", b=FB, l=P)).then_inc(loaded, 16)
                    if rest:
                        sp.dma_start(raw[0:rest, k, FB, :], a[full:full + rest * P].rearrange("(t l) -> t l", l=P)).then_inc(loaded, 16)
                    if tail:
                        sp.dma_start(raw[rest:rest + 1, k, FB, 0:tail], a[E - tail:E].rearrange("(t l) -> t l", t=1)).then_inc(loaded, 16)
                sp.wait_ge(in_rows, 2)
                sp.dma_start(cs.local_rows.rearrange("(b r) l -> r b l", b=4), rows[:, 0, :, :]).then_inc(written, 16)
                body = cs.keys[1:1 + PAIRS * P]
                sp.dma_start(body.rearrange("(b r l) -> r b l", b=4, l=P), rows[:, 1, :, :]).then_inc(written, 16)
                sp.dma_start(cs.keys[0:1].rearrange("(a b) -> a b", a=1), edge1[:, 0:1]).then_inc(written, 16)
                sp.dma_start(cs.keys[1 + PAIRS * P:2 + PAIRS * P].rearrange("(a b) -> a b", a=1), edge1[:, 1:2]).then_inc(written, 16)
                sp.wait_ge(written, 64)
                for k in range(2):
                    sp.dma_start(near[:, k, :, :], cs.keys[1 + k:1 + k + PAIRS * P].rearrange("(b r l) -> r b l", b=4, l=P)).then_inc(near_in, 16)
                sp.wait_ge(near_in, 32)

            @block.vector
            def _(v):
                v.memset(raw_of[0][:, FB, :], int(NO_DST)).then_inc(filled, 1)
                v.memset(raw_of[1][:, FB, :], 0).then_inc(filled, 1)
                link = chain(v, v_link)
                link(v.memset(edge1[:], NO_KEY))
                link(v.memset(lanes[:], 0.0))
                v.wait_ge(loaded, 16 * n_loads)
                v.tensor_copy(val[:, 0, :, :], raw_of[0])
                v.tensor_copy(val[:, 1, :, :], raw_of[1]).then_inc(cast, 1)
                v.wait_ge(cast, 1)
                for j in range(1, NT):
                    link(v.tensor_scalar(junk[:], val[:, 0, :, :].rearrange("p b l -> p (b l)"), float(TN * j), 0.0, ALU.is_lt, ALU.add,
                                         accum_out=less[:, j - 1:j]))
                v.sem_inc(cast, 1)
                v.wait_ge(turned, 2)
                for k in range(2):
                    link(v.tensor_copy(lanes[:, k, NT - 1:NT - 1 + NB * P], pt[k][:].rearrange("p b l -> p (b l)")))
                v.wait_ge(summed, 1)
                link(v.tensor_copy(firsti[:], pn[:]))
                link(v.tensor_scalar(firsti[:], firsti[:], 7, None, ALU.arith_shift_right))
                link(v.tensor_copy(first[:], firsti[:]))
                link(v.scalar_tensor_tensor(out=first[:], in0=first[:], scalar=1.0, in1=cs.count_row[:, 0:NT - 1], op0=ALU.add, op1=ALU.add))
                link(v.memset(tile_f[:], 0.0))
                link(v.tensor_copy(dstx[:], lanes[:, 0, NT - 1:NT - 1 + PAIRS]))
                link(v.tensor_copy(srcx[:], lanes[:, 1, NT - 1:NT - 1 + PAIRS]))
                for j in range(1, NT):
                    at = first[:, j - 1:j]
                    link(v.tensor_scalar(mask[:], count, at, None, ALU.is_ge))
                    link(v.copy_predicated(dstx[:], mask[:], lanes[:, 0, NT - 1 - j:NT - 1 - j + PAIRS]))
                    link(v.copy_predicated(srcx[:], mask[:], lanes[:, 1, NT - 1 - j:NT - 1 - j + PAIRS]))
                    link(v.scalar_tensor_tensor(out=tile_f[:], in0=count, scalar=at, in1=tile_f[:], op0=ALU.is_ge, op1=ALU.add))
                link(v.tensor_copy(cs.src_of[:], srcx[:]))
                link(v.tensor_copy(cs.tile_of[:], tile_f[0:1, :]))
                link(v.scalar_tensor_tensor(out=cs.local[:], in0=tile_f[:], scalar=-float(TN), in1=dstx[:], op0=ALU.mult, op1=ALU.add))
                link(v.tensor_scalar(cs.neg_local[:], cs.local[:], -1.0, None, ALU.mult))
                link(v.tensor_scalar(valid[:], cs.local[:], 0.0, None, ALU.is_ge))
                link(v.scalar_tensor_tensor(out=valid[:], in0=cs.local[:], scalar=float(TN), in1=valid[:], op0=ALU.is_lt, op1=ALU.mult))
                link(v.tensor_scalar(cs.neg_big[:], valid[:], BIG, -BIG, ALU.mult, ALU.add))
                link(v.scalar_tensor_tensor(out=key[:], in0=dstx[:], scalar=1.0, in1=valid[:], op0=ALU.add, op1=ALU.mult))
                link(v.tensor_scalar(key[:], key[:], -1.0, None, ALU.add))
                v.sem_inc(tables, 1)
                for k in range(2):
                    v.wait_ge(rowed, k + 1)
                    v.tensor_copy(rows[:, k, :, :], pr[k][:]).then_inc(in_rows, 1)
                v.wait_ge(near_in, 32)
                v.tensor_tensor(near[:, 0, :, :], near[:, 0, :, :], near[:, 1, :, :], ALU.not_equal).then_inc(ends, 1)
                v.wait_ge(ended, 1)
                link(v.tensor_copy(cs.last_of[:].rearrange("p (b r) -> p b r", b=4), pe_end[:, :, 0:PR]))

            @block.tensor
            def _(pe):
                pe.wait_ge(cast, 1)
                for k in range(2):
                    for b in range(NB):
                        ins = pe.transpose(pt[k][:, b, :], val[:, k, b, :], cs.ident[:])
                    ins.then_inc(turned, 1)
                pe.wait_ge(cast, 2)
                pe.matmul(pn[:], cs.ones[:], less[:], start=True, stop=True).then_inc(summed, 1)
                pe.wait_ge(tables, 1)
                for k, table in enumerate((cs.local, key)):
                    for b in range(4):
                        ins = pe.transpose(pr[k][:, b, :], table[:, b * PR:(b + 1) * PR], cs.ident[:])
                    ins.then_inc(rowed, 1)
                pe.wait_ge(ends, 1)
                for b in range(4):
                    ins = pe.transpose(pe_end[:, b, 0:PR], near[:, 0, b, :], cs.ident[0:PR, 0:PR])
                ins.then_inc(ended, 1)


class EdgeSort:

    def __init__(self, sb, edges, pay, pos):
        self.tiles = edges // P
        self.turns = self.tiles // TURN
        self.pay, self.pos = pay, pos
        self.lanes = sb("sort_lanes", [P, 2, self.tiles])
        self.a_of, self.b_of = (sb(k, [P, self.tiles + 2 * PB]) for k in ("sort_a", "sort_b"))
        self.ident = sb("sort_ident", [P, P], BF16)
        self.start = sb("sort_start", [NT, TN])
        self.earlier = sb("sort_earlier", [P, 2 * P])


def make_hots(v, cs, es, tiles, hotA, hotB):
    wide = lambda x, n: x[:, tiles].unsqueeze(2).to_broadcast([P, PB, n])
    number = lambda n: cs.count_row[:, 0:n].unsqueeze(1).to_broadcast([P, PB, n])
    v.tensor_tensor(hotA, number(NT), wide(es.a_of, NT), ALU.is_equal)
    return v.tensor_tensor(hotB, number(TN), wide(es.b_of, TN), ALU.is_equal)


def histogram(nc, cs, edge_index, es):
    NB = es.tiles // P
    A = NT
    with Phase(nc, "hist") as ph:
        raw = ph.sb("raw", [P, 2, NB, P], I32)
        val = ph.sb("val", [P, 2, NB, P])
        upper = ph.sb("upper", [A, A])
        zero = ph.sb("zero", [P, TN], BF16)
        hotA = ph.sb("hotA", [P, RING, PB, A], BF16)
        hotB = ph.sb("hotB", [P, RING, PB, TN], BF16)
        hist, incl, zeros = (ph.sb(k, [A, TN]) for k in ("hist", "incl", "zeros"))
        before = ph.sb("before", [A, 1])
        pt = [ph.psum(f"pt{k}", [P, NB, P]) for k in range(2)]
        counts = ph.psum("counts", [A, 512])
        below = ph.psum("below", [A, 512])
        loaded, cast, turned, consts, v_link, g_link, hot1, summed1, hist_out, off, off_in, pe_on, dve_on = (
            ph.sem(k) for k in ("loaded", "cast", "turned", "consts", "v_link", "g_link", "hot1", "summed1", "hist", "off", "off_in",
                                "pe_on", "dve_on"))
        with nc.Block() as block:
            @block.sync
            def _(sp):
                for k in range(2):
                    sp.dma_start(raw[:, k, :, :], edge_index[1 - k].rearrange("(b t l) -> t b l", b=NB, l=P)).then_inc(loaded, 16)

            @block.gpsimd
            def _(g):
                link = chain(g, g_link)
                link(g.memset(es.earlier[:], 1.0))
                link(g.memset(upper[:], 1.0))
                tri = es.earlier[:, P:2 * P]
                link(g.affine_select(out=tri, in_=tri, compare_op=ALU.is_gt, fill=0.0, base=0, pattern=[[-1, P]], channel_multiplier=1))
                link(g.affine_select(out=upper[:], in_=upper[:], compare_op=ALU.is_gt, fill=0.0, base=0,
                                     pattern=[[1, A]], channel_multiplier=-1))
                g.sem_inc(consts, 1)

            @block.vector
            def _(v):
                link = chain(v, v_link)
                v.wait_ge(loaded, 32)
                v.tensor_copy(val[:], raw[:]).then_inc(cast, 1)
                link(v.memset(es.a_of[:], 0.0))
                link(v.memset(es.b_of[:], 0.0))
                link(v.tensor_copy(es.ident[:], cs.ident[:]))
                link(v.memset(zero[:], 0.0))
                link(v.memset(zeros[:], 0.0))
                v.wait_ge(turned, 2)
                for k in range(2):
                    link(v.tensor_copy(es.lanes[:, k, :], pt[k][:].rearrange("p b l -> p (b l)")))
                    link(v.tensor_copy(es.pay[:, :, k], es.lanes[:, k, :]))
                dst, a_of, b_of = es.lanes[:, 0, :], es.a_of[:, 0:es.tiles], es.b_of[:, 0:es.tiles]
                for j in range(1, A):
                    link(v.scalar_tensor_tensor(out=a_of, in0=dst, scalar=float(TN * j), in1=a_of, op0=ALU.is_ge, op1=ALU.add))
                link(v.scalar_tensor_tensor(out=b_of, in0=a_of, scalar=-float(TN), in1=dst, op0=ALU.mult, op1=ALU.add))
                with v.Fori(0, es.turns) as i:
                    for q in range(RING):
                        v.wait_ge(summed1, i * RING + (q + 1))
                        v.sem_inc(dve_on, 1)
                        make_hots(v, cs, es, bass.ds(i * TURN + q * PB, PB), hotA[:, q, :, :], hotB[:, q, :, :]).then_inc(hot1, 1)
                v.wait_ge(summed1, es.turns * RING + RING)
                v.tensor_copy(hist[:], counts[:, 0:TN]).then_inc(hist_out, 1)
                v.wait_ge(hist_out, 1)
                link(v.tensor_tensor_scan(incl[:], zeros[:], hist[:], 0.0, ALU.add, ALU.add))
                v.sem_inc(off, 1)
                v.wait_ge(off_in, 1)
                link(v.tensor_copy(before[:], below[:, 0:1]))
                link(v.tensor_tensor(es.start[:], incl[:], hist[:], ALU.subtract))
                link(v.tensor_scalar(es.start[:], es.start[:], before[:, 0:1], None, ALU.add))

            @block.tensor
            def _(pe):
                pe.wait_ge(cast, 1)
                for k in range(2):
                    for b in range(NB):
                        ins = pe.transpose(pt[k][:, b, :], val[:, k, b, :], cs.ident[:])
                    ins.then_inc(turned, 1)
                pe.sem_inc(summed1, RING)
                pe.wait_ge(hot1, 1)
                pe.matmul(counts[:, 0:TN], zero[:, 0:A], zero[:], start=True, stop=True)
                with pe.Fori(0, es.turns) as i:
                    for q in range(RING):
                        pe.wait_ge(hot1, i * RING + (q + 1))
                        pe.sem_inc(pe_on, 1)
                        for u in range(PB):
                            ins = pe.matmul(counts[:, 0:TN], hotA[:, q, u, :], hotB[:, q, u, :], start=False, stop=True, skip_group_check=True)
                        ins.then_inc(summed1, 1)
                pe.wait_ge(off, 1)
                pe.wait_ge(consts, 1)
                pe.matmul(below[:, 0:1], upper[:], incl[:, TN - 1:TN], start=True, stop=True).then_inc(off_in, 1)


class Ranks:

    def __init__(self, ph, nc, cs, es, edge_index):
        self.nc, self.cs, self.es, self.edge_index = nc, cs, es, edge_index
        self.rows = ph.sb("r_rows", [P, RING, PB * P], I32)
        self.hotA = ph.sb("r_hotA", [P, RING, PB, NT], BF16)
        self.hotB = ph.sb("r_hotB", [P, RING, PB, TN], BF16)
        self.hotT = ph.sb("r_hotT", [NT, 2, PB, P])
        self.snap = ph.sb("r_snap", [NT, 2, 2, TN])
        self.same = ph.sb("r_same", [P, PB, 2 * P])
        self.pick = ph.sb("r_pick", [P, PB, TN])
        self.n_same, self.n_before = ph.sb("r_n_same", [P, 2, PB]), ph.sb("r_n_before", [P, 2, PB])
        self.counts = ph.psum("r_counts", [NT, 512])
        self.pa = ph.psum("r_pa", [NT, 2 * PB, P], BF16)
        self.pr = [ph.psum(f"r_pr{k}", [P, 512]) for k in range(2)]
        self.hots, self.hot_turned, self.hot_copied, self.snapped, self.grown, self.ranked, self.looked, self.compared, self.placed = (
            ph.sem(f"r_{k}") for k in ("hots", "hot_turned", "hot_copied", "snapped", "grown", "ranked", "looked", "compared", "placed"))
        self.pe_on, self.act_on, self.sp_on, self.dve_on = (
            ph.sem(f"r_{k}") for k in ("pe_on", "act_on", "sp_on", "dve_on"))
        self.rows_in = [ph.sem(f"r_rows{q}") for q in range(RING)]

    def load(self, sp, i, q):
        sp.wait_ge(self.compared, i * RING + (q + 1))
        sp.sem_inc(self.sp_on, 1)
        sp.dma_start(self.rows[:, q, :], self.edge_index[1, bass.ds(i * (TURN * P) + q * PB * P, PB * P)].partition_broadcast(P))\
          .then_inc(self.rows_in[q], 16)

    def turn_hots(self, pe, slot):
        for u in range(PB):
            ins = pe.transpose(self.pa[:, u, :], self.hotA[:, slot, u, :], self.es.ident[:])
        ins.then_inc(self.hot_turned, 1)

    def start_tensor(self, pe):
        pe.matmul(self.counts[:, 0:TN], self.cs.ident[0:NT, 0:NT], self.es.start[:], start=True, stop=True).then_inc(self.grown, 1)
        pe.wait_ge(self.hots, 1)
        self.turn_hots(pe, 0)
        pe.sem_inc(self.ranked, 1)

    def grow(self, pe, q, s):
        for u in (2 * s, 2 * s + 1):
            ins = pe.matmul(self.counts[:, 0:TN], self.hotA[:, q, u, :], self.hotB[:, q, u, :], start=False, stop=True,
                            skip_group_check=True)
        ins.then_inc(self.grown, 1)

    def tensor(self, pe, i, q):
        pe.wait_ge(self.snapped, i * (2 * RING) + (2 * q + 1))
        pe.sem_inc(self.pe_on, 1)
        self.grow(pe, q, 0)
        pe.wait_ge(self.hots, i * RING + (q + 2))
        pe.sem_inc(self.pe_on, 1)
        pe.wait_ge(self.hot_copied, i * RING + (q + 1))
        pe.sem_inc(self.pe_on, 1)
        self.turn_hots(pe, (q + 1) % RING)
        pe.wait_ge(self.snapped, i * (2 * RING) + (2 * q + 2))
        pe.sem_inc(self.pe_on, 1)
        self.grow(pe, q, 1)
        pe.wait_ge(self.looked, i * RING + (q + 1))
        pe.sem_inc(self.pe_on, 1)
        for u in range(PB):
            ins = pe.matmul(self.pr[q % 2][:, u * TN:(u + 1) * TN], self.hotT[:, q % 2, u, :], self.snap[:, q % 2, u // 2, :],
                            start=True, stop=True)
        ins.then_inc(self.ranked, 1)

    def keep_counts(self, slot, s):
        self.nc.scalar.copy(self.snap[:, slot, s, :], self.counts[:, 0:TN]).then_inc(self.snapped, 1)

    def copy_hots(self, slot):
        self.nc.scalar.copy(self.hotT[:, slot, :, :], self.pa[:, 0:PB, :]).then_inc(self.hot_copied, 1)

    def start_scalar(self, act):
        act.wait_ge(self.grown, 1)
        self.keep_counts(0, 0)
        act.wait_ge(self.hot_turned, 1)
        self.copy_hots(0)

    def scalar(self, act, i, q):
        act.wait_ge(self.grown, i * (2 * RING) + (2 * q + 2))
        act.sem_inc(self.act_on, 1)
        self.keep_counts(q % 2, 1)
        act.wait_ge(self.ranked, i * RING + (q + 1))
        act.sem_inc(self.act_on, 1)
        act.wait_ge(self.hot_turned, i * RING + (q + 2))
        act.sem_inc(self.act_on, 1)
        self.copy_hots((q + 1) % 2)
        act.wait_ge(self.grown, i * (2 * RING) + (2 * q + 3))
        act.sem_inc(self.act_on, 1)
        self.keep_counts((q + 1) % 2, 0)

    def make(self, v, i, q):
        slot = q % RING
        make_hots(v, self.cs, self.es, bass.ds(i * TURN + q * PB, PB), self.hotA[:, slot, :, :],
                  self.hotB[:, slot, :, :]).then_inc(self.hots, 1)

    def start_vector(self, v):
        self.make(v, 0, 0)
        self.make(v, 0, 1)
        v.sem_inc(self.looked, 2)
        v.sem_inc(self.placed, 2)
        v.sem_inc(self.compared, RING)

    def compare(self, v, i, q):
        self.make(v, i, q + 2)
        v.wait_ge(self.placed, i * RING + (q + 1))
        v.sem_inc(self.dve_on, 1)
        v.wait_ge(self.rows_in[q], i * 16 + 16)
        v.sem_inc(self.dve_on, 1)
        for u in range(PB):
            w = (u % 2 + 1) * P
            ins = v.scalar_tensor_tensor(out=self.same[:, u, 0:w], in0=self.rows[:, q, (u + 1) * P - w:(u + 1) * P],
                                         scalar=self.es.lanes[:, 0, bass.ds(i * TURN + q * PB + u, 1)], in1=self.es.earlier[:, 2 * P - w:2 * P],
                                         op0=ALU.is_equal, op1=ALU.mult, accum_out=self.n_same[:, q % 2, u:u + 1])
        ins.then_inc(self.compared, 1)

    def place(self, v, i, q):
        v.wait_ge(self.ranked, i * RING + (q + 2))
        v.sem_inc(self.dve_on, 1)
        for u in range(PB):
            ins = v.tensor_tensor_reduce(out=self.pick[:, u, :], in0=self.pr[q % 2][:, u * TN:(u + 1) * TN], in1=self.hotB[:, q, u, :],
                                         scale=1.0, scalar=0.0, op0=ALU.mult, op1=ALU.add, accum_out=self.n_before[:, q % 2, u:u + 1])
        ins.then_inc(self.looked, 1)
        v.wait_ge(self.looked, i * RING + (q + 3))
        v.sem_inc(self.dve_on, 1)
        v.tensor_tensor(self.es.pos[:, bass.ds(i * TURN + q * PB, PB)], self.n_same[:, q % 2, :], self.n_before[:, q % 2, :],
                        ALU.add).then_inc(self.placed, 1)

    def end_vector(self, v):
        v.wait_ge(self.placed, self.es.tiles // PB + 2)


def scatter_edges(g, es, joined, at, payload, out, copied, pool_on):
    def turn(i, first):
        for q in range(RING):
            if not first:
                g.wait_ge(out[q], i * (16 * PB))
                g.sem_inc(pool_on, 1)
            tiles = bass.ds(i * TURN + q * PB, PB)
            g.tensor_copy(at[:, q, :], es.pos[:, tiles])
            g.tensor_copy(payload[:, q, :, :], es.pay[:, tiles, :]).then_inc(copied, 1)
            g.wait_ge(copied, i * RING + (q + 1))
            g.sem_inc(pool_on, 1)
            for u in range(PB):
                g.indirect_dma_start(out=joined, out_offset=bass.IndirectOffsetOnAxis(ap=at[:, q, u:u + 1], axis=0),
                                     in_=payload[:, q, u, :], in_offset=None).then_inc(out[q], 16)
    turn(0, True)
    with g.Fori(1, es.turns) as i:
        turn(i, False)
    for q in range(RING):
        g.wait_ge(out[q], 16 * PB * es.turns)


def gather_pairs(g, cs, table, ring, idx, idx_ready, slot_free, got, passed):
    with g.Fori(0, cs.loops) as i:
        for q in range(RING):
            g.wait_ge(slot_free, i * RING + (q + 1))
            g.tensor_copy(idx[:, q, :], cs.src_of[:, bass.ds(i * (TURN) + q * PB, PB)]).then_inc(idx_ready, 1)
            g.wait_ge(idx_ready, i * RING + (q + 1))
            g.sem_inc(passed, 1)
            for u in range(PB):
                g.indirect_dma_start(out=ring[:, q * PB + u, :], out_offset=None, in_=table,
                                     in_offset=bass.IndirectOffsetOnAxis(ap=idx[:, q, u:u + 1], axis=0)).then_inc(got[q], 16)


def load_tiles(eng, regs, cs, i, q):
    eng.load(regs, cs.tile_of[0:1, bass.ds(i * TURN + q * PB, PB)])
    return [eng.snap(r, min_val=0, max_val=NT - 1) for r in regs]


def load_local_rows(sp, cs, Lb, lb_got, hot_ready, passed, i, q):
    sp.wait_ge(hot_ready, i * RING + (q + 1))
    sp.sem_inc(passed, 1)
    rows = cs.local_rows[bass.ds(i * (TURN) + q * PB, PB), :].rearrange("r l -> (r l)")
    sp.dma_start(Lb[:, q, :], rows.partition_broadcast(TN)).then_inc(lb_got[q], 16)


def node_hots(nc, act, cs, Lb, hotT, dist, lb_got, hot_ready, dist_ready, i, q):
    act.wait_ge(lb_got[q], i * 16 + 16)
    act.sem_inc(dist_ready[1], 1)
    nc.scalar.activation(dist[:, q, :], Lb[:, q, :], ACT.Abs, bias=cs.neg_col[0:TN, :]).then_inc(dist_ready[0], 1)
    act.wait_ge(dist_ready[0], i * RING + (q + 1))
    nc.scalar.activation(hotT[:, q, :], dist[:, q, :], ACT.Relu, scale=-1.0, bias=1.0).then_inc(hot_ready, 1)


def edge_scores(nc, cs, q_dram, K, S, es, edge_index):
    with Phase(nc, "score") as ph:
        ring = ph.sb("ring", [P, TURN, D])
        idx = ph.sb("idx", [P, RING, PB], I32)
        Lb = ph.sb("Lb", [TN, RING, PB * P])
        hotT = ph.sb("hotT", [TN, RING, PB * P])
        dist = ph.sb("dist", [TN, RING, PB * P])
        prod = ph.sb("prod", [P, 2, PB * D])
        kd = [ph.psum(f"kd{q}", [P, PB * D]) for q in range(2)]
        idx_ready, hot_ready, kd_ready, multiplied, reduced, dist_ready, pool_on, sp_on, act_on, pe_on, dve_on = (
            ph.sem(k) for k in ("idx", "hot", "kd", "multiplied", "reduced", "dist", "pool_on", "sp_on", "act_on", "pe_on", "dve_on"))
        got = [ph.sem(f"got{q}") for q in range(RING)]
        lb_got = [ph.sem(f"lb{q}") for q in range(RING)]
        ranks = Ranks(ph, nc, cs, es, edge_index)

        def turns(eng, step, rank):
            with eng.Fori(0, es.turns) as i:
                for q in range(RING):
                    step(i, q)
                    rank(eng, i, q)
            with eng.Fori(es.turns, cs.loops) as i:
                for q in range(RING):
                    step(i, q)

        with nc.Block() as block:
            @block.gpsimd
            def _(g):
                gather_pairs(g, cs, q_dram, ring, idx, idx_ready, multiplied, got, pool_on)

            @block.sync
            def _(sp):
                turns(sp, lambda i, q: load_local_rows(sp, cs, Lb, lb_got, hot_ready, sp_on, i, q), ranks.load)

            @block.scalar
            def _(act):
                act.sem_inc(hot_ready, RING)
                ranks.start_scalar(act)

                def step(i, q):
                    act.wait_ge(kd_ready, i * RING + (q + 1))
                    act.sem_inc(act_on, 1)
                    node_hots(nc, act, cs, Lb, hotT, dist, lb_got, hot_ready, (dist_ready, act_on), i, q)
                step(0, 0)
                with act.Fori(0, es.turns) as i:
                    for q in range(RING):
                        step(i + (q + 1) // RING, (q + 1) % RING)
                        ranks.scalar(act, i, q)
                for q in range(1, RING):
                    step(es.turns, q)
                with act.Fori(es.turns + 1, cs.loops) as i:
                    for q in range(RING):
                        step(i, q)

            @block.tensor
            def _(pe):
                pe.sem_inc(kd_ready, RING)
                ranks.start_tensor(pe)
                regs = [pe.alloc_register(f"{ph.name}_tile{u}") for u in range(PB)]

                def step(i, q):
                    pe.wait_ge(hot_ready, i * RING + (RING + q + 1))
                    pe.sem_inc(pe_on, 1)
                    pe.wait_ge(multiplied, i * RING + (q + 3))
                    pe.sem_inc(pe_on, 1)
                    tiles = load_tiles(pe, regs, cs, i, q)
                    for u in range(PB):
                        ins = pe.matmul(kd[q % 2][:, u * D:(u + 1) * D], hotT[:, q, u * P:(u + 1) * P], K[:, tiles[u], :], start=True, stop=True)
                    ins.then_inc(kd_ready, 1)
                turns(pe, step, ranks.tensor)

            @block.vector
            def _(v):
                v.sem_inc(multiplied, RING)
                v.sem_inc(reduced, 2)
                ranks.start_vector(v)

                def multiply(i, q):
                    v.wait_ge(got[q], i * (16 * PB) + 16 * PB)
                    v.sem_inc(dve_on, 1)
                    v.wait_ge(reduced, i * RING + (q + 1))
                    v.sem_inc(dve_on, 1)
                    v.wait_ge(kd_ready, i * RING + (RING + q + 1))
                    v.tensor_tensor(prod[:, q % 2, :], kd[q % 2][:], ring[:, q * PB:(q + 1) * PB, :].rearrange("p u d -> p (u d)"),
                                    ALU.mult).then_inc(multiplied, 1)

                def reduce(i, q):
                    v.wait_ge(multiplied, i * RING + (RING + q + 1))
                    v.sem_inc(dve_on, 1)
                    v.tensor_reduce(S[:, bass.ds(i * (TURN) + q * PB, PB), :].rearrange("p u h -> p (u h)"),
                                    prod[:, q % 2, :].rearrange("p (g d) -> p g d", d=D // H), AX.X, ALU.add).then_inc(reduced, 1)

                with v.Fori(0, es.turns) as i:
                    for q in range(RING):
                        multiply(i, q)
                        ranks.compare(v, i, q)
                        reduce(i, q)
                        ranks.place(v, i, q)
                with v.Fori(es.turns, cs.loops) as i:
                    for q in range(RING):
                        multiply(i, q)
                        reduce(i, q)
                v.wait_ge(reduced, cs.loops * RING + 2)
                ranks.end_vector(v)


def segment_max(nc, cs, name, S, heads, M, carry_dram):
    B = P // heads
    NB = cs.pairs // B
    R = cs.pairs * heads
    with Phase(nc, name) as ph:
        T = ph.sb("T", [P, NB, P])
        fwd = ph.sb("fwd", [P, NB, P])
        bwd = ph.sb("bwd", [P, NB, P])
        n_start = ph.sb("n_start", [P, NB, P])
        n_end = ph.sb("n_end", [P, NB, P])
        side = ph.sb("side", [P, 4, NB])
        lane0 = ph.sb("lane0", [P, NB])
        lane127 = ph.sb("lane127", [P, NB])
        sideT = ph.sb("sideT", [4 * NB, P])
        line = ph.sb("line", [1, 2, R + 2 * heads])
        cinT = ph.sb("cinT", [2 * NB, P])
        pt = [ph.psum(f"pt{b}", [P, P]) for b in range(4)]
        pc = ph.psum("pc", [P, P])
        keys_in, masked, turned, copied, sides, sideturned, side_out, side_stored, line_in, carried, cin_stored, cin_in, cinturned, joined, back, used, v_link = (
            ph.sem(k) for k in ("keys", "masked", "turned", "copied", "sides", "sideturned", "side_out", "side_stored", "line", "carried",
                                "cin_stored", "cin_in", "cinturned", "joined", "back", "used", "link"))

        def key_view(k):
            return bass.AP(cs.keys_t, k, [[P, B], [0, heads], [B * P, NB], [1, P]])

        flat = "p b l -> p (b l)"
        side_d, cin_d = carry_dram
        with nc.Block() as block:
            @block.sync
            def _(sp):
                for k, dest in enumerate((n_start, fwd, n_end)):
                    for b in range(NB):
                        sp.dma_start(dest[:, b, :], bass.AP(cs.keys_t, k + b * B * P, [[P, B], [0, heads], [1, P]])).then_inc(keys_in, 16)
                sp.wait_ge(side_out, 1)
                sp.dma_start(side_d, sideT[:]).then_inc(side_stored, 16)
                sp.wait_ge(side_stored, 16)
                sp.wait_ge(carried, 1)
                for k in range(2):
                    sp.dma_start(line[:, :, heads:R + heads],
                                 side_d[k * 2 * NB:(k + 1) * 2 * NB, :].rearrange("(a s b) r -> a s (b r)", a=1, s=2)).then_inc(line_in, 16)
                    sp.wait_ge(carried, k + 2)
                    sp.dma_start(cin_d[k * NB:(k + 1) * NB, :].rearrange("(a b) r -> a (b r)", a=1),
                                 line[:, 0, 2 * k * heads:2 * k * heads + R]).then_inc(cin_stored, 16)
                    sp.wait_ge(cin_stored, 16 * (k + 1))
                sp.wait_ge(cin_stored, 32)
                sp.dma_start(cinT[:], cin_d).then_inc(cin_in, 16)

            @block.tensor
            def _(pe):
                pe.wait_ge(masked, 1)
                for b in range(NB):
                    if b >= 4:
                        pe.wait_ge(copied, b - 3)
                    pe.transpose(pt[b % 4][:], S[:, b * B:(b + 1) * B, :].rearrange("p a h -> p (a h)"), cs.ident[:]).then_inc(turned, 1)
                pe.wait_ge(sides, 1)
                pe.transpose(pc[0:4 * NB, :], side[:].rearrange("p s b -> p (s b)"), cs.ident[:]).then_inc(sideturned, 1)
                pe.wait_ge(cin_in, 16)
                pe.wait_ge(side_out, 1)
                pe.transpose(pc[:, 0:2 * NB], cinT[:], cs.ident[0:2 * NB, 0:2 * NB]).then_inc(cinturned, 1)
                pe.wait_ge(joined, 1)
                pe.wait_ge(copied, NB)
                for b in range(NB):
                    if b >= 4:
                        pe.wait_ge(used, b - 3)
                    pe.transpose(pt[b % 4][:], fwd[:, b, :], cs.ident[:]).then_inc(back, 1)

            @block.scalar
            def _(act):
                for b in range(NB):
                    act.wait_ge(turned, b + 1)
                    nc.scalar.copy(T[:, b, :], pt[b % 4][:]).then_inc(copied, 1)
                act.wait_ge(sideturned, 1)
                nc.scalar.copy(sideT[:], pc[0:4 * NB, :]).then_inc(side_out, 1)
                for b in range(NB):
                    act.wait_ge(back, b + 1)
                    nc.scalar.copy(M[:, b * B:(b + 1) * B, :].rearrange("p a h -> p (a h)"), pt[b % 4][:]).then_inc(used, 1)
                act.wait_ge(used, NB)

            @block.vector
            def _(v):
                v.tensor_tensor(S[:], S[:], cs.neg_big[:].unsqueeze(2).to_broadcast([P, cs.pairs, heads]), ALU.add).then_inc(masked, 1)
                link = chain(v, v_link)
                v.wait_ge(keys_in, 48 * NB)
                link(v.tensor_tensor(n_start[:], n_start[:], fwd[:], ALU.not_equal))
                link(v.tensor_tensor(n_end[:], n_end[:], fwd[:], ALU.not_equal))
                link(v.tensor_scalar(n_start[:], n_start[:], -BIG, None, ALU.mult))
                link(v.tensor_scalar(n_end[:], n_end[:], -BIG, None, ALU.mult))
                link(v.tensor_copy(lane0[:], n_start[:, :, 0]))
                link(v.tensor_copy(lane127[:], n_end[:, :, P - 1]))
                link(v.tensor_reduce(side[:, 1, :], n_start[:], AX.X, ALU.min))
                link(v.tensor_reduce(side[:, 3, :], n_end[:], AX.X, ALU.min))
                link(v.memset(n_start[:, :, 0], -BIG))
                link(v.memset(n_end[:, :, P - 1], -BIG))
                v.wait_ge(copied, NB)

                def scans():
                    link(v.tensor_tensor_scan(fwd[:].rearrange(flat), n_start[:].rearrange(flat), T[:].rearrange(flat),
                                              -BIG, ALU.add, ALU.max))
                    link(v.tensor_tensor_scan(bwd[:].rearrange(flat)[:, ::-1], n_end[:].rearrange(flat)[:, ::-1], T[:].rearrange(flat)[:, ::-1],
                                              -BIG, ALU.add, ALU.max))
                scans()
                link(v.tensor_copy(side[:, 0, :], fwd[:, :, P - 1]))
                v.tensor_copy(side[:, 2, :], bwd[:, :, 0]).then_inc(sides, 1)
                link(v.memset(line[:], -BIG))
                v.sem_inc(carried, 1)
                for k in range(2):
                    v.wait_ge(line_in, 16 * (k + 1))
                    way = 1 - 2 * k
                    for h in range(heads):
                        of = lambda r: line[:, r, heads:R + heads].rearrange("a (r h) -> a h r", h=heads)[:, h, ::way]
                        link(v.tensor_tensor_scan(of(0), of(1), of(0), -BIG, ALU.add, ALU.max))
                    v.sem_inc(carried, 1)
                v.wait_ge(cinturned, 1)
                link(v.tensor_tensor(lane0[:], lane0[:], pc[:, 0:NB], ALU.add))
                link(v.tensor_tensor(lane127[:], lane127[:], pc[:, NB:2 * NB], ALU.add))
                link(v.tensor_tensor(T[:, :, 0], T[:, :, 0], lane0[:], ALU.max))
                link(v.tensor_tensor(T[:, :, P - 1], T[:, :, P - 1], lane127[:], ALU.max))
                scans()
                v.tensor_tensor(fwd[:], fwd[:], bwd[:], ALU.max).then_inc(joined, 1)


def edge_weights(nc, name, S, M, Wt):
    with Phase(nc, name) as ph:
        shifted = ph.sem("shifted")
        raised = ph.sem("raised")
        with nc.Block() as block:
            @block.vector
            def _(v):
                v.tensor_tensor(S[:], S[:], M[:], ALU.subtract).then_inc(shifted, 1)

            @block.scalar
            def _(act):
                act.wait_ge(shifted, 1)
                nc.scalar.activation(Wt, S[:], ACT.Exp).then_inc(raised, 1)
                act.wait_ge(raised, 1)


def lane_hots(nc, act, cs, hot, dist, hot_free, hot_ready, dist_ready, act_on):
    with act.Fori(0, cs.loops) as i:
        for q in range(RING):
            act.wait_ge(hot_free, i * RING + (q + 1))
            act.sem_inc(act_on, 1)
            for u in range(PB):
                p = i * (TURN) + (q * PB + u)
                ins = nc.scalar.activation(dist[:, q, u, :], cs.count_row[:, 0:TN], ACT.Abs, bias=cs.neg_local[:, bass.ds(p, 1)])
            ins.then_inc(dist_ready, 1)
            act.wait_ge(dist_ready, i * RING + (q + 1))
            nc.scalar.activation(hot[:, q, :, :], dist[:, q, :, :], ACT.Relu, scale=-1.0, bias=1.0).then_inc(hot_ready, 1)


def weigh_values(nc, cs, v_dram, Wt, acc):
    C = D + H + 1
    with Phase(nc, "value") as ph:
        ring = ph.sb("ring", [P, TURN, D])
        idx = ph.sb("idx", [P, RING, PB], I32)
        hot = ph.sb("hot", [P, RING, PB, TN])
        dist = ph.sb("dist", [P, RING, PB, TN])
        wv = ph.sb("wv", [P, RING, PB, D])
        part = [ph.psum(f"part{u}", [TN, 512]) for u in range(2 * PB)]
        idx_ready, hot_ready, weighed, summed, added, dist_ready, pool_on, act_on, pe_on, dve_on = (
            ph.sem(k) for k in ("idx", "hot", "weighed", "summed", "added", "dist", "pool_on", "act_on", "pe_on", "dve_on"))
        cleared = ph.sem("cleared")
        got = [ph.sem(f"got{q}") for q in range(RING)]
        HB = PB // 2
        with nc.Block() as block:
            @block.gpsimd
            def _(g):
                gather_pairs(g, cs, v_dram, ring, idx, idx_ready, weighed, got, pool_on)

            @block.scalar
            def _(act):
                lane_hots(nc, act, cs, hot, dist, summed, hot_ready, dist_ready, act_on)

            @block.vector
            def _(v):
                v.memset(acc[:], 0.0).then_inc(cleared, 1)
                v.wait_ge(cleared, 1)
                v.sem_inc(weighed, RING)
                v.sem_inc(added, 2 * PB)
                regs = [v.alloc_register(f"{ph.name}_vtile{u}") for u in range(PB)]

                def weigh(i, q):
                    v.wait_ge(got[q], i * (16 * PB) + 16 * PB)
                    v.sem_inc(dve_on, 1)
                    v.wait_ge(summed, i * RING + (q + 1))
                    v.sem_inc(dve_on, 1)
                    w = Wt[:, bass.ds(i * TURN + q * PB, PB), 0:H]
                    v.tensor_tensor(wv[:, q, :, :].rearrange("p u (h d) -> p u h d", h=H),
                                    ring[:, q * PB:(q + 1) * PB, :].rearrange("p u (h d) -> p u h d", h=H),
                                    w.unsqueeze(3).to_broadcast([P, PB, H, D // H]), ALU.mult).then_inc(weighed, 1)

                def add(i, q):
                    tiles = load_tiles(v, regs, cs, i, q)
                    v.wait_ge(summed, i * RING + (RING + q + 1))
                    v.sem_inc(dve_on, 1)
                    for u in range(PB):
                        v.wait_ge(added, i * TURN + (q * PB + u + 2 * PB))
                        v.sem_inc(dve_on, 1)
                        sum_ = acc[:, tiles[u], :]
                        v.tensor_tensor(sum_, sum_, part[(q % 2) * PB + u][:, 0:C], ALU.add).then_inc(added, 1)

                for q in range(RING):
                    weigh(0, q)
                    if q:
                        add(0, q - 1)
                with v.Fori(1, cs.loops) as i:
                    for q in range(RING):
                        weigh(i, q)
                        add(i if q else i - 1, (q - 1) % RING)
                add(cs.loops - 1, RING - 1)
                v.wait_ge(added, cs.pairs + 2 * PB)

            @block.tensor
            def _(pe):
                pe.sem_inc(summed, RING)
                with pe.Fori(0, cs.loops) as i:
                    for q in range(RING):
                        pe.wait_ge(hot_ready, i * RING + (q + 1))
                        pe.sem_inc(pe_on, 1)
                        pe.wait_ge(weighed, i * RING + (RING + q + 1))
                        pe.sem_inc(pe_on, 1)
                        pe.wait_ge(added, i * (TURN) + (q * PB + PB))
                        pe.sem_inc(pe_on, 1)
                        for u in range(PB):
                            p = i * (TURN) + (q * PB + u)
                            out = part[(q % 2) * PB + u]
                            pe.matmul(out[:, 0:D], hot[:, q, u, :], wv[:, q, u, :], start=True, stop=True)
                            ins = pe.matmul(out[:, D:C], hot[:, q, u, :], Wt[:, p, :], start=True, stop=True)
                        ins.then_inc(summed, 1)


def neighbour_sums(nc, name, cs, table, width, acc, bias_rows=None):
    per_bank = 512 // width
    with Phase(nc, name) as ph:
        ring = ph.sb("ring", [P, TURN, width])
        idx = ph.sb("idx", [P, RING, PB], I32)
        hot = ph.sb("hot", [P, RING, PB, TN])
        dist = ph.sb("dist", [P, RING, PB, TN])
        zero = ph.sb("zero", [1, 512])
        idx_ready, hot_ready, summed, dist_ready, zeroed, pool_on, act_on, pe_on = (
            ph.sem(k) for k in ("idx", "hot", "summed", "dist", "zeroed", "pool_on", "act_on", "pe_on"))
        got = [ph.sem(f"got{q}") for q in range(RING)]
        with nc.Block() as block:
            @block.vector
            def _(v):
                v.memset(zero[:], 0.0).then_inc(zeroed, 1)

            @block.gpsimd
            def _(g):
                gather_pairs(g, cs, table, ring, idx, idx_ready, summed, got, pool_on)

            @block.scalar
            def _(act):
                lane_hots(nc, act, cs, hot, dist, summed, hot_ready, dist_ready, act_on)

            @block.tensor
            def _(pe):
                pe.wait_ge(zeroed, 1)
                for b in range((NT + per_bank - 1) // per_bank):
                    pe.matmul(acc[:, b * 512:(b + 1) * 512], zero[:, 0:TN], zero[:], start=True, stop=True)
                pe.sem_inc(summed, RING)
                regs = [pe.alloc_register(f"{ph.name}_tile{u}") for u in range(PB)]
                with pe.Fori(0, cs.loops) as i:
                    for q in range(RING):
                        pe.wait_ge(hot_ready, i * RING + (q + 1))
                        pe.sem_inc(pe_on, 1)
                        pe.wait_ge(got[q], i * (16 * PB) + 16 * PB)
                        pe.sem_inc(pe_on, 1)
                        tiles = load_tiles(pe, regs, cs, i, q)
                        for u in range(PB):
                            p = i * (TURN) + (q * PB + u)
                            tile = tiles[u]
                            ins = pe.matmul(acc[:, bass.ds(tile * width, width)], hot[:, q, u, :], ring[:, q * PB + u, :],
                                            start=False, stop=True, skip_group_check=True)
                        ins.then_inc(summed, 1)
                pe.wait_ge(summed, cs.loops * RING + RING)


def experts(nc, name, cs, UT, Y, gates, w1, b1, w2, b2, n_experts, func):
    F = 512
    FT = F // P
    CT = 5
    CW = CT * TN
    halves = [(0, 313), (313, CW)]
    with Phase(nc, name) as ph:
        W1 = ph.sb("W1", [P, 2, 2, F])
        W2 = ph.sb("W2", [P, 2, FT, D])
        B2 = ph.sb("B2", [TN, 2, D])
        brow = ph.sb("brow", [n_experts * FT, P])
        bcol = ph.sb("bcol", [P, n_experts * FT])
        hidden = ph.sb("hidden", [P, 2, FT, CW])
        plus = ph.sb("plus", [TN, 2, D])
        hp = [ph.psum(f"hp{k}", [P, 2, 512]) for k in range(2)]
        yp = [ph.psum(f"yp{k}", [TN, D]) for k in range(2)]
        bp = ph.psum("bp", [P, n_experts * FT])
        b_in, b_turned, b_ready, up, acted, down, added, biased, act_on, sp_on, dve_on = (
            ph.sem(k) for k in ("b_in", "b_turned", "b_ready", "up", "acted", "down", "added", "biased", "act_on", "sp_on", "dve_on"))
        w_in = [ph.sem(f"w_in{k}") for k in range(2)]
        NW = 3 if b2 is not None else 2
        C = 50
        with nc.Block() as block:
            @block.sync
            def _(sp):
                sp.dma_start(brow[:], b1.rearrange("e (f p) -> (e f) p", p=P)).then_inc(b_in, 16)
                with sp.Fori(0, n_experts // 2) as i:
                    for k in range(2):
                        sp.wait_ge(down, i * 50 + (25 * k + 25))
                        sp.sem_inc(sp_on, 1)
                        if b2 is not None:
                            sp.wait_ge(biased, i * 50 + (25 * k + 25))
                            sp.sem_inc(sp_on, 1)
                        e = i * 2 + k
                        sp.dma_start(W1[:, k, :, :], w1[bass.ds(e, 1), :, :].rearrange("e (c p) f -> p (e c) f", p=P)).then_inc(w_in[k], 16)
                        sp.dma_start(W2[:, k, :, :], w2[bass.ds(e, 1), :, :].rearrange("e (c p) d -> p (e c) d", p=P)).then_inc(w_in[k], 16)
                        if b2 is not None:
                            sp.dma_start(B2[:, k, :], b2[bass.ds(e, 1), :].rearrange("e d -> (e d)").partition_broadcast(TN)).then_inc(w_in[k], 16)

            @block.tensor
            def _(pe):
                pe.wait_ge(b_in, 16)
                pe.transpose(bp[:], brow[:], cs.ident[0:n_experts * FT, 0:n_experts * FT]).then_inc(b_turned, 1)
                pe.sem_inc(down, C)
                with pe.Fori(0, n_experts // 2) as i:
                    for k in range(2):
                        pe.wait_ge(w_in[k], i * (16 * NW) + 16 * NW)
                        pe.sem_inc(sp_on, 1)
                        for c in range(5):
                            n = 5 * k + c
                            for f in range(FT):
                                pe.wait_ge(acted, i * 40 + (n * FT + f + 1))
                                for (lo, hi) in halves:
                                    for kk in range(2):
                                        ins = pe.matmul(hp[f % 2][:, lo // 313, 0:hi - lo], W1[:, k, kk, f * P:(f + 1) * P],
                                                        UT[:, kk, c * CW + lo:c * CW + hi], start=(kk == 0), stop=(kk == 1))
                                ins.then_inc(up, 1)
                            pe.wait_ge(acted, i * 40 + (n * FT + FT + 2))
                            for t in range(CT):
                                m = n * CT + t
                                pe.wait_ge(added, i * 50 + (m + 1))
                                for f in range(FT):
                                    ins = pe.matmul(yp[m % 2][:], hidden[:, n % 2, f, t * TN:(t + 1) * TN], W2[:, k, f, :],
                                                    start=(f == 0), stop=(f == FT - 1))
                                ins.then_inc(down, 1)

            @block.scalar
            def _(act):
                act.sem_inc(acted, 2)
                with act.Fori(0, n_experts // 2) as i:
                    for n in range(10):
                        act.wait_ge(down, i * 50 + (5 * n + C - 5))
                        act.sem_inc(act_on, 1)
                        if n == 0:
                            act.wait_ge(b_ready, 1)
                        for f in range(FT):
                            act.wait_ge(up, i * 40 + (n * FT + f + 1))
                            act.sem_inc(act_on, 1)
                            bias = bcol[:, bass.ds(i * (2 * FT) + ((n // 5) * FT + f), 1)]
                            for (lo, hi) in halves:
                                ins = nc.scalar.activation(hidden[:, n % 2, f, lo:hi], hp[f % 2][:, lo // 313, 0:hi - lo], func, bias=bias)
                            ins.then_inc(acted, 1)

            @block.vector
            def _(v):
                v.wait_ge(b_turned, 1)
                v.tensor_copy(bcol[:], bp[:]).then_inc(b_ready, 1)
                v.sem_inc(added, 2)
                v.sem_inc(biased, C)
                with v.Fori(0, n_experts // 2) as i:
                    for m in range(50):
                        v.wait_ge(down, i * 50 + (m + 1 + C))
                        k, t = m // 25, m % 25
                        y = yp[m % 2][:]
                        if b2 is not None:
                            v.tensor_tensor(plus[:, m % 2, :], y, B2[:, k, :], ALU.add).then_inc(biased, 1)
                            v.wait_ge(biased, i * 50 + (m + 1 + C))
                            y = plus[:, m % 2, :]
                        v.sem_inc(dve_on, 1)
                        v.scalar_tensor_tensor(out=Y[:, t, :], in0=y, scalar=gates[:, t, bass.ds(i * 2 + k, 1)], in1=Y[:, t, :],
                                               op0=ALU.mult, op1=ALU.add).then_inc(added, 1)
                v.wait_ge(added, n_experts * 25 + 2)


N_EXP, F_EXP = 16, 512
SLOT_TILES = (2 * N + N_EXP * (P - 1)) // P
X_TILES = SLOT_TILES + 3
OWNERS = SLOT_TILES + 4


def start_loads(nc, pairs, sem):
    with nc.Block() as block:
        @block.sync
        def _(sp):
            for dest, source in pairs:
                sp.dma_start(dest, source).then_inc(sem, 16)


def route(nc, cs, hots, pos, expert_of):
    W = NT * N_EXP
    with Phase(nc, "route") as ph:
        upper = ph.sb("upper", [TN, TN])
        both = ph.sb("both", [TN, NT, N_EXP])
        tot = ph.sb("tot", [TN, N_EXP, NT])
        keep = ph.sb("keep", [TN, N_EXP, NT])
        incl = ph.sb("incl", [TN, N_EXP, NT])
        tiles_i = ph.sb("tiles_i", [TN, N_EXP], I32)
        tiles, upto, zeros = (ph.sb(k, [TN, N_EXP]) for k in ("tiles", "upto", "zeros"))
        place = ph.sb("place", [TN, NT, N_EXP])
        pick = ph.sb("pick", [TN, NT, N_EXP])
        pos_f = ph.sb("pos_f", [TN, NT, 2])
        owner = ph.sb("owner", [1, OWNERS, N_EXP])
        owner_f = ph.sb("owner_f", [1, OWNERS])
        pw, pt = ph.psum("pw", [TN, 512]), ph.psum("pt", [TN, 512])
        made, ready, summed, link_s = (ph.sem(k) for k in ("made", "ready", "summed", "link"))
        by_expert = "p t e -> p e t"
        with nc.Block() as block:
            @block.gpsimd
            def _(g):
                link = chain(g, made)
                link(g.memset(upper[:], 1.0))
                link(g.affine_select(out=upper[:], in_=upper[:], compare_op=ALU.is_gt, fill=0.0, base=0,
                                     pattern=[[1, TN]], channel_multiplier=-1))

            @block.tensor
            def _(pe):
                pe.wait_ge(made, 2)
                pe.wait_ge(ready, 1)
                flat = both[:].rearrange("p t e -> p (t e)")
                pe.matmul(pw[:, 0:W], upper[:], flat, start=True, stop=True)
                pe.matmul(pt[:, 0:W], cs.ones[0:TN, 0:TN], flat, start=True, stop=True).then_inc(summed, 1)

            @block.vector
            def _(v):
                link = chain(v, link_s)
                v.tensor_tensor(both[:], hots[:, :, 0, :], hots[:, :, 1, :], ALU.add).then_inc(ready, 1)
                link(v.memset(keep[:], 1.0))
                link(v.memset(keep[:, :, 0], 0.0))
                link(v.memset(zeros[:], 0.0))
                v.wait_ge(summed, 1)
                tot_p = pt[:, 0:W].rearrange("p (t e) -> p t e", e=N_EXP).rearrange(by_expert)
                link(v.tensor_copy(tot[:], tot_p))
                link(v.tensor_tensor_scan(incl[:].rearrange("p e t -> p (e t)"), keep[:].rearrange("p e t -> p (e t)"),
                                          tot[:].rearrange("p e t -> p (e t)"), 0.0, ALU.mult, ALU.add))
                link(v.tensor_scalar(tiles_i[:], incl[:, :, NT - 1], float(P - 1), None, ALU.add))
                link(v.tensor_scalar(tiles_i[:], tiles_i[:], 7, None, ALU.arith_shift_right))
                link(v.tensor_copy(tiles[:], tiles_i[:]))
                link(v.tensor_tensor_scan(upto[:], zeros[:], tiles[:], 0.0, ALU.add, ALU.add))
                link(v.tensor_tensor(upto[:], upto[:], tiles[:], ALU.subtract))
                link(v.tensor_tensor(incl[:], incl[:], tot[:], ALU.subtract))
                link(v.tensor_tensor(place[:], pw[:, 0:W].rearrange("p (t e) -> p t e", e=N_EXP), incl[:].rearrange("p e t -> p t e"),
                                     ALU.add))
                link(v.scalar_tensor_tensor(out=tiles[:], in0=upto[:], scalar=float(P), in1=zeros[:], op0=ALU.mult, op1=ALU.add))
                link(v.tensor_tensor(place[:], place[:], tiles[:].unsqueeze(1).to_broadcast([TN, NT, N_EXP]), ALU.add))
                for k in range(2):
                    link(v.tensor_tensor(pick[:], place[:], hots[:, :, k, :], ALU.mult))
                    link(v.tensor_reduce(pos_f[:, :, k], pick[:], AX.X, ALU.add))
                link(v.tensor_copy(pos[:], pos_f[:]))
                link(v.tensor_tensor(owner[:], upto[0:1, :].unsqueeze(1).to_broadcast([1, OWNERS, N_EXP]),
                                     cs.count_row[0:1, 0:OWNERS].unsqueeze(2).to_broadcast([1, OWNERS, N_EXP]), ALU.is_le))
                link(v.tensor_reduce(owner_f[:], owner[:], AX.X, ALU.add))
                link(v.tensor_scalar(owner_f[:], owner_f[:], -1.0, None, ALU.add))
                link(v.tensor_copy(expert_of[:], owner_f[:]))


def send_rows(nc, rows, pos, x_slots):
    with Phase(nc, "send") as ph:
        ring = ph.sb("ring", [TN, 5, D])
        at = ph.sb("at", [TN, 5, 2], I32)
        ready, pool_on, dve_on, sp_on = (ph.sem(k) for k in ("ready", "pool_on", "dve_on", "sp_on"))
        row_in = [ph.sem(f"row_in{s}") for s in range(5)]
        sent = [ph.sem(f"sent{s}") for s in range(5)]
        with nc.Block() as block:
            @block.gpsimd
            def _(g):
                with g.Fori(0, 5) as i:
                    for s in range(5):
                        g.wait_ge(ready, i * 5 + (s + 1))
                        g.sem_inc(pool_on, 1)
                        g.wait_ge(row_in[s], i * 16 + 16)
                        g.sem_inc(pool_on, 1)
                        for k in range(2):
                            g.indirect_dma_start(out=x_slots, out_offset=bass.IndirectOffsetOnAxis(ap=at[:, s, k:k + 1], axis=0),
                                                 in_=ring[:, s, :], in_offset=None).then_inc(sent[s], 16)
                for s in range(5):
                    g.wait_ge(sent[s], 5 * 32)

            @block.sync
            def _(sp):
                def load(i, first):
                    for s in range(5):
                        if not first:
                            sp.wait_ge(sent[s], i * 32)
                            sp.sem_inc(sp_on, 1)
                        sp.dma_start(ring[:, s, :], rows[bass.ds((i * 5 + s) * TN, TN), :]).then_inc(row_in[s], 16)
                load(0, True)
                with sp.Fori(1, 5) as i:
                    load(i, False)

            @block.vector
            def _(v):
                def fill(i, first):
                    for s in range(5):
                        if not first:
                            v.wait_ge(sent[s], i * 32)
                            v.sem_inc(dve_on, 1)
                        v.tensor_copy(at[:, s, :], pos[:, i * 5 + s, :]).then_inc(ready, 1)
                fill(0, True)
                with v.Fori(1, 5) as i:
                    fill(i, False)


def slot_experts(nc, cs, x_slots, y_slots, W1, W2, b1, b2, expert_of, up_in, down_in, es, joined):
    FT = F_EXP // P
    with Phase(nc, "slot") as ph:
        x = ph.sb("x", [P, 4, D])
        xT = ph.sb("xT", [P, 2, 2, P])
        h = ph.sb("h", [P, 2, F_EXP])
        hT = ph.sb("hT", [P, 2, FT, P])
        y = ph.sb("y", [P, 4, D])
        B2 = ph.sb("B2", [P, 4, D])
        brow = ph.sb("brow", [N_EXP * FT, P])
        bcol = ph.sb("bcol", [P, N_EXP * FT])
        x_ps = [ph.psum(f"x_ps{k}", [P, 4, P]) for k in range(2)]
        h_ps = [ph.psum(f"h_ps{k}", [P, F_EXP]) for k in range(2)]
        hT_ps = [ph.psum(f"hT_ps{k}", [P, FT, P]) for k in range(2)]
        y_ps = [ph.psum(f"y_ps{k}", [P, 512]) for k in range(2)]
        b_in, b_turned, b_ready, x_turned, x_copied, up, h_copied, h_turned, relued, down, y_ready, pe_on, act_on, dve_on, sp_on, pool_on = (
            ph.sem(k) for k in ("b_in", "b_turned", "b_ready", "x_turned", "x_copied", "up", "h_copied", "h_turned", "relued", "down",
                                "y_ready", "pe_on", "act_on", "dve_on", "sp_on", "pool_on"))
        x_in = [ph.sem(f"x_in{q}") for q in range(4)]
        y_out = [ph.sem(f"y_out{q}") for q in range(4)]
        bias_in = [ph.sem(f"bias_in{q}") for q in range(4)]
        b2_line = b2.rearrange("e d -> (e d)")
        at = ph.sb("at", [P, RING, PB], I32)
        payload = ph.sb("payload", [P, RING, PB, 2], I32)
        edges_copied = ph.sem("edges_copied")
        edges_out = [ph.sem(f"edges_out{q}") for q in range(RING)]
        TURNS = SLOT_TILES // 4

        def store_y(sp, i, q):
            sp.dma_start(y_slots[bass.ds(i * (4 * P) + q * P, P), :], y[:, q, :]).then_inc(y_out[q], 16)

        def load_x(sp, i, q):
            sp.dma_start(x[:, q, :], x_slots[bass.ds(i * (4 * P) + q * P, P), :]).then_inc(x_in[q], 16)

        with nc.Block() as block:
            @block.sync
            def _(sp):
                sp.dma_start(brow[:], b1.rearrange("e (f p) -> (e f) p", p=P)).then_inc(b_in, 16)
                regs = [sp.alloc_register(f"{ph.name}_sexpert{u}") for u in range(4)]

                def experts_of(i):
                    sp.load(regs, expert_of[0:1, bass.ds(i * 4, 4)])
                    return [sp.snap(r, min_val=0, max_val=N_EXP - 1) for r in regs]

                def load_bias(q, e):
                    sp.dma_start(B2[:, q, :], b2_line[bass.ds(e * D, D)].partition_broadcast(P)).then_inc(bias_in[q], 16)

                e = experts_of(0)
                for q in range(4):
                    load_x(sp, 0, q)
                    load_bias(q, e[q])
                with sp.Fori(1, TURNS) as i:
                    e = experts_of(i)
                    for q in range(4):
                        sp.wait_ge(x_turned, i * 4 + (q - 3))
                        sp.sem_inc(sp_on, 1)
                        load_x(sp, i, q)
                        sp.wait_ge(y_ready, i * 4 + (q - 1))
                        sp.sem_inc(sp_on, 1)
                        store_y(sp, i - 1, q)
                        load_bias(q, e[q])
                for q in range(3):
                    sp.wait_ge(x_turned, SLOT_TILES + q - 3)
                    load_x(sp, TURNS, q)
                for q in range(4):
                    sp.wait_ge(y_ready, SLOT_TILES + q - 1)
                    store_y(sp, TURNS - 1, q)
                for q in range(4):
                    sp.wait_ge(y_out[q], 16 * TURNS)

            @block.tensor
            def _(pe):
                regs = [pe.alloc_register(f"{ph.name}_expert{u}") for u in range(8)]

                def turn_x(i, k):
                    pe.wait_ge(x_in[k % 4], (i + k // 4) * 16 + 16)
                    pe.sem_inc(pe_on, 1)
                    pe.wait_ge(x_copied, i * 4 + (k + 1))
                    pe.sem_inc(pe_on, 1)
                    for c in range(2):
                        ins = pe.transpose(x_ps[k % 2][:, c, :], x[:, k % 4, c * P:(c + 1) * P], cs.ident[:])
                    ins.then_inc(x_turned, 1)

                def layer1(i, k, e):
                    pe.wait_ge(x_copied, i * 4 + (k + 3))
                    pe.sem_inc(pe_on, 1)
                    pe.wait_ge(h_copied, i * 4 + (k + 1))
                    pe.sem_inc(pe_on, 1)
                    for c in range(2):
                        ins = pe.matmul(h_ps[k % 2][:], xT[:, k % 2, c, :], W1[:, e, c, :], start=(c == 0), stop=(c == 1))
                    ins.then_inc(up, 1)

                def turn_h(i, k):
                    pe.wait_ge(h_copied, i * 4 + (k + 3))
                    pe.sem_inc(pe_on, 1)
                    pe.wait_ge(relued, i * 4 + (k + 1))
                    pe.sem_inc(pe_on, 1)
                    for f in range(FT):
                        ins = pe.transpose(hT_ps[k % 2][:, f, :], h[:, k % 2, f * P:(f + 1) * P], cs.ident[:])
                    ins.then_inc(h_turned, 1)

                def layer2(i, k, e):
                    pe.wait_ge(relued, i * 4 + (k + 3))
                    pe.sem_inc(pe_on, 1)
                    pe.wait_ge(y_ready, i * 4 + (k + 1))
                    pe.sem_inc(pe_on, 1)
                    for f in range(FT):
                        ins = pe.matmul(y_ps[k % 2][:, 0:D], hT[:, k % 2, f, :], W2[:, e, f, :], start=(f == 0), stop=(f == FT - 1))
                    ins.then_inc(down, 1)

                def experts_of(i):
                    pe.load(regs[0:4], expert_of[0:1, bass.ds(i * 4, 4)])
                    pe.load(regs[4:8], expert_of[0:1, bass.ds(i * 4 + 4, 4)])
                    return [pe.snap(r, min_val=0, max_val=N_EXP - 1) for r in regs]

                pe.wait_ge(b_in, 16)
                pe.transpose(h_ps[0][:, 0:N_EXP * FT], brow[:], cs.ident[0:N_EXP * FT, 0:N_EXP * FT]).then_inc(b_turned, 1)
                pe.wait_ge(b_ready, 1)
                pe.sem_inc(up, 2)
                pe.sem_inc(h_turned, 2)
                pe.sem_inc(down, 2)
                pe.wait_ge(up_in, 16)
                pe.wait_ge(down_in, 16)
                e = experts_of(0)
                for k in range(3):
                    turn_x(0, k)
                for k in range(2):
                    layer1(0, k, e[k])
                turn_h(0, 0)
                with pe.Fori(0, TURNS) as i:
                    e = experts_of(i)
                    for k in range(4):
                        layer1(i, k + 2, e[k + 2])
                        turn_h(i, k + 1)
                        layer2(i, k, e[k])
                        turn_x(i, k + 3)

            @block.scalar
            def _(act):
                regs = [act.alloc_register(f"{ph.name}_aexpert{u}") for u in range(8)]

                def copy_x(i, k):
                    act.wait_ge(x_turned, i * 4 + (k + 1))
                    act.sem_inc(act_on, 1)
                    act.wait_ge(up, i * 4 + (k + 1))
                    act.sem_inc(act_on, 1)
                    nc.scalar.copy(xT[:, k % 2, :, :], x_ps[k % 2][:, 0:2, :]).then_inc(x_copied, 1)

                def relu(i, k, e):
                    act.wait_ge(h_turned, i * 4 + (k + 3))
                    act.sem_inc(act_on, 1)
                    act.wait_ge(down, i * 4 + (k + 1))
                    act.sem_inc(act_on, 1)
                    for f in range(FT):
                        ins = nc.scalar.activation(hT[:, k % 2, f, :], hT_ps[k % 2][:, f, :], ACT.Relu, bias=bcol[:, bass.ds(e * FT + f, 1)])
                    ins.then_inc(relued, 1)

                def experts_of(i):
                    act.load(regs[0:4], expert_of[0:1, bass.ds(i * 4, 4)])
                    act.load(regs[4:8], expert_of[0:1, bass.ds(i * 4 + 4, 4)])
                    return [act.snap(r, min_val=0, max_val=N_EXP - 1) for r in regs]

                act.wait_ge(b_ready, 1)
                act.sem_inc(x_copied, 2)
                act.sem_inc(relued, 2)
                e = experts_of(0)
                for k in range(3):
                    copy_x(0, k)
                relu(0, 0, e[0])
                with act.Fori(0, TURNS) as i:
                    e = experts_of(i)
                    for k in range(4):
                        relu(i, k + 1, e[k + 1])
                        copy_x(i, k + 3)

            @block.vector
            def _(v):
                def copy_h(i, k):
                    v.wait_ge(up, i * 4 + (k + 3))
                    v.sem_inc(dve_on, 1)
                    v.wait_ge(h_turned, i * 4 + (k + 1))
                    v.sem_inc(dve_on, 1)
                    v.tensor_copy(h[:, k % 2, :], h_ps[k % 2][:]).then_inc(h_copied, 1)

                def turn(i, first):
                    for k in range(4):
                        copy_h(i, k + 2)
                        v.wait_ge(down, i * 4 + (k + 3))
                        v.sem_inc(dve_on, 1)
                        v.wait_ge(bias_in[k], i * 16 + 16)
                        v.sem_inc(dve_on, 1)
                        if not first:
                            v.wait_ge(y_out[k], i * 16)
                            v.sem_inc(dve_on, 1)
                        v.tensor_tensor(y[:, k, :], y_ps[k % 2][:, 0:D], B2[:, k, :], ALU.add).then_inc(y_ready, 1)

                v.wait_ge(b_turned, 1)
                v.tensor_copy(bcol[:], h_ps[0][:, 0:N_EXP * FT]).then_inc(b_ready, 1)
                v.sem_inc(h_copied, 2)
                v.sem_inc(y_ready, 2)
                for k in range(2):
                    copy_h(0, k)
                turn(0, True)
                with v.Fori(1, TURNS) as i:
                    turn(i, False)

            @block.gpsimd
            def _(g):
                scatter_edges(g, es, joined, at, payload, edges_out, edges_copied, pool_on)


def collect_rows(nc, y_slots, pos, weights, Y):
    with Phase(nc, "coll") as ph:
        ring = ph.sb("ring", [TN, 10, D])
        at = ph.sb("at", [TN, 5, 2], I32)
        at_ready, added, half, pool_on, dve_on = (ph.sem(k) for k in ("at", "added", "half", "pool_on", "dve_on"))
        got = [ph.sem(f"got{s}") for s in range(5)]
        with nc.Block() as block:
            @block.gpsimd
            def _(g):
                with g.Fori(0, 5) as i:
                    for s in range(5):
                        g.wait_ge(added, i * 5 + (s + 1))
                        g.sem_inc(pool_on, 1)
                        g.tensor_copy(at[:, s, :], pos[:, i * 5 + s, :]).then_inc(at_ready, 1)
                        g.wait_ge(at_ready, i * 5 + (s + 1))
                        g.sem_inc(pool_on, 1)
                        for k in range(2):
                            g.indirect_dma_start(out=ring[:, 2 * s + k, :], out_offset=None, in_=y_slots,
                                                 in_offset=bass.IndirectOffsetOnAxis(ap=at[:, s, k:k + 1], axis=0)).then_inc(got[s], 16)

            @block.vector
            def _(v):
                v.sem_inc(added, 5)
                with v.Fori(0, 5) as i:
                    for s in range(5):
                        t = i * 5 + s
                        v.wait_ge(got[s], i * 32 + 32)
                        v.sem_inc(dve_on, 1)
                        for k in range(2):
                            v.scalar_tensor_tensor(out=Y[:, t, :], in0=ring[:, 2 * s + k, :], scalar=weights[:, t, k:k + 1], in1=Y[:, t, :],
                                                   op0=ALU.mult, op1=ALU.add).then_inc(half if k == 0 else added, 1)
                            if k == 0:
                                v.wait_ge(half, i * 5 + (s + 1))
                                v.sem_inc(dve_on, 1)
                v.wait_ge(added, 30)


def table_rows(table):
    return table.rearrange("(t p) w -> p t w", p=TN)


def move(nc, name, pairs):
    with Phase(nc, name) as ph:
        moved = ph.sem("moved")
        with nc.Block() as block:
            @block.sync
            def _(sp):
                for to, of in pairs:
                    sp.dma_start(to, of).then_inc(moved, 16)
                sp.wait_ge(moved, 16 * len(pairs))


def vector_steps(nc, name, steps, loads=()):
    with Phase(nc, name) as ph:
        link_s, asked, answered, loaded = (ph.sem(k) for k in ("link", "asked", "answered", "loaded"))
        asks = []
        with nc.Block() as block:
            @block.sync
            def _(sp):
                for to, of in loads:
                    sp.dma_start(to, of).then_inc(loaded, 16)
                if loads:
                    sp.wait_ge(loaded, 16 * len(loads))

            @block.vector
            def _(v):
                if loads:
                    v.wait_ge(loaded, 16 * len(loads))

                def act_do(*a):
                    asks.append(a)
                    v.sem_inc(asked, 1)
                    v.wait_ge(answered, len(asks))
                steps(v, chain(v, link_s), act_do)

            @block.scalar
            def _(act):
                for n, (out, in_, func) in enumerate(asks):
                    act.wait_ge(asked, n + 1)
                    nc.scalar.activation(out, in_, func).then_inc(answered, 1)


def top2_gates(nc, name, cs, scores, n, gates=None, hots=None, weights=None):
    W = scores.shape[2]
    with Phase(nc, name + "_b") as ph:
        best = ph.sb("best", [TN, NT, 8])
        at_i = ph.sb("at_i", [TN, NT, 8], U32)
        at = ph.sb("at", [TN, NT, 8])
        diff, rest = (ph.sb(k, [TN, NT]) for k in ("diff", "rest"))
        hot = ph.sb("hot", [TN, NT, n])

        def steps(v, link, act_do):
            for t in range(NT):
                link(v.max(best[:, t, :], scores[:, t, :]))
                link(v.max_index(at_i[:, t, :], best[:, t, :], scores[:, t, :]))
            link(v.tensor_copy(at[:], at_i[:]))
            link(v.tensor_tensor(diff[:], best[:, :, 1], best[:, :, 0], ALU.subtract))
            act_do(diff[:], diff[:], ACT.Exp)
            link(v.tensor_scalar(rest[:], diff[:], 1.0, None, ALU.add))
            link(v.reciprocal(rest[:], rest[:]))
            link(v.tensor_tensor(diff[:], diff[:], rest[:], ALU.mult))
            number = cs.count_row[0:TN, 0:n].unsqueeze(1).to_broadcast([TN, NT, n])
            wide = lambda a: a.unsqueeze(2).to_broadcast([TN, NT, n])
            if hots is not None:
                for k, w in enumerate((rest, diff)):
                    link(v.tensor_tensor(hots[:, :, k, :], number, wide(at[:, :, k]), ALU.is_equal))
                    link(v.tensor_copy(weights[:, :, k], w[:]))
                return
            link(v.tensor_tensor(hot[:], number, wide(at[:, :, 0]), ALU.is_equal))
            link(v.tensor_tensor(gates[:], hot[:], wide(rest[:]), ALU.mult))
            link(v.tensor_tensor(hot[:], number, wide(at[:, :, 1]), ALU.is_equal))
            link(v.tensor_tensor(hot[:], hot[:], wide(diff[:]), ALU.mult))
            link(v.tensor_tensor(gates[:], gates[:], hot[:], ALU.add))
        vector_steps(nc, name, steps)


def take_sums(nc, name, acc, rows, dinv, width):
    def steps(v, link, act_do):
        link(v.tensor_tensor(rows[:], acc[:, 0:NT * width].rearrange("p (t w) -> p t w", w=width), rows[:], ALU.add))
        link(v.tensor_tensor(rows[:], rows[:], dinv[:].unsqueeze(2).to_broadcast([TN, NT, width]), ALU.mult))
    vector_steps(nc, name, steps)


def batch_norm(nc, name, cs, rows, bias, gamma, beta, width, XT):
    with Phase(nc, name) as ph:
        cols = ph.sb("cols", [width, 3])
        parts = ph.sb("parts", [width, 7, 6])
        ms = ph.sb("ms", [width, 2])
        scale, move_ = ph.sb("scale", [width, 1]), ph.sb("shift", [width, 1])
        tp = [ph.psum(f"tp{k}", [width, TN]) for k in range(4)]
        loaded, turned, copied, link_s, asked, answered, relu = (
            ph.sem(k) for k in ("loaded", "turned", "copied", "link", "asked", "answered", "relu"))
        with nc.Block() as block:
            @block.sync
            def _(sp):
                for k, a in enumerate((bias, gamma, beta)):
                    sp.dma_start(cols[:, k:k + 1], a.rearrange("(p a) -> p a", a=1)).then_inc(loaded, 16)
                sp.wait_ge(loaded, 48)

            @block.vector
            def _(v):
                v.wait_ge(loaded, 48)
                v.wait_ge(copied, NT)
                link = chain(v, link_s)
                for k in range(7):
                    lo, hi = k * 500, min(N, k * 500 + 500)
                    link(v.bn_stats(out=parts[:, k, :], in_=XT[:, lo:hi]))
                link(v.bn_aggr(out=ms[:], in_=parts[:].rearrange("p k s -> p (k s)")))
                link(v.tensor_scalar(ms[:, 1:2], ms[:, 1:2], EPS, None, ALU.add))
                v.sem_inc(asked, 1)
                v.wait_ge(answered, 1)
                link(v.reciprocal(scale[:], ms[:, 1:2]))
                link(v.tensor_tensor(scale[:], scale[:], cols[:, 1:2], ALU.mult))
                link(v.scalar_tensor_tensor(out=move_[:], in0=scale[:], scalar=ms[:, 0:1], in1=cols[:, 2:3], op0=ALU.mult, op1=ALU.subtract))
                link(v.tensor_scalar(move_[:], move_[:], -1.0, None, ALU.mult))
                v.sem_inc(asked, 1)

            @block.tensor
            def _(pe):
                for t in range(NT):
                    if t >= 4:
                        pe.wait_ge(copied, t - 3)
                    pe.transpose(tp[t % 4][:], rows[:, t, :], cs.ident[0:TN, 0:TN]).then_inc(turned, 1)

            @block.scalar
            def _(act):
                act.wait_ge(loaded, 48)
                for t in range(NT):
                    act.wait_ge(turned, t + 1)
                    nc.scalar.activation(XT[:, t * TN:(t + 1) * TN], tp[t % 4][:], ACT.Identity, bias=cols[:, 0:1]).then_inc(copied, 1)
                act.wait_ge(asked, 1)
                nc.scalar.activation(ms[:, 1:2], ms[:, 1:2], ACT.Sqrt).then_inc(answered, 1)
                act.wait_ge(asked, 2)
                nc.scalar.activation(XT[:], XT[:], ACT.Relu, scale=scale[:], bias=move_[:]).then_inc(relu, 1)
                act.wait_ge(relu, 1)


def from_features(nc, name, groups, cols, finish, loads):
    with Phase(nc, name) as ph:
        ps = [ph.psum(f"ps{k}", [TN, 512]) for k in range(4)]
        loaded, summed, finished, link_s = (ph.sem(k) for k in ("loaded", "summed", "finished", "link"))
        with nc.Block() as block:
            @block.sync
            def _(sp):
                for to, of in loads:
                    sp.dma_start(to, of).then_inc(loaded, 16)
                sp.wait_ge(loaded, 16 * len(loads))

            @block.tensor
            def _(pe):
                pe.wait_ge(loaded, 16 * len(loads))
                for t in range(NT):
                    if t >= 4:
                        pe.wait_ge(finished, t - 3)
                    for k, (XT, W) in enumerate(groups):
                        ins = pe.matmul(ps[t % 4][:, 0:cols], XT[:, t * TN:(t + 1) * TN], W, start=(k == 0), stop=(k == len(groups) - 1))
                    ins.then_inc(summed, 1)

            @block.vector
            def _(v):
                v.wait_ge(loaded, 16 * len(loads))
                link = chain(v, link_s)
                for t in range(NT):
                    v.wait_ge(summed, t + 1)
                    finish(v, link, t, ps[t % 4][:, 0:cols]).then_inc(finished, 1)
                v.wait_ge(finished, NT)


def gat_scores(nc, cs, table, AD, GT, S):
    C = GH * GE + GH
    with Phase(nc, "gscore") as ph:
        ring = ph.sb("ring", [P, TURN, C])
        idx = ph.sb("idx", [P, RING, PB], I32)
        Lb = ph.sb("Lb", [TN, RING, PB * P])
        hotT = ph.sb("hotT", [TN, RING, PB * P])
        dist = ph.sb("dist", [TN, RING, PB * P])
        ad = [ph.psum(f"ad{q}", [P, PB, GH]) for q in range(RING)]
        idx_ready, hot_ready, ad_ready, taken, dist_ready, pool_on, sp_on, act_on, pe_on, dve_on, leaked = (
            ph.sem(k) for k in ("idx", "hot", "ad", "taken", "dist", "pool_on", "sp_on", "act_on", "pe_on", "dve_on", "leaked"))
        got = [ph.sem(f"got{q}") for q in range(RING)]
        lb_got = [ph.sem(f"lb{q}") for q in range(RING)]
        with nc.Block() as block:
            @block.gpsimd
            def _(g):
                gather_pairs(g, cs, table, ring, idx, idx_ready, taken, got, pool_on)

            @block.sync
            def _(sp):
                with sp.Fori(0, cs.loops) as i:
                    for q in range(RING):
                        load_local_rows(sp, cs, Lb, lb_got, hot_ready, sp_on, i, q)

            @block.scalar
            def _(act):
                act.sem_inc(hot_ready, RING)
                with act.Fori(0, cs.loops) as i:
                    for q in range(RING):
                        act.wait_ge(ad_ready, i * RING + (q + 1))
                        act.sem_inc(act_on, 1)
                        node_hots(nc, act, cs, Lb, hotT, dist, lb_got, hot_ready, (dist_ready, act_on), i, q)

            @block.tensor
            def _(pe):
                pe.sem_inc(ad_ready, RING)
                regs = [pe.alloc_register(f"{ph.name}_tile{u}") for u in range(PB)]
                with pe.Fori(0, cs.loops) as i:
                    for q in range(RING):
                        pe.wait_ge(hot_ready, i * RING + (RING + q + 1))
                        pe.sem_inc(pe_on, 1)
                        pe.wait_ge(taken, i * RING + (q + 1))
                        pe.sem_inc(pe_on, 1)
                        tiles = load_tiles(pe, regs, cs, i, q)
                        for u in range(PB):
                            tile = tiles[u]
                            ins = pe.matmul(ad[q][:, u, :], hotT[:, q, u * P:(u + 1) * P], AD[:, tile, :], start=True, stop=True)
                        ins.then_inc(ad_ready, 1)

            @block.vector
            def _(v):
                v.sem_inc(taken, RING)
                with v.Fori(0, cs.loops) as i:
                    for q in range(RING):
                        v.wait_ge(got[q], i * (16 * PB) + 16 * PB)
                        v.sem_inc(dve_on, 1)
                        batch = bass.ds(i * (TURN) + q * PB, PB)
                        part = ring[:, q * PB:(q + 1) * PB, :]
                        v.tensor_copy(GT[:, batch, :], part)
                        v.wait_ge(ad_ready, i * RING + (RING + q + 1))
                        v.sem_inc(dve_on, 1)
                        v.tensor_tensor(S[:, batch, :], ad[q][:], part[:, :, GH * GE:C], ALU.add).then_inc(taken, 1)
                v.wait_ge(taken, cs.loops * RING + RING)
                v.scalar_tensor_tensor(out=S[:], in0=S[:], scalar=0.2, in1=S[:], op0=ALU.mult, op1=ALU.max).then_inc(leaked, 1)
                v.wait_ge(leaked, 1)


def gat_sums(nc, cs, RW, acc):
    C = RW.shape[2]
    with Phase(nc, "gsum") as ph:
        hot = ph.sb("hot", [P, RING, PB, TN])
        zero = ph.sb("zero", [1, 512])
        hot_ready, summed, zeroed, pe_on, dve_on = (ph.sem(k) for k in ("hot", "summed", "zeroed", "pe_on", "dve_on"))
        with nc.Block() as block:
            @block.vector
            def _(v):
                v.memset(zero[:], 0.0).then_inc(zeroed, 1)
                with v.Fori(0, cs.loops) as i:
                    for q in range(RING):
                        v.wait_ge(summed, i * RING + (q + 1))
                        v.sem_inc(dve_on, 1)
                        own = cs.local[:, bass.ds(i * (TURN) + q * PB, PB)]
                        v.tensor_tensor(hot[:, q, :, :], cs.count_row[:, 0:TN].unsqueeze(1).to_broadcast([P, PB, TN]),
                                        own.unsqueeze(2).to_broadcast([P, PB, TN]), ALU.is_equal).then_inc(hot_ready, 1)

            @block.tensor
            def _(pe):
                pe.wait_ge(zeroed, 1)
                for b in range(2):
                    pe.matmul(acc[:, b * 512:(b + 1) * 512], zero[:, 0:TN], zero[:], start=True, stop=True)
                pe.sem_inc(summed, RING)
                regs = [pe.alloc_register(f"{ph.name}_tile{u}") for u in range(PB)]
                with pe.Fori(0, cs.loops) as i:
                    for q in range(RING):
                        pe.wait_ge(hot_ready, i * RING + (q + 1))
                        pe.sem_inc(pe_on, 1)
                        tiles = load_tiles(pe, regs, cs, i, q)
                        for u in range(PB):
                            p = i * (TURN) + (q * PB + u)
                            tile = tiles[u]
                            ins = pe.matmul(acc[:, bass.ds(tile * 32, C)], hot[:, q, u, :], RW[:, p, :],
                                            start=False, stop=True, skip_group_check=True)
                        ins.then_inc(summed, 1)
                pe.wait_ge(summed, cs.loops * RING + RING)


def build(nc, a, out):
    with ExitStack() as ctx:
        def sb(name, shape, dt=F32, c=ctx):
            return c.enter_context(nc.sbuf_tensor(name, shape, dt))

        def dram(name, shape):
            return nc.dram_tensor(name, shape, F32)

        cs = Consts(sb)
        g1 = Graph("g1", sb, dram, cs, E1)
        g2 = Graph("g2", sb, dram, cs, E2)
        sorted_edges = nc.dram_tensor("sorted_edges", [E2, 2], I32).ap()
        q_dram, v_dram, h1_dram, h2_dram, g_dram = (dram(k, [N, w]).ap() for k, w in (
            ("q_rows", D), ("v_rows", D), ("h1_rows", 128), ("h2_rows", 64), ("g_rows", GH * GE + GH)))
        carries = {h: (dram(f"side{h}", [4 * pairs * h // P, P]).ap(), dram(f"cin{h}", [2 * pairs * h // P, P]).ap())
                   for h, pairs in ((H, g1.pairs), (GH, g2.pairs))}

        X = sb("X", [TN, NT, D])
        rstd, shift = sb("rstd", [TN, NT]), sb("shift", [TN, NT])
        dinv = sb("dinv", [TN, NT])
        sort_pay, sort_pos = sb("sort_pay", [P, E2 // P, 2], I32), sb("sort_pos", [P, E2 // P], I32)
        x_slots, y_slots = (dram(k, [tiles * P, D]).ap() for k, tiles in (("x_slots", X_TILES), ("y_slots", SLOT_TILES)))
        rows_dram = dram("u_rows", [N, D]).ap()
        slots_filled, up_in, down_in = (nc.alloc_semaphore(k) for k in ("slots_filled", "up_in", "down_in"))

        constants(nc, cs)
        with ExitStack() as start:
            zeros = sb("zeros", [P, D], c=start)

            def no_rows(v, link, act_do):
                link(v.memset(zeros[:], 0.0))
            vector_steps(nc, "zero", no_rows)
            start_loads(nc, [(x_slots.rearrange("(t p) d -> p t d", p=P), zeros[:].unsqueeze(1).to_broadcast([P, X_TILES, D]))],
                        slots_filled)
            index_tables(nc, g1, a["src"], a["dst"])
            with nc.Block() as block:
                @block.sync
                def _(sp):
                    sp.wait_ge(slots_filled, 16)
        move(nc, "in", [(X[:], table_rows(a["x"]))])

        with ExitStack() as l1:
            T = sb("T", [TN, NT, D], c=l1)
            with ExitStack() as att:
                S = sb("S", [P, g1.pairs, H], c=att)
                es = EdgeSort(lambda *k: sb(*k, c=att), E2, sort_pay, sort_pos)
                histogram(nc, cs, a["L1_ffn_edge_index"], es)
                row_stats(nc, "st0", X, rstd, shift)
                normalise(nc, "nm0", X, rstd, shift, T)
                row_stats(nc, "st1", T, rstd, shift)
                with ExitStack() as kq:
                    K = sb("K", [TN, NT, D], c=kq)
                    with ExitStack() as qv:
                        Q, V = sb("Q", [TN, NT, D], c=qv), sb("V", [TN, NT, D], c=qv)
                        BQ = sb("BQ", [TN, 3 * D], c=qv)
                        SCALE = D ** -0.5

                        def scale_bq(v, link, act_do):
                            link(v.tensor_scalar(BQ[:, 0:D], BQ[:, 0:D], SCALE, None, ALU.mult))
                        vector_steps(nc, "bq", scale_bq, [(BQ[:], a["L0_gnn_bqkv"].partition_broadcast(TN))])

                        def finish(v, j, tile, s, ps):
                            if j == 0:
                                v.scalar_tensor_tensor(out=Q[:, tile, :], in0=ps[:, 0:D], scalar=SCALE, in1=BQ[:, 0:D], op0=ALU.mult, op1=ALU.add)
                                return v.tensor_tensor(K[:, tile, :], ps[:, D:2 * D], BQ[:, D:2 * D], ALU.add)
                            return v.tensor_tensor(V[:, tile, :], ps, BQ[:, 2 * D:3 * D], ALU.add)
                        project(nc, "qkv", cs, T, rstd, shift, a["L0_gnn_Wqkv"], [(0, 512), (512, 256)], finish,
                                affine=(a["L0_gnn_ln_attn_g"], a["L0_gnn_ln_attn_b"]))
                        move(nc, "qv", [(table_rows(q_dram), Q[:]), (table_rows(v_dram), V[:])])
                    edge_scores(nc, g1, q_dram, K, S, es, a["L1_ffn_edge_index"])
                with ExitStack() as mw:
                    M = sb("M", [P, g1.pairs, H], c=mw)
                    segment_max(nc, g1, "max8", S, H, M, carries[H])
                    Wt = sb("Wt", [P, g1.pairs, H + 1], c=mw)
                    edge_weights(nc, "w8", S, M, Wt[:, :, 0:H])

                    def one_column(v, link, act_do):
                        link(v.memset(Wt[:, :, H], 1.0))
                    vector_steps(nc, "one", one_column)
                    acc = sb("acc", [TN, NT, D + H + 1], c=mw)
                    weigh_values(nc, g1, v_dram, Wt, acc)

                    def combine(v, link, act_do):
                        w = acc[:, :, D:D + H]
                        link(v.tensor_scalar(w, w, 0.5, None, ALU.max))
                        link(v.reciprocal(w, w))
                        val = acc[:, :, 0:D].rearrange("p t (h d) -> p t h d", h=H)
                        link(v.tensor_tensor(val, val, w.unsqueeze(3).to_broadcast([TN, NT, H, D // H]), ALU.mult))
                        link(v.tensor_tensor(T[:], T[:], acc[:, :, 0:D], ALU.add))
                        link(v.tensor_scalar(dinv[:], acc[:, :, D + H], 1.0, None, ALU.add))
                        act_do(dinv[:], dinv[:], ACT.Sqrt)
                        link(v.reciprocal(dinv[:], dinv[:]))
                    vector_steps(nc, "comb", combine)
            with ExitStack() as ff:
                UT = sb("UT0", [P, 2, N], c=ff)
                bo = sb("bo", [TN, D], c=ff)
                gate1 = sb("gate1", [TN, NT, 2], c=ff)
                row_stats(nc, "st2", T, rstd, shift)
                project(nc, "ln2", cs, T, rstd, shift, None, [], None,
                        affine=(a["L0_gnn_ln_res_g"], a["L0_gnn_ln_res_b"]), UT=UT)

                def start(v, link, act_do):
                    link(v.memset(gate1[:], 1.0))
                    link(v.tensor_tensor(X[:], X[:], T[:], ALU.add))
                    link(v.tensor_tensor(X[:], X[:], bo[:].unsqueeze(1).to_broadcast([TN, NT, D]), ALU.add))
                vector_steps(nc, "y0", start, [(bo[:], a["L0_gnn_b_out"].partition_broadcast(TN))])
                w_in = a["L0_gnn_W_in"].rearrange("d (e f) -> e d f", e=2)
                experts(nc, "ff0", cs, UT, X, gate1, w_in, a["L0_gnn_b_in"].rearrange("(e f) -> e f", e=2),
                        a["L0_gnn_W_out"].rearrange("(e f) d -> e f d", e=2), None, 2, ACT.Gelu)
        with ExitStack() as moe:
            logits = sb("logits", [TN, NT, N_EXP], c=moe)
            hots, weights = sb("hots", [TN, NT, 2, N_EXP], c=moe), sb("weights", [TN, NT, 2], c=moe)
            pos, expert_of = sb("pos", [TN, NT, 2], I32, c=moe), sb("expert_of", [1, OWNERS], I32, c=moe)
            gb = sb("gb", [TN, 3 * D], c=moe)
            with ExitStack() as big:
                UP = sb("UP", [P, N_EXP, 2, F_EXP], c=big)
                start_loads(nc, [(UP[:], a["L0_ffn_w1"].rearrange("e (c p) f -> p e c f", p=P))], up_in)
                row_stats(nc, "st3", X, rstd, shift)
                move(nc, "gb", [(gb[:, 0:N_EXP], a["L0_ffn_gate_b"].partition_broadcast(TN)),
                                (gb[:, D:2 * D], a["L0_ffn_gamma"].partition_broadcast(TN)),
                                (gb[:, 2 * D:3 * D], a["L0_ffn_beta"].partition_broadcast(TN))])
                with ExitStack() as norm:
                    U = sb("U1", [TN, NT, D], c=norm)
                    project(nc, "gate", cs, X, rstd, shift, a["L0_ffn_gate_w"], [(0, N_EXP)],
                            lambda v, j, tile, s, ps: v.tensor_tensor(logits[:, tile, :], ps, gb[:, 0:N_EXP], ALU.add),
                            rows_out=U)
                    move(nc, "rows", [(table_rows(rows_dram), U[:])])
                DOWN = sb("DOWN", [P, N_EXP, F_EXP // P, D], c=big)
                start_loads(nc, [(DOWN[:], a["L0_ffn_w2"].rearrange("e (f p) d -> p e f d", p=P))], down_in)
                top2_gates(nc, "top16", cs, logits, N_EXP, hots=hots, weights=weights)
                route(nc, cs, hots, pos, expert_of)
                send_rows(nc, rows_dram, pos, x_slots)
                slot_experts(nc, cs, x_slots, y_slots, UP, DOWN, a["L0_ffn_b1"], a["L0_ffn_b2"], expert_of,
                             up_in, down_in, es, sorted_edges)
            Y = sb("Y1", [TN, NT, D], c=moe)
            move(nc, "back", [(Y[:], table_rows(rows_dram))])
            collect_rows(nc, y_slots, pos, weights, Y)
            row_stats(nc, "st4", Y, rstd, shift)
            normalise(nc, "nm4", Y, rstd, shift, Y)

            def add_moe(v, link, act_do):
                wide = lambda k: gb[:, k * D:(k + 1) * D].unsqueeze(1).to_broadcast([TN, NT, D])
                link(v.tensor_tensor(Y[:], Y[:], wide(1), ALU.mult))
                link(v.tensor_tensor(Y[:], Y[:], wide(2), ALU.add))
                link(v.tensor_tensor(X[:], X[:], Y[:], ALU.add))
            vector_steps(nc, "addm", add_moe)
        index_tables(nc, g2, joined=sorted_edges)
        with ExitStack() as gcn:
            UT = sb("UT2", [P, 2, N], c=gcn)
            H1 = sb("H1", [TN, NT, 128], c=gcn)
            H2 = sb("H2", [TN, NT, 64], c=gcn)
            XT1 = sb("XT1", [128, N], c=gcn)
            XT2 = sb("XT2", [64, N], c=gcn)
            W2, Wfc, Wfc2 = sb("gW2", [128, 64], c=gcn), sb("Wfc", [P, 3, D], c=gcn), sb("Wfc2", [64, D], c=gcn)
            bfc = sb("bfc", [TN, D], c=gcn)
            relu = sb("relu", [TN, 4, D], c=gcn)
            row_stats(nc, "st5", X, rstd, shift)
            project(nc, "gc1", cs, X, rstd, shift, a["L1_gnn_W1"], [(0, 128)],
                    lambda v, j, tile, s, ps: v.tensor_scalar(H1[:, tile, :], ps, dinv[:, bass.ds(tile, 1)], None, ALU.mult),
                    UT=UT)
            move(nc, "h1", [(table_rows(h1_dram), H1[:])])
            with nc.psum_tensor("acc1", [TN, 7 * 512], F32) as acc1:
                neighbour_sums(nc, "sum1", g1, h1_dram, 128, acc1)
                take_sums(nc, "take1", acc1, H1, dinv, 128)
            batch_norm(nc, "bn1", cs, H1, a["L1_gnn_b1"], a["L1_gnn_g1"], a["L1_gnn_be1"], 128, XT1)
            from_features(nc, "gc2", [(XT1, W2[:])], 64,
                          lambda v, link, t, ps: v.tensor_scalar(H2[:, t, :], ps, dinv[:, t:t + 1], None, ALU.mult),
                          [(W2[:], a["L1_gnn_W2"])])
            move(nc, "h2", [(table_rows(h2_dram), H2[:])])
            with nc.psum_tensor("acc2", [TN, 4 * 512], F32) as acc2:
                neighbour_sums(nc, "sum2", g1, h2_dram, 64, acc2)
                take_sums(nc, "take2", acc2, H2, dinv, 64)
            batch_norm(nc, "bn2", cs, H2, a["L1_gnn_b2"], a["L1_gnn_g2"], a["L1_gnn_be2"], 64, XT2)

            def add_fc(v, link, t, ps):
                r = relu[:, t % 4, :]
                link(v.tensor_tensor(r, ps, bfc[:], ALU.add))
                return v.scalar_tensor_tensor(out=X[:, t, :], in0=r, scalar=0.0, in1=X[:, t, :], op0=ALU.max, op1=ALU.add)
            from_features(nc, "fc", [(UT[:, 0, :], Wfc[:, 0, :]), (UT[:, 1, :], Wfc[:, 1, :]), (XT1, Wfc[:, 2, :]), (XT2, Wfc2[:])],
                          D, add_fc, [(Wfc[:], a["L1_gnn_Wfc"][0:384, :].rearrange("(k p) n -> p k n", p=P)),
                                      (Wfc2[:], a["L1_gnn_Wfc"][384:448, :]),
                                      (bfc[:], a["L1_gnn_bfc"].partition_broadcast(TN))])
        with ExitStack() as gat:
            UT = sb("UT3", [P, 2, N], c=gat)
            gates = sb("gates4", [TN, NT, 4], c=gat)
            HG = sb("HG", [TN, NT, 20], c=gat)
            AD = sb("AD", [TN, NT, 4], c=gat)
            tmp = sb("tmpg", [TN, NT, 16], c=gat)
            vec = sb("vecg", [TN, 5, 16], c=gat)
            row_stats(nc, "st6", X, rstd, shift)
            project(nc, "gat", cs, X, rstd, shift, a["L1_ffn_W_gat"], [(0, 16)],
                    lambda v, j, tile, s, ps: v.tensor_copy(HG[:, tile, 0:16], ps), UT=UT)
            wide16 = lambda k: vec[:, k, :].unsqueeze(1).to_broadcast([TN, NT, 16])

            def attend(v, link, act_do):
                for k, dest in ((0, HG[:, :, 16:20]), (1, AD[:])):
                    link(v.tensor_tensor(tmp[:], HG[:, :, 0:16], wide16(k), ALU.mult))
                    link(v.tensor_reduce(dest, tmp[:].rearrange("p t (h e) -> p t h e", h=GH), AX.X, ALU.add))
            vector_steps(nc, "att", attend, [(vec[:, k, :], v.partition_broadcast(TN)) for k, v in enumerate(
                (a["L1_ffn_att_src"].rearrange("h e -> (h e)"), a["L1_ffn_att_dst"].rearrange("h e -> (h e)"),
                 a["L1_ffn_b_gat"], a["L1_ffn_ln_gamma"], a["L1_ffn_ln_beta"]))])
            move(nc, "g", [(table_rows(g_dram), HG[:])])
            accs = sb("accs", [TN, NT, 25], c=gat)
            with ExitStack() as edges:
                S = sb("Sg", [P, g2.pairs, GH], c=edges)
                M = sb("Mg", [P, g2.pairs, GH], c=edges)
                RW = sb("RW", [P, g2.pairs, 25], c=edges)
                with ExitStack() as gt:
                    GT = sb("GT", [P, g2.pairs, 20], c=gt)
                    gat_scores(nc, g2, g_dram, AD, GT, S)
                    segment_max(nc, g2, "max4", S, GH, M, carries[GH])
                    edge_weights(nc, "w4", S, M, RW[:, :, 16:20])

                    def rows25(v, link, act_do):
                        w = RW[:, :, 16:20].unsqueeze(3).to_broadcast([P, g2.pairs, GH, GE])
                        link(v.tensor_tensor(RW[:, :, 0:16].rearrange("p t (h e) -> p t h e", h=GH),
                                             GT[:, :, 0:16].rearrange("p t (h e) -> p t h e", h=GH), w, ALU.mult))
                        link(v.tensor_tensor(RW[:, :, 20:24], M[:], g2.last_of[:].unsqueeze(2).to_broadcast([P, g2.pairs, GH]), ALU.mult))
                        link(v.tensor_copy(RW[:, :, 24], g2.last_of[:]))
                    vector_steps(nc, "rw", rows25)
                with nc.psum_tensor("acc3", [TN, 1024], F32) as acc3:
                    gat_sums(nc, g2, RW, acc3)

                    def keep(v, link, act_do):
                        link(v.tensor_copy(accs[:], acc3[:, 0:800].rearrange("p (t c) -> p t c", c=32)[:, :, 0:25]))
                    vector_steps(nc, "keep", keep)
            with ExitStack() as node:
                m1, own, m = (sb(k, [TN, NT, GH], c=node) for k in ("m1", "own", "mx"))
                agg, sq = sb("agg", [TN, NT, 16], c=node), sb("sq", [TN, NT, 16], c=node)
                mean, var = sb("mean", [TN, NT], c=node), sb("var", [TN, NT], c=node)
                sc8 = sb("sc8", [TN, NT, 8], c=node)

                def finish_gat(v, link, act_do):
                    four = lambda x: x.unsqueeze(3).to_broadcast([TN, NT, GH, GE])
                    heads = lambda x: x.rearrange("p t (h e) -> p t h e", h=GH)
                    link(v.tensor_scalar(mean[:], accs[:, :, 24], -1.0, BIG, ALU.add, ALU.mult))
                    link(v.tensor_tensor(m1[:], accs[:, :, 20:24], mean[:].unsqueeze(2).to_broadcast([TN, NT, GH]), ALU.add))
                    link(v.tensor_tensor(own[:], HG[:, :, 16:20], AD[:], ALU.add))
                    link(v.scalar_tensor_tensor(out=own[:], in0=own[:], scalar=0.2, in1=own[:], op0=ALU.mult, op1=ALU.max))
                    link(v.tensor_tensor(m[:], m1[:], own[:], ALU.max))
                    link(v.tensor_tensor(m1[:], m1[:], m[:], ALU.subtract))
                    link(v.tensor_tensor(own[:], own[:], m[:], ALU.subtract))
                    act_do(m1[:], m1[:], ACT.Exp)
                    act_do(own[:], own[:], ACT.Exp)
                    link(v.tensor_tensor(m[:], accs[:, :, 16:20], m1[:], ALU.mult))
                    link(v.tensor_tensor(m[:], m[:], own[:], ALU.add))
                    link(v.tensor_scalar(m[:], m[:], 1e-16, None, ALU.add))
                    link(v.reciprocal(m[:], m[:]))
                    link(v.tensor_tensor(heads(agg[:]), heads(accs[:, :, 0:16]), four(m1[:]), ALU.mult))
                    link(v.tensor_tensor(heads(sq[:]), heads(HG[:, :, 0:16]), four(own[:]), ALU.mult))
                    link(v.tensor_tensor(agg[:], agg[:], sq[:], ALU.add))
                    link(v.tensor_tensor(heads(agg[:]), heads(agg[:]), four(m[:]), ALU.mult))
                    link(v.tensor_tensor(agg[:], agg[:], wide16(2), ALU.add))
                    w16 = lambda x: x.unsqueeze(2).to_broadcast([TN, NT, 16])
                    link(v.tensor_reduce(mean[:], agg[:], AX.X, ALU.add))
                    link(v.tensor_scalar(mean[:], mean[:], 1.0 / 16, None, ALU.mult))
                    link(v.tensor_tensor(agg[:], agg[:], w16(mean[:]), ALU.subtract))
                    link(v.tensor_tensor(sq[:], agg[:], agg[:], ALU.mult))
                    link(v.tensor_reduce(var[:], sq[:], AX.X, ALU.add))
                    link(v.tensor_scalar(var[:], var[:], 1.0 / 16, EPS, ALU.mult, ALU.add))
                    act_do(var[:], var[:], ACT.Sqrt)
                    link(v.reciprocal(var[:], var[:]))
                    link(v.tensor_tensor(agg[:], agg[:], w16(var[:]), ALU.mult))
                    link(v.tensor_tensor(agg[:], agg[:], wide16(3), ALU.mult))
                    link(v.tensor_tensor(agg[:], agg[:], wide16(4), ALU.add))
                    link(v.memset(sc8[:], -BIG))
                    link(v.tensor_reduce(sc8[:, :, 0:4], agg[:].rearrange("p t (h e) -> p t e h", h=GH), AX.X, ALU.add))
                    link(v.tensor_scalar(sc8[:, :, 0:4], sc8[:, :, 0:4], 0.25, None, ALU.mult))
                vector_steps(nc, "fin", finish_gat)
                top2_gates(nc, "top4", cs, sc8, 4, gates)
            experts(nc, "ff1", cs, UT, X, gates, a["L1_ffn_W1"], a["L1_ffn_b1"], a["L1_ffn_W2"], a["L1_ffn_b2"], 4, ACT.Gelu)
        move(nc, "out", [(table_rows(out), X[:])])


NAMES = ['x', 'src', 'dst', 'L0_gnn_Wqkv', 'L0_gnn_bqkv', 'L0_gnn_ln_attn_g', 'L0_gnn_ln_attn_b', 'L0_gnn_ln_res_g',
         'L0_gnn_ln_res_b', 'L0_gnn_W_in', 'L0_gnn_b_in', 'L0_gnn_W_out', 'L0_gnn_b_out', 'L0_ffn_gate_w', 'L0_ffn_gate_b',
         'L0_ffn_w1', 'L0_ffn_b1', 'L0_ffn_w2', 'L0_ffn_b2', 'L0_ffn_gamma', 'L0_ffn_beta', 'L1_gnn_W1', 'L1_gnn_b1',
         'L1_gnn_g1', 'L1_gnn_be1', 'L1_gnn_W2', 'L1_gnn_b2', 'L1_gnn_g2', 'L1_gnn_be2', 'L1_gnn_Wfc', 'L1_gnn_bfc',
         'L1_ffn_W_gat', 'L1_ffn_att_src', 'L1_ffn_att_dst', 'L1_ffn_b_gat', 'L1_ffn_ln_gamma', 'L1_ffn_ln_beta',
         'L1_ffn_W1', 'L1_ffn_b1', 'L1_ffn_W2', 'L1_ffn_b2',
         'L1_ffn_edge_index']


def kernel(**inputs):
    import concourse.bacc as bacc
    from concourse.bass_utils import run_bass_kernel_spmd

    nc = bacc.Bacc("TRN2", target_bir_lowering=False, num_devices=1)
    arrays, aps = {}, {}
    for name in NAMES:
        arrays[f"in_{name}"] = np.ascontiguousarray(inputs[name])
        aps[name] = nc.dram_tensor(f"in_{name}", arrays[f"in_{name}"].shape, mybir.dt.from_np(arrays[f"in_{name}"].dtype),
                                   kind="ExternalInput").ap()
    out = nc.dram_tensor("out_x", (N, D), F32, kind="ExternalOutput").ap()
    build(nc, aps, out)
    got = run_bass_kernel_spmd(nc, [arrays], core_ids=[0])
    return got.results[0]["out_x"]
```

```python
from contextlib import ExitStack

import numpy as np
import concourse.bass as bass
from concourse import mybir

F32 = mybir.dt.float32
BF16 = mybir.dt.bfloat16
I32 = mybir.dt.int32
U32 = mybir.dt.uint32
ALU = mybir.AluOpType
ACT = mybir.ActivationFunctionType
AX = mybir.AxisListType

P = 128
N, D = 3125, 256
TN, NT = 125, 25
E1, E2 = 50000, 32768
PB, RING = 4, 4
TURN = PB * RING
H = 8
GH, GE = 4, 4
BIG = 1e30
NO_DST, NO_KEY = 8191.0, -7.0
EPS = 1e-5


class Phase:

    def __init__(self, nc, name):
        self.nc, self.name = nc, name

    def __enter__(self):
        self.ctx, self.sems = ExitStack(), []
        return self

    def sb(self, name, shape, dt=F32):
        return self.ctx.enter_context(self.nc.sbuf_tensor(f"{self.name}_{name}", shape, dt))

    def psum(self, name, shape, dt=F32):
        return self.ctx.enter_context(self.nc.psum_tensor(f"{self.name}_{name}", shape, dt))

    def sem(self, name):
        s = self.nc.alloc_semaphore(f"{self.name}_{name}")
        self.sems.append(s)
        return s

    def __exit__(self, kind, value, trace):
        self.ctx.close()
        if kind is None:
            self.nc.clear_and_free_semaphores(self.sems)
            self.nc.all_engine_barrier()


def chain(eng, sem, base=0):
    n = [0]

    def link(ins, early=False):
        n[0] += 1
        ins.then_inc(sem, 1)
        if not (early and n[0] == 1):
            eng.wait_ge(sem, base + n[0] - int(early))
    return link


def row_stats(nc, name, X, rstd, shift, parts, taken_before=False, source=None):
    with Phase(nc, name) as ph:
        a, b, c = (ph.sb(k, [TN, NT]) for k in "abc")
        taken, link_s, var_ready, root_ready, normed = (ph.sem(k) for k in ("taken", "link", "var", "root", "normed"))
        with nc.Block() as block:
            @block.vector
            def _(v):
                if not taken_before:
                    for t in range(NT):
                        if source is not None:
                            v.wait_ge(normed, t + 1)
                        v.bn_stats(out=parts[:, t, :], in_=X[:, t, :]).then_inc(taken, 1)
                    v.wait_ge(taken, NT)
                link = chain(v, link_s)
                link(v.tensor_tensor(a[:], parts[:, :, 1], parts[:, :, 4], ALU.add))
                link(v.tensor_tensor(b[:], parts[:, :, 1], parts[:, :, 4], ALU.subtract))
                link(v.tensor_tensor(c[:], parts[:, :, 2], parts[:, :, 5], ALU.add))
                link(v.tensor_tensor(b[:], b[:], b[:], ALU.mult))
                link(v.scalar_tensor_tensor(out=b[:], in0=b[:], scalar=D / 4.0, in1=c[:], op0=ALU.mult, op1=ALU.add))
                v.tensor_scalar(c[:], b[:], 1.0 / D, EPS, ALU.mult, ALU.add).then_inc(var_ready, 1)
                v.wait_ge(root_ready, 1)
                link(v.reciprocal(rstd[:], b[:]))
                link(v.scalar_tensor_tensor(out=shift[:], in0=a[:], scalar=-0.5, in1=rstd[:], op0=ALU.mult, op1=ALU.mult))

            @block.scalar
            def _(act):
                if source is not None:
                    for t in range(NT):
                        nc.scalar.activation(X[:, t, :], source[:, t, :], ACT.Identity, scale=rstd[:, t:t + 1], bias=shift[:, t:t + 1])\
                          .then_inc(normed, 1)
                act.wait_ge(var_ready, 1)
                nc.scalar.activation(b[:], c[:], ACT.Sqrt).then_inc(root_ready, 1)


def project(nc, name, cs, X, rstd, shift, weight, jobs, finish, affine=None, UT=None, rows_out=None, stores=()):
    J = len(jobs)
    S5 = 5
    with Phase(nc, name) as ph:
        row = ph.sb("row", [TN, S5, D])
        rowT = ph.sb("rowT", [P, S5, 2, TN])
        tp = [ph.psum(f"tp{s}", [P, 512]) for s in range(3)]
        pj = [ph.psum(f"pj{s}", [TN, 512]) for s in range(5)] if J else []
        W = ph.sb("W", [P, 2, weight.shape[1]]) if J else None
        G = ph.sb("G", [TN, 2, D]) if affine else None
        loaded, row_ready, turned, copied, projected, finished, link_s, passed, kept, pool_on, dve_on, act_on = (
            ph.sem(k) for k in ("loaded", "row", "turned", "copied", "projected", "finished", "link", "passed", "kept", "pool_on",
                                "dve_on", "act_on"))
        stored, sp_on = ph.sem("stored"), ph.sem("sp_on")
        keep_rows, keep_turned = rows_out is not None, UT is not None and J > 0

        def turns(eng, lead, ahead, step):
            def one_turn(i, last):
                for s in range(S5):
                    if not (last and s >= S5 - lead):
                        ahead(i + (s + lead) // S5, (s + lead) % S5)
                    step(i, s)
            for s in range(lead):
                ahead(0, s)
            with eng.Fori(0, NT // S5 - 1) as i:
                one_turn(i, False)
            one_turn(NT // S5 - 1, True)

        with nc.Block() as block:
            @block.sync
            def _(sp):
                if J:
                    sp.dma_start(W[:], weight.rearrange("(k p) n -> p k n", p=P)).then_inc(loaded, 16)
                if affine:
                    for k in range(2):
                        sp.dma_start(G[:, k, :], affine[k].partition_broadcast(TN)).then_inc(loaded, 16)
                if stores:
                    with sp.Fori(0, NT // S5) as i:
                        for s in range(S5):
                            sp.wait_ge(finished, i * (S5 * J) + (s * J + J + 5))
                            sp.sem_inc(sp_on, 1)
                            if keep_rows:
                                sp.wait_ge(kept, i * S5 + (s + 6))
                                sp.sem_inc(sp_on, 1)
                            for table, buffer in stores:
                                sp.dma_start(table[bass.ds(i * (S5 * TN) + s * TN, TN), :], buffer[:, i * S5 + s, :]).then_inc(stored, 16)
                    sp.wait_ge(stored, 16 * NT * len(stores))

            @block.vector
            def _(v):
                if affine:
                    v.wait_ge(loaded, 16 * (2 + (J > 0)))
                v.sem_inc(finished, 5)

                def make_row(i, s):
                    t = i * S5 + s
                    at = bass.ds(t, 1)
                    v.wait_ge(copied, i * S5 + (s + 1))
                    v.sem_inc(dve_on, 1)
                    if keep_rows:
                        v.wait_ge(kept, i * S5 + (s + 1))
                        v.sem_inc(dve_on, 1)
                    ins = v.tensor_scalar(row[:, s, :], X[:, t, :], rstd[:, at], shift[:, at], ALU.mult, ALU.add)
                    if affine:
                        link = chain(v, link_s, i * (2 * S5) + 2 * s)
                        link(ins)
                        link(v.tensor_tensor(row[:, s, :], row[:, s, :], G[:, 0, :], ALU.mult))
                        ins = v.tensor_tensor(row[:, s, :], row[:, s, :], G[:, 1, :], ALU.add)
                    ins.then_inc(row_ready, 1)

                def finish_tile(i, s):
                    for j in range(J):
                        q = s * J + j
                        v.wait_ge(projected, i * (S5 * J) + (q + 1))
                        v.sem_inc(dve_on, 1)
                        finish(v, j, i * S5 + s, s, pj[q % 5][:, 0:jobs[j][1]]).then_inc(finished, 1)

                turns(v, 3, make_row, finish_tile)
                v.wait_ge(finished, NT * J + 5)

            @block.tensor
            def _(pe):
                if J:
                    pe.wait_ge(loaded, 16 * (1 + 2 * bool(affine)))

                def turn(i, s):
                    pe.wait_ge(row_ready, i * S5 + (s + 1))
                    pe.sem_inc(passed, 1)
                    pe.wait_ge(copied, i * S5 + (4, 5, 3, 6, 7)[s])
                    pe.sem_inc(passed, 1)
                    for k in range(2):
                        ins = pe.transpose(tp[s % 3][:, k * TN:(k + 1) * TN], row[:, s, k * P:(k + 1) * P], cs.ident[0:TN, 0:TN])
                    ins.then_inc(turned, 1)

                def products(i, s):
                    if J == 0:
                        return
                    pe.wait_ge(copied, i * S5 + (s + 6))
                    for j, (c0, w) in enumerate(jobs):
                        q = s * J + j
                        pe.wait_ge(finished, i * (S5 * J) + (q + 1))
                        for k in range(2):
                            ins = pe.matmul(pj[q % 5][:, 0:w], rowT[:, s, k, :], W[:, k, c0:c0 + w],
                                            start=(k == 0), stop=(k == 1))
                        ins.then_inc(projected, 1)

                turns(pe, 1, turn, products)

            @block.scalar
            def _(act):
                act.sem_inc(copied, S5)
                with act.Fori(0, NT // S5) as i:
                    for s in range(S5):
                        t = i * S5 + s
                        act.wait_ge(turned, i * S5 + (s + 1))
                        act.sem_inc(act_on, 1)
                        if keep_turned:
                            act.wait_ge(kept, i * S5 + (s + 1))
                            act.sem_inc(act_on, 1)
                        tile = tp[s % 3][:, 0:2 * TN].rearrange("p (k n) -> p k n", k=2)
                        dest = rowT[:, s, :, :] if J else UT[:, :, bass.ds(t * TN, TN)]
                        nc.scalar.copy(dest, tile).then_inc(copied, 1)

            @block.gpsimd
            def _(g):
                if keep_rows or keep_turned:
                    g.sem_inc(kept, S5)
                    with g.Fori(0, NT // S5) as i:
                        for s in range(S5):
                            t = i * S5 + s
                            g.wait_ge(copied, i * S5 + (s + 6))
                            g.sem_inc(pool_on, 1)
                            if keep_rows:
                                ins = g.tensor_copy(rows_out[:, t, :], row[:, s, :])
                            if keep_turned:
                                ins = g.tensor_copy(UT[:, :, bass.ds(t * TN, TN)], rowT[:, s, :, :])
                            ins.then_inc(kept, 1)
                    g.wait_ge(kept, NT + S5)


class Consts:

    def __init__(self, sb):
        self.ident = sb("ident", [P, P])
        self.ones = sb("ones", [P, P])
        self.count_row = sb("count_row", [P, pairs_of(E1)])
        self.count_col = sb("count_col", [P, 1])
        self.neg_col = sb("neg_col", [P, 1])


def pairs_of(edges):
    most = (edges + P - 1) // P + NT - 1
    return (most // 32 + 1) * 32


class Graph:

    def __init__(self, name, sb, dram, consts, edges):
        self.ident, self.ones, self.count_row = consts.ident, consts.ones, consts.count_row
        self.count_col, self.neg_col = consts.count_col, consts.neg_col
        self.name, self.edges, self.pairs = name, edges, pairs_of(edges)
        self.loops = self.pairs // TURN
        self.src_of = sb(f"{name}_src_of", [P, self.pairs], I32)
        self.tile_of = sb(f"{name}_tile_of", [1, self.pairs], I32)
        self.local = sb(f"{name}_local", [P, self.pairs])
        self.neg_local = sb(f"{name}_neg_local", [P, self.pairs])
        self.neg_big = sb(f"{name}_neg_big", [P, self.pairs])
        self.last_of = sb(f"{name}_last_of", [P, self.pairs])
        self.local_rows = dram(f"{name}_local_rows", [self.pairs, P]).ap()
        self.keys_t = dram(f"{name}_keys", [self.pairs * P + 2])
        self.keys = self.keys_t.ap()


def constants(nc, cs):
    with Phase(nc, "const") as ph:
        made = ph.sem("made")
        t32 = ph.sb("t32", [P, cs.count_row.shape[1]], I32)
        p32 = ph.sb("p32", [P, 1], I32)
        with nc.Block() as block:
            @block.gpsimd
            def _(g):
                link = chain(g, made)
                link(g.memset(cs.ident[:], 0.0))
                link(g.affine_select(out=cs.ident[:], in_=cs.ident[:], compare_op=ALU.not_equal, fill=1.0,
                                     base=0, pattern=[[-1, P]], channel_multiplier=1))
                link(g.iota(t32[:], pattern=[[1, cs.count_row.shape[1]]], base=0, channel_multiplier=0))
                link(g.tensor_copy(cs.count_row[:], t32[:]))
                link(g.iota(p32[:], pattern=[[1, 1]], base=0, channel_multiplier=1))
                link(g.tensor_copy(cs.count_col[:], p32[:]))
                link(g.tensor_scalar(cs.neg_col[:], cs.count_col[:], -1.0, None, ALU.mult))
                link(g.memset(cs.ones[:], 1.0))


class IndexTables:

    def __init__(self, ph, nc, cs, src=None, dst=None, joined=None):
        PAIRS, E = cs.pairs, cs.edges
        PR = PAIRS // 4
        NB = (PAIRS + P - 1) // P
        count = cs.count_row[:, 0:PAIRS]
        raw = ph.sb("raw", [P, 2, NB, P] if joined is None else [P, NB, P, 2], I32)
        raw_of = [raw[:, k, :, :] if joined is None else raw[:, :, :, k] for k in range(2)]
        val = ph.sb("val", [P, 2, NB, P])
        W = NT - 1 + NB * P
        lanes = ph.sb("lanes", [P, 2, W])
        less = ph.sb("less", [P, NT - 1])
        junk = ph.sb("junk", [P, 2, NB * P])
        first = ph.sb("first", [P, NT - 1])
        firsti = ph.sb("firsti", [P, NT - 1], I32)
        mask = ph.sb("mask", [P, 2, PAIRS], I32)
        srcx = ph.sb("srcx", [P, PAIRS])
        dstx = ph.sb("dstx", [P, PAIRS])
        tile_f = ph.sb("tile_f", [P, PAIRS])
        valid = ph.sb("valid", [P, PAIRS])
        key = ph.sb("key", [P, PAIRS])
        rows = ph.sb("rows", [PR, 2, 4, P])
        near = ph.sb("near", [PR, 2, 4, P])
        edge1 = ph.sb("edge1", [1, 2])
        banks = [ph.psum(f"bank{b}", [P, 512]) for b in range(3)]
        pt = [banks[b][:, 0:NB * P].rearrange("p (b l) -> p b l", l=P) for b in range(2)]
        pr = [banks[b][0:PR, :].rearrange("p (b l) -> p b l", l=P) for b in range(2)]
        pn = banks[2][:, 0:NT - 1]
        pe_end = banks[2][:, :].rearrange("p (b l) -> p b l", l=P)
        filled, loaded, cast, turned, summed, tables, rowed, in_rows, written, near_in, ends, ended, v_link = (
            ph.sem(f"t_{k}") for k in ("filled", "loaded", "cast", "turned", "summed", "tables", "rowed", "in_rows", "written",
                                "near_in", "ends", "ended", "link"))
        FB = E // (P * P)
        full = FB * P * P
        rest = (E - full) // P
        tail = E - full - rest * P
        n_loads = 1 if joined is not None else 2 * (1 + (rest > 0) + (tail > 0))
        assert joined is None or full == E

        def sync(sp):
            sp.wait_ge(filled, 2)
            if joined is not None:
                sp.dma_start(raw[:, 0:FB, :, :], joined.rearrange("(b t l) k -> t b l k", b=FB, l=P)).then_inc(loaded, 16)
            for k, a in enumerate((dst, src) if joined is None else ()):
                sp.dma_start(raw[:, k, 0:FB, :], a[0:full].rearrange("(b t l) -> t b l", b=FB, l=P)).then_inc(loaded, 16)
                if rest:
                    sp.dma_start(raw[0:rest, k, FB, :], a[full:full + rest * P].rearrange("(t l) -> t l", l=P)).then_inc(loaded, 16)
                if tail:
                    sp.dma_start(raw[rest:rest + 1, k, FB, 0:tail], a[E - tail:E].rearrange("(t l) -> t l", t=1)).then_inc(loaded, 16)
            sp.wait_ge(in_rows, 2)
            sp.dma_start(cs.local_rows.rearrange("(b r) l -> r b l", b=4), rows[:, 0, :, :]).then_inc(written, 16)
            body = cs.keys[1:1 + PAIRS * P]
            sp.dma_start(body.rearrange("(b r l) -> r b l", b=4, l=P), rows[:, 1, :, :]).then_inc(written, 16)
            sp.dma_start(cs.keys[0:1].rearrange("(a b) -> a b", a=1), edge1[:, 0:1]).then_inc(written, 16)
            sp.dma_start(cs.keys[1 + PAIRS * P:2 + PAIRS * P].rearrange("(a b) -> a b", a=1), edge1[:, 1:2]).then_inc(written, 16)
            sp.wait_ge(written, 64)
            for k in range(2):
                sp.dma_start(near[:, k, :, :], cs.keys[1 + k:1 + k + PAIRS * P].rearrange("(b r l) -> r b l", b=4, l=P)).then_inc(near_in, 16)
            sp.wait_ge(near_in, 32)

        def vector(v):
            v.memset(raw_of[0][:, FB, :], int(NO_DST)).then_inc(filled, 1)
            v.memset(raw_of[1][:, FB, :], 0).then_inc(filled, 1)
            link = chain(v, v_link)
            link(v.memset(edge1[:], NO_KEY))
            link(v.memset(lanes[:], 0.0))
            v.wait_ge(loaded, 16 * n_loads)
            v.tensor_copy(val[:, 0, :, :], raw_of[0])
            v.tensor_copy(val[:, 1, :, :], raw_of[1]).then_inc(cast, 1)
            v.wait_ge(cast, 1)
            for j in range(1, NT):
                link(v.tensor_scalar(junk[:, j % 2, :], val[:, 0, :, :].rearrange("p b l -> p (b l)"), float(TN * j), 0.0,
                                     ALU.is_lt, ALU.add, accum_out=less[:, j - 1:j]), early=j < NT - 1)
            v.sem_inc(cast, 1)
            v.wait_ge(turned, 2)
            for k in range(2):
                link(v.tensor_copy(lanes[:, k, NT - 1:NT - 1 + NB * P], pt[k].rearrange("p b l -> p (b l)")))
            v.wait_ge(summed, 1)
            link(v.tensor_copy(firsti[:], pn))
            link(v.tensor_scalar(firsti[:], firsti[:], 7, None, ALU.arith_shift_right))
            link(v.tensor_copy(first[:], firsti[:]))
            link(v.scalar_tensor_tensor(out=first[:], in0=first[:], scalar=1.0, in1=cs.count_row[:, 0:NT - 1], op0=ALU.add, op1=ALU.add))
            link(v.memset(tile_f[:], 0.0))
            link(v.tensor_copy(dstx[:], lanes[:, 0, NT - 1:NT - 1 + PAIRS]))
            link(v.tensor_copy(srcx[:], lanes[:, 1, NT - 1:NT - 1 + PAIRS]))
            for j in range(1, NT):
                at = first[:, j - 1:j]
                link(v.tensor_scalar(mask[:, j % 2, :], count, at, None, ALU.is_ge), early=True)
                link(v.scalar_tensor_tensor(out=tile_f[:], in0=count, scalar=at, in1=tile_f[:], op0=ALU.is_ge, op1=ALU.add), early=True)
                link(v.copy_predicated(dstx[:], mask[:, j % 2, :], lanes[:, 0, NT - 1 - j:NT - 1 - j + PAIRS]), early=True)
                link(v.copy_predicated(srcx[:], mask[:, j % 2, :], lanes[:, 1, NT - 1 - j:NT - 1 - j + PAIRS]), early=j < NT - 1)
            link(v.tensor_copy(cs.src_of[:], srcx[:]))
            link(v.tensor_copy(cs.tile_of[:], tile_f[0:1, :]))
            link(v.scalar_tensor_tensor(out=cs.local[:], in0=tile_f[:], scalar=-float(TN), in1=dstx[:], op0=ALU.mult, op1=ALU.add))
            link(v.tensor_scalar(cs.neg_local[:], cs.local[:], -1.0, None, ALU.mult))
            link(v.tensor_scalar(valid[:], cs.local[:], 0.0, None, ALU.is_ge))
            link(v.scalar_tensor_tensor(out=valid[:], in0=cs.local[:], scalar=float(TN), in1=valid[:], op0=ALU.is_lt, op1=ALU.mult))
            link(v.tensor_scalar(cs.neg_big[:], valid[:], BIG, -BIG, ALU.mult, ALU.add))
            link(v.scalar_tensor_tensor(out=key[:], in0=dstx[:], scalar=1.0, in1=valid[:], op0=ALU.add, op1=ALU.mult))
            link(v.tensor_scalar(key[:], key[:], -1.0, None, ALU.add))
            v.sem_inc(tables, 1)
            for k in range(2):
                v.wait_ge(rowed, k + 1)
                v.tensor_copy(rows[:, k, :, :], pr[k]).then_inc(in_rows, 1)
            v.wait_ge(near_in, 32)
            v.tensor_tensor(near[:, 0, :, :], near[:, 0, :, :], near[:, 1, :, :], ALU.not_equal).then_inc(ends, 1)
            v.wait_ge(ended, 1)
            link(v.tensor_copy(cs.last_of[:].rearrange("p (b r) -> p b r", b=4), pe_end[:, :, 0:PR]))

        def tensor0(pe):
            pe.wait_ge(cast, 1)
            for k in range(2):
                for b in range(NB):
                    ins = pe.transpose(pt[k][:, b, :], val[:, k, b, :], cs.ident[:])
                ins.then_inc(turned, 1)

        def tensor1(pe):
            pe.wait_ge(cast, 2)
            pe.matmul(pn, cs.ones[:], less[:], start=True, stop=True).then_inc(summed, 1)

        def tensor2(pe):
            pe.wait_ge(tables, 1)
            for k, table in enumerate((cs.local, key)):
                for b in range(4):
                    ins = pe.transpose(pr[k][:, b, :], table[:, b * PR:(b + 1) * PR], cs.ident[:])
                ins.then_inc(rowed, 1)

        def tensor3(pe):
            pe.wait_ge(ends, 1)
            for b in range(4):
                ins = pe.transpose(pe_end[:, b, 0:PR], near[:, 0, b, :], cs.ident[0:PR, 0:PR])
            ins.then_inc(ended, 1)

        self.sync, self.vector, self.tensor = sync, vector, (tensor0, tensor1, tensor2, tensor3)


def index_tables(nc, cs, src=None, dst=None, joined=None):
    with Phase(nc, cs.name) as ph:
        tables = IndexTables(ph, nc, cs, src, dst, joined)
        with nc.Block() as block:
            @block.sync
            def _(sp):
                tables.sync(sp)

            @block.vector
            def _(v):
                tables.vector(v)

            @block.tensor
            def _(pe):
                for step in tables.tensor:
                    step(pe)


class EdgeSort:

    def __init__(self, sb, edges, pay, pos):
        self.tiles = edges // P
        self.turns = self.tiles // TURN
        self.pay, self.pos = pay, pos
        self.lanes = sb("sort_lanes", [P, 2, self.tiles])
        self.a_of, self.b_of = (sb(k, [P, self.tiles + 2 * PB]) for k in ("sort_a", "sort_b"))
        self.ident = sb("sort_ident", [P, P], BF16)
        self.start = sb("sort_start", [NT, TN])
        self.earlier = sb("sort_earlier", [P, 2 * P])


def make_hots(v, cs, es, tiles, hotA, hotB):
    wide = lambda x, n: x[:, tiles].unsqueeze(2).to_broadcast([P, PB, n])
    number = lambda n: cs.count_row[:, 0:n].unsqueeze(1).to_broadcast([P, PB, n])
    v.tensor_tensor(hotA, number(NT), wide(es.a_of, NT), ALU.is_equal)
    return v.tensor_tensor(hotB, number(TN), wide(es.b_of, TN), ALU.is_equal)


def histogram(nc, cs, edge_index, es):
    NB = es.tiles // P
    A = NT
    with Phase(nc, "hist") as ph:
        raw = ph.sb("raw", [P, 2, NB, P], I32)
        val = ph.sb("val", [P, 2, NB, P])
        upper = ph.sb("upper", [A, A])
        zero = ph.sb("zero", [P, TN], BF16)
        hotA = ph.sb("hotA", [P, RING, PB, A], BF16)
        hotB = ph.sb("hotB", [P, RING, PB, TN], BF16)
        hist, incl, zeros = (ph.sb(k, [A, TN]) for k in ("hist", "incl", "zeros"))
        before = ph.sb("before", [A, 1])
        near = ph.sb("near", [P, es.tiles], I32)
        pt = [ph.psum(f"pt{k}", [P, NB, P]) for k in range(2)]
        counts = ph.psum("counts", [A, 512])
        below = ph.psum("below", [A, 512])
        loaded, cast, turned, consts, v_link, g_link, hot1, summed1, hist_out, off, off_in, pe_on, dve_on = (
            ph.sem(k) for k in ("loaded", "cast", "turned", "consts", "v_link", "g_link", "hot1", "summed1", "hist", "off", "off_in",
                                "pe_on", "dve_on"))
        with nc.Block() as block:
            @block.sync
            def _(sp):
                for k in range(2):
                    sp.dma_start(raw[:, k, :, :], edge_index[1 - k].rearrange("(b t l) -> t b l", b=NB, l=P)).then_inc(loaded, 16)

            @block.gpsimd
            def _(g):
                link = chain(g, g_link)
                link(g.memset(es.earlier[:], 1.0))
                link(g.memset(upper[:], 1.0))
                tri = es.earlier[:, P:2 * P]
                link(g.affine_select(out=tri, in_=tri, compare_op=ALU.is_gt, fill=0.0, base=0, pattern=[[-1, P]], channel_multiplier=1))
                link(g.affine_select(out=upper[:], in_=upper[:], compare_op=ALU.is_gt, fill=0.0, base=0,
                                     pattern=[[1, A]], channel_multiplier=-1))
                g.sem_inc(consts, 1)

            @block.vector
            def _(v):
                link = chain(v, v_link)
                v.wait_ge(loaded, 32)
                v.tensor_copy(val[:], raw[:]).then_inc(cast, 1)
                link(v.memset(es.a_of[:], 0.0))
                link(v.memset(es.b_of[:], 0.0))
                link(v.tensor_copy(es.ident[:], cs.ident[:]))
                link(v.memset(zero[:], 0.0))
                link(v.memset(zeros[:], 0.0))
                v.wait_ge(turned, 2)
                for k in range(2):
                    link(v.tensor_copy(es.lanes[:, k, :], pt[k][:].rearrange("p b l -> p (b l)")))
                    link(v.tensor_copy(es.pay[:, :, k], es.lanes[:, k, :]))
                dst, a_of, b_of = es.lanes[:, 0, :], es.a_of[:, 0:es.tiles], es.b_of[:, 0:es.tiles]
                link(v.tensor_scalar(near[:], dst, 1.0 / TN, 0.5 / TN - 0.5, ALU.mult, ALU.add))
                link(v.tensor_copy(a_of, near[:]))
                link(v.scalar_tensor_tensor(out=b_of, in0=a_of, scalar=-float(TN), in1=dst, op0=ALU.mult, op1=ALU.add))
                link(v.scalar_tensor_tensor(out=a_of, in0=b_of, scalar=float(TN), in1=a_of, op0=ALU.is_ge, op1=ALU.add))
                link(v.scalar_tensor_tensor(out=b_of, in0=b_of, scalar=0.0, in1=a_of, op0=ALU.is_lt, op1=ALU.subtract))
                link(v.tensor_scalar(a_of, b_of, -1.0, None, ALU.mult))
                link(v.scalar_tensor_tensor(out=b_of, in0=a_of, scalar=-float(TN), in1=dst, op0=ALU.mult, op1=ALU.add))
                with v.Fori(0, es.turns) as i:
                    for q in range(RING):
                        v.wait_ge(summed1, i * RING + (q + 1))
                        v.sem_inc(dve_on, 1)
                        make_hots(v, cs, es, bass.ds(i * TURN + q * PB, PB), hotA[:, q, :, :], hotB[:, q, :, :]).then_inc(hot1, 1)
                v.wait_ge(summed1, es.turns * RING + RING)
                v.tensor_copy(hist[:], counts[:, 0:TN]).then_inc(hist_out, 1)
                v.wait_ge(hist_out, 1)
                link(v.tensor_tensor_scan(incl[:], zeros[:], hist[:], 0.0, ALU.add, ALU.add))
                v.sem_inc(off, 1)
                v.wait_ge(off_in, 1)
                link(v.tensor_copy(before[:], below[:, 0:1]))
                link(v.tensor_tensor(es.start[:], incl[:], hist[:], ALU.subtract))
                link(v.tensor_scalar(es.start[:], es.start[:], before[:, 0:1], None, ALU.add))

            @block.tensor
            def _(pe):
                pe.wait_ge(cast, 1)
                for k in range(2):
                    for b in range(NB):
                        ins = pe.transpose(pt[k][:, b, :], val[:, k, b, :], cs.ident[:])
                    ins.then_inc(turned, 1)
                pe.sem_inc(summed1, RING)
                pe.wait_ge(hot1, 1)
                pe.matmul(counts[:, 0:TN], zero[:, 0:A], zero[:], start=True, stop=True)
                with pe.Fori(0, es.turns) as i:
                    for q in range(RING):
                        pe.wait_ge(hot1, i * RING + (q + 1))
                        pe.sem_inc(pe_on, 1)
                        for u in range(PB):
                            ins = pe.matmul(counts[:, 0:TN], hotA[:, q, u, :], hotB[:, q, u, :], start=False, stop=True, skip_group_check=True)
                        ins.then_inc(summed1, 1)
                pe.wait_ge(off, 1)
                pe.wait_ge(consts, 1)
                pe.matmul(below[:, 0:1], upper[:], incl[:, TN - 1:TN], start=True, stop=True).then_inc(off_in, 1)


class Ranks:

    def __init__(self, ph, nc, cs, es, edge_index):
        self.nc, self.cs, self.es, self.edge_index = nc, cs, es, edge_index
        self.rows = ph.sb("r_rows", [P, RING, PB * P], I32)
        self.hotA = ph.sb("r_hotA", [P, RING, PB, NT], BF16)
        self.hotB = ph.sb("r_hotB", [P, RING, PB, TN], BF16)
        self.hotT = ph.sb("r_hotT", [NT, 2, PB, P])
        self.snap = ph.sb("r_snap", [NT, 2, 2, TN])
        self.same = ph.sb("r_same", [P, PB, 2 * P])
        self.pick = ph.sb("r_pick", [P, PB, TN])
        self.n_same, self.n_before = ph.sb("r_n_same", [P, 2, PB]), ph.sb("r_n_before", [P, 2, PB])
        self.counts = ph.psum("r_counts", [NT, 512])
        self.pa = ph.psum("r_pa", [NT, 2 * PB, P], BF16)
        self.pr = [ph.psum(f"r_pr{k}", [P, 512]) for k in range(2)]
        self.hots, self.hot_turned, self.hot_copied, self.snapped, self.grown, self.ranked, self.looked, self.compared, self.placed = (
            ph.sem(f"r_{k}") for k in ("hots", "hot_turned", "hot_copied", "snapped", "grown", "ranked", "looked", "compared", "placed"))
        self.pe_on, self.act_on, self.sp_on, self.dve_on = (
            ph.sem(f"r_{k}") for k in ("pe_on", "act_on", "sp_on", "dve_on"))
        self.rows_in = [ph.sem(f"r_rows{q}") for q in range(RING)]

    def load(self, sp, i, q):
        sp.wait_ge(self.compared, i * RING + (q + 1))
        sp.sem_inc(self.sp_on, 1)
        sp.dma_start(self.rows[:, q, :], self.edge_index[1, bass.ds(i * (TURN * P) + q * PB * P, PB * P)].partition_broadcast(P))\
          .then_inc(self.rows_in[q], 16)

    def turn_hots(self, pe, slot):
        for u in range(PB):
            ins = pe.transpose(self.pa[:, u, :], self.hotA[:, slot, u, :], self.es.ident[:])
        ins.then_inc(self.hot_turned, 1)

    def start_tensor(self, pe):
        pe.matmul(self.counts[:, 0:TN], self.cs.ident[0:NT, 0:NT], self.es.start[:], start=True, stop=True).then_inc(self.grown, 1)
        pe.wait_ge(self.hots, 1)
        self.turn_hots(pe, 0)
        pe.sem_inc(self.ranked, 1)

    def grow(self, pe, q, s):
        for u in (2 * s, 2 * s + 1):
            ins = pe.matmul(self.counts[:, 0:TN], self.hotA[:, q, u, :], self.hotB[:, q, u, :], start=False, stop=True,
                            skip_group_check=True)
        ins.then_inc(self.grown, 1)

    def tensor(self, pe, i, q):
        pe.wait_ge(self.snapped, i * (2 * RING) + (2 * q + 1))
        pe.sem_inc(self.pe_on, 1)
        self.grow(pe, q, 0)
        pe.wait_ge(self.hots, i * RING + (q + 2))
        pe.sem_inc(self.pe_on, 1)
        pe.wait_ge(self.hot_copied, i * RING + (q + 1))
        pe.sem_inc(self.pe_on, 1)
        self.turn_hots(pe, (q + 1) % RING)
        pe.wait_ge(self.snapped, i * (2 * RING) + (2 * q + 2))
        pe.sem_inc(self.pe_on, 1)
        self.grow(pe, q, 1)
        pe.wait_ge(self.looked, i * RING + (q + 1))
        pe.sem_inc(self.pe_on, 1)
        for u in range(PB):
            ins = pe.matmul(self.pr[q % 2][:, u * TN:(u + 1) * TN], self.hotT[:, q % 2, u, :], self.snap[:, q % 2, u // 2, :],
                            start=True, stop=True)
        ins.then_inc(self.ranked, 1)

    def keep_counts(self, slot, s):
        self.nc.scalar.copy(self.snap[:, slot, s, :], self.counts[:, 0:TN]).then_inc(self.snapped, 1)

    def copy_hots(self, slot):
        self.nc.scalar.copy(self.hotT[:, slot, :, :], self.pa[:, 0:PB, :]).then_inc(self.hot_copied, 1)

    def start_scalar(self, act):
        act.wait_ge(self.grown, 1)
        self.keep_counts(0, 0)
        act.wait_ge(self.hot_turned, 1)
        self.copy_hots(0)

    def scalar(self, act, i, q):
        act.wait_ge(self.grown, i * (2 * RING) + (2 * q + 2))
        act.sem_inc(self.act_on, 1)
        self.keep_counts(q % 2, 1)
        act.wait_ge(self.ranked, i * RING + (q + 1))
        act.sem_inc(self.act_on, 1)
        act.wait_ge(self.hot_turned, i * RING + (q + 2))
        act.sem_inc(self.act_on, 1)
        self.copy_hots((q + 1) % 2)
        act.wait_ge(self.grown, i * (2 * RING) + (2 * q + 3))
        act.sem_inc(self.act_on, 1)
        self.keep_counts((q + 1) % 2, 0)

    def make(self, v, i, q):
        slot = q % RING
        make_hots(v, self.cs, self.es, bass.ds(i * TURN + q * PB, PB), self.hotA[:, slot, :, :],
                  self.hotB[:, slot, :, :]).then_inc(self.hots, 1)

    def start_vector(self, v):
        self.make(v, 0, 0)
        self.make(v, 0, 1)
        v.sem_inc(self.looked, 2)
        v.sem_inc(self.placed, 2)
        v.sem_inc(self.compared, RING)

    def compare(self, v, i, q):
        self.make(v, i, q + 2)
        v.wait_ge(self.placed, i * RING + (q + 1))
        v.sem_inc(self.dve_on, 1)
        v.wait_ge(self.rows_in[q], i * 16 + 16)
        v.sem_inc(self.dve_on, 1)
        for u in range(PB):
            w = (u % 2 + 1) * P
            ins = v.scalar_tensor_tensor(out=self.same[:, u, 0:w], in0=self.rows[:, q, (u + 1) * P - w:(u + 1) * P],
                                         scalar=self.es.lanes[:, 0, bass.ds(i * TURN + q * PB + u, 1)], in1=self.es.earlier[:, 2 * P - w:2 * P],
                                         op0=ALU.is_equal, op1=ALU.mult, accum_out=self.n_same[:, q % 2, u:u + 1])
        ins.then_inc(self.compared, 1)

    def place(self, v, i, q):
        v.wait_ge(self.ranked, i * RING + (q + 2))
        v.sem_inc(self.dve_on, 1)
        for u in range(PB):
            ins = v.tensor_tensor_reduce(out=self.pick[:, u, :], in0=self.pr[q % 2][:, u * TN:(u + 1) * TN], in1=self.hotB[:, q, u, :],
                                         scale=1.0, scalar=0.0, op0=ALU.mult, op1=ALU.add, accum_out=self.n_before[:, q % 2, u:u + 1])
        ins.then_inc(self.looked, 1)
        v.wait_ge(self.looked, i * RING + (q + 3))
        v.sem_inc(self.dve_on, 1)
        v.tensor_tensor(self.es.pos[:, bass.ds(i * TURN + q * PB, PB)], self.n_same[:, q % 2, :], self.n_before[:, q % 2, :],
                        ALU.add).then_inc(self.placed, 1)

    def end_vector(self, v):
        v.wait_ge(self.placed, self.es.tiles // PB + 2)


def scatter_edges(g, es, joined, at, payload, out, copied, pool_on):
    def turn(i, first):
        for q in range(RING):
            if not first:
                g.wait_ge(out[q], i * (16 * PB))
                g.sem_inc(pool_on, 1)
            tiles = bass.ds(i * TURN + q * PB, PB)
            g.tensor_copy(at[:, q, :], es.pos[:, tiles])
            g.tensor_copy(payload[:, q, :, :], es.pay[:, tiles, :]).then_inc(copied, 1)
            g.wait_ge(copied, i * RING + (q + 1))
            g.sem_inc(pool_on, 1)
            for u in range(PB):
                g.indirect_dma_start(out=joined, out_offset=bass.IndirectOffsetOnAxis(ap=at[:, q, u:u + 1], axis=0),
                                     in_=payload[:, q, u, :], in_offset=None).then_inc(out[q], 16)
    turn(0, True)
    with g.Fori(1, es.turns) as i:
        turn(i, False)
    for q in range(RING):
        g.wait_ge(out[q], 16 * PB * es.turns)


def gather_pairs(g, cs, table, ring, idx, idx_ready, slot_free, got, passed):
    with g.Fori(0, cs.loops // 2) as i:
        for h in range(2):
            g.tensor_copy(idx[:, h, :], cs.src_of[:, bass.ds(i * (2 * TURN) + h * TURN, TURN)]).then_inc(idx_ready, 1)
            g.wait_ge(idx_ready, i * 2 + (h + 1))
            g.sem_inc(passed, 1)
            for q in range(RING):
                g.wait_ge(slot_free, i * (2 * RING) + (h * RING + q + 1))
                g.sem_inc(passed, 1)
                for u in range(PB):
                    k = q * PB + u
                    g.indirect_dma_start(out=ring[:, k, :], out_offset=None, in_=table,
                                         in_offset=bass.IndirectOffsetOnAxis(ap=idx[:, h, k:k + 1], axis=0)).then_inc(got[q], 16)


def load_tiles(eng, regs, cs, i, q):
    eng.load(regs, cs.tile_of[0:1, bass.ds(i * TURN + q * PB, PB)])
    return [eng.snap(r, min_val=0, max_val=NT - 1) for r in regs]


def load_local_rows(sp, cs, Lb, lb_got, hot_ready, passed, i, q):
    sp.wait_ge(hot_ready, i * RING + (q + 1))
    sp.sem_inc(passed, 1)
    rows = cs.local_rows[bass.ds(i * (TURN) + q * PB, PB), :].rearrange("r l -> (r l)")
    sp.dma_start(Lb[:, q, :], rows.partition_broadcast(TN)).then_inc(lb_got[q], 16)


def node_hots(nc, act, cs, Lb, hotT, dist, lb_got, hot_ready, dist_ready, i, q):
    act.wait_ge(lb_got[q], i * 16 + 16)
    act.sem_inc(dist_ready[1], 1)
    nc.scalar.activation(dist[:, q, :], Lb[:, q, :], ACT.Abs, bias=cs.neg_col[0:TN, :]).then_inc(dist_ready[0], 1)
    act.wait_ge(dist_ready[0], i * RING + (q + 1))
    nc.scalar.activation(hotT[:, q, :], dist[:, q, :], ACT.Relu, scale=-1.0, bias=1.0).then_inc(hot_ready, 1)


def edge_scores(nc, cs, q_dram, K, S, es, edge_index):
    with Phase(nc, "score") as ph:
        ring = ph.sb("ring", [P, TURN, D])
        idx = ph.sb("idx", [P, 2, TURN], I32)
        Lb = ph.sb("Lb", [TN, RING, PB * P])
        hotT = ph.sb("hotT", [TN, RING, PB * P])
        dist = ph.sb("dist", [TN, RING, PB * P])
        prod = ph.sb("prod", [P, 2, PB * D])
        kd = [ph.psum(f"kd{q}", [P, PB * D]) for q in range(2)]
        idx_ready, hot_ready, kd_ready, multiplied, reduced, dist_ready, pool_on, sp_on, act_on, pe_on, dve_on = (
            ph.sem(k) for k in ("idx", "hot", "kd", "multiplied", "reduced", "dist", "pool_on", "sp_on", "act_on", "pe_on", "dve_on"))
        got = [ph.sem(f"got{q}") for q in range(RING)]
        lb_got = [ph.sem(f"lb{q}") for q in range(RING)]
        ranks = Ranks(ph, nc, cs, es, edge_index)

        def turns(eng, step, rank):
            with eng.Fori(0, es.turns) as i:
                for q in range(RING):
                    step(i, q)
                    rank(eng, i, q)
            with eng.Fori(es.turns, cs.loops) as i:
                for q in range(RING):
                    step(i, q)

        with nc.Block() as block:
            @block.gpsimd
            def _(g):
                gather_pairs(g, cs, q_dram, ring, idx, idx_ready, multiplied, got, pool_on)

            @block.sync
            def _(sp):
                turns(sp, lambda i, q: load_local_rows(sp, cs, Lb, lb_got, hot_ready, sp_on, i, q), ranks.load)

            @block.scalar
            def _(act):
                act.sem_inc(hot_ready, RING)
                ranks.start_scalar(act)

                def step(i, q):
                    act.wait_ge(kd_ready, i * RING + (q + 1))
                    act.sem_inc(act_on, 1)
                    node_hots(nc, act, cs, Lb, hotT, dist, lb_got, hot_ready, (dist_ready, act_on), i, q)
                step(0, 0)
                with act.Fori(0, es.turns) as i:
                    for q in range(RING):
                        step(i + (q + 1) // RING, (q + 1) % RING)
                        ranks.scalar(act, i, q)
                for q in range(1, RING):
                    step(es.turns, q)
                with act.Fori(es.turns + 1, cs.loops) as i:
                    for q in range(RING):
                        step(i, q)

            @block.tensor
            def _(pe):
                pe.sem_inc(kd_ready, RING)
                ranks.start_tensor(pe)
                regs = [pe.alloc_register(f"{ph.name}_tile{u}") for u in range(PB)]

                def step(i, q):
                    pe.wait_ge(hot_ready, i * RING + (RING + q + 1))
                    pe.sem_inc(pe_on, 1)
                    pe.wait_ge(multiplied, i * RING + (q + 3))
                    pe.sem_inc(pe_on, 1)
                    tiles = load_tiles(pe, regs, cs, i, q)
                    for u in range(PB):
                        ins = pe.matmul(kd[q % 2][:, u * D:(u + 1) * D], hotT[:, q, u * P:(u + 1) * P], K[:, tiles[u], :], start=True, stop=True)
                    ins.then_inc(kd_ready, 1)
                turns(pe, step, ranks.tensor)

            @block.vector
            def _(v):
                v.sem_inc(multiplied, RING)
                v.sem_inc(reduced, 2)
                ranks.start_vector(v)

                def multiply(i, q):
                    v.wait_ge(got[q], i * (16 * PB) + 16 * PB)
                    v.sem_inc(dve_on, 1)
                    v.wait_ge(reduced, i * RING + (q + 1))
                    v.sem_inc(dve_on, 1)
                    v.wait_ge(kd_ready, i * RING + (RING + q + 1))
                    v.tensor_tensor(prod[:, q % 2, :], kd[q % 2][:], ring[:, q * PB:(q + 1) * PB, :].rearrange("p u d -> p (u d)"),
                                    ALU.mult).then_inc(multiplied, 1)

                def reduce(i, q):
                    v.wait_ge(multiplied, i * RING + (RING + q + 1))
                    v.sem_inc(dve_on, 1)
                    v.tensor_reduce(S[:, bass.ds(i * (TURN) + q * PB, PB), :].rearrange("p u h -> p (u h)"),
                                    prod[:, q % 2, :].rearrange("p (g d) -> p g d", d=D // H), AX.X, ALU.add).then_inc(reduced, 1)

                with v.Fori(0, es.turns) as i:
                    for q in range(RING):
                        multiply(i, q)
                        ranks.compare(v, i, q)
                        reduce(i, q)
                        ranks.place(v, i, q)
                with v.Fori(es.turns, cs.loops) as i:
                    for q in range(RING):
                        multiply(i, q)
                        reduce(i, q)
                v.wait_ge(reduced, cs.loops * RING + 2)
                ranks.end_vector(v)


def segment_max(nc, cs, name, S, heads, M, carry_dram, beside=None):
    B = P // heads
    NB = cs.pairs // B
    R = cs.pairs * heads
    with Phase(nc, name) as ph:
        T = ph.sb("T", [P, NB, P])
        fwd = ph.sb("fwd", [P, NB, P])
        keys_bwd = ph.sb("keys_bwd", [P, NB * (P + 2)])
        keys = keys_bwd[:].rearrange("p (b l) -> p b l", l=P + 2)
        bwd = keys_bwd[:, 0:NB * P].rearrange("p (b l) -> p b l", l=P)
        n_start = ph.sb("n_start", [P, NB, P])
        n_end = ph.sb("n_end", [P, NB, P])
        side = ph.sb("side", [P, 4, NB])
        lane0 = ph.sb("lane0", [P, NB])
        lane127 = ph.sb("lane127", [P, NB])
        sideT = ph.sb("sideT", [4 * NB, P])
        line = ph.sb("line", [1, 2, R + 2 * heads])
        cinT = ph.sb("cinT", [2 * NB, P])
        pt = [ph.psum(f"pt{b}", [P, P]) for b in range(4)]
        pc = ph.psum("pc", [P, P])
        keys_in, masked, turned, copied, sides, sideturned, side_out, side_stored, line_in, carried, cin_stored, cin_in, cinturned, joined, back, used, v_link = (
            ph.sem(k) for k in ("keys", "masked", "turned", "copied", "sides", "sideturned", "side_out", "side_stored", "line", "carried",
                                "cin_stored", "cin_in", "cinturned", "joined", "back", "used", "link"))

        def load_keys(eng, half):
            for b in range(half, NB, 2):
                eng.dma_start(keys[:, b, :], bass.AP(cs.keys_t, b * B * P, [[P, B], [0, heads], [1, P + 2]])).then_inc(keys_in, 16)

        flat = "p b l -> p (b l)"
        side_d, cin_d = carry_dram
        with nc.Block() as block:
            @block.sync
            def _(sp):
                load_keys(sp, 0)
                sp.wait_ge(side_out, 1)
                sp.dma_start(side_d, sideT[:]).then_inc(side_stored, 16)
                sp.wait_ge(side_stored, 16)
                sp.wait_ge(carried, 1)
                for k in range(2):
                    sp.dma_start(line[:, :, heads:R + heads],
                                 side_d[k * 2 * NB:(k + 1) * 2 * NB, :].rearrange("(a s b) r -> a s (b r)", a=1, s=2)).then_inc(line_in, 16)
                    sp.wait_ge(carried, k + 2)
                    sp.dma_start(cin_d[k * NB:(k + 1) * NB, :].rearrange("(a b) r -> a (b r)", a=1),
                                 line[:, 0, 2 * k * heads:2 * k * heads + R]).then_inc(cin_stored, 16)
                    sp.wait_ge(cin_stored, 16 * (k + 1))
                sp.wait_ge(cin_stored, 32)
                sp.dma_start(cinT[:], cin_d).then_inc(cin_in, 16)

            @block.tensor
            def _(pe):
                pe.wait_ge(masked, 1)
                for b in range(NB):
                    if b >= 4:
                        pe.wait_ge(copied, b - 3)
                    pe.transpose(pt[b % 4][:], S[:, b * B:(b + 1) * B, :].rearrange("p a h -> p (a h)"), cs.ident[:]).then_inc(turned, 1)
                pe.wait_ge(sides, 1)
                pe.transpose(pc[0:4 * NB, :], side[:].rearrange("p s b -> p (s b)"), cs.ident[:]).then_inc(sideturned, 1)
                pe.wait_ge(cin_in, 16)
                pe.wait_ge(side_out, 1)
                pe.transpose(pc[:, 0:2 * NB], cinT[:], cs.ident[0:2 * NB, 0:2 * NB]).then_inc(cinturned, 1)
                pe.wait_ge(joined, 1)
                pe.wait_ge(copied, NB)
                for b in range(NB):
                    if b >= 4:
                        pe.wait_ge(used, b - 3)
                    pe.transpose(pt[b % 4][:], fwd[:, b, :], cs.ident[:]).then_inc(back, 1)

            @block.scalar
            def _(act):
                load_keys(act, 1)
                for b in range(NB):
                    act.wait_ge(turned, b + 1)
                    nc.scalar.copy(T[:, b, :], pt[b % 4][:]).then_inc(copied, 1)
                act.wait_ge(sideturned, 1)
                nc.scalar.copy(sideT[:], pc[0:4 * NB, :]).then_inc(side_out, 1)
                for b in range(NB):
                    act.wait_ge(back, b + 1)
                    nc.scalar.copy(M[:, b * B:(b + 1) * B, :].rearrange("p a h -> p (a h)"), pt[b % 4][:]).then_inc(used, 1)
                act.wait_ge(used, NB)

            @block.vector
            def _(v):
                v.tensor_tensor(S[:], S[:], cs.neg_big[:].unsqueeze(2).to_broadcast([P, cs.pairs, heads]), ALU.add).then_inc(masked, 1)
                link = chain(v, v_link)
                v.wait_ge(keys_in, 16 * NB)
                link(v.tensor_tensor(n_start[:], keys[:, :, 0:P], keys[:, :, 1:P + 1], ALU.not_equal))
                link(v.tensor_tensor(n_end[:], keys[:, :, 2:P + 2], keys[:, :, 1:P + 1], ALU.not_equal))
                link(v.tensor_scalar(n_start[:], n_start[:], -BIG, None, ALU.mult))
                link(v.tensor_scalar(n_end[:], n_end[:], -BIG, None, ALU.mult))
                link(v.tensor_copy(lane0[:], n_start[:, :, 0]))
                link(v.tensor_copy(lane127[:], n_end[:, :, P - 1]))
                link(v.tensor_reduce(side[:, 1, :], n_start[:], AX.X, ALU.min))
                link(v.tensor_reduce(side[:, 3, :], n_end[:], AX.X, ALU.min))
                link(v.memset(n_start[:, :, 0], -BIG))
                link(v.memset(n_end[:, :, P - 1], -BIG))
                v.wait_ge(copied, NB)

                def scans():
                    link(v.tensor_tensor_scan(fwd[:].rearrange(flat), n_start[:].rearrange(flat), T[:].rearrange(flat),
                                              -BIG, ALU.add, ALU.max))
                    link(v.tensor_tensor_scan(bwd[:].rearrange(flat)[:, ::-1], n_end[:].rearrange(flat)[:, ::-1], T[:].rearrange(flat)[:, ::-1],
                                              -BIG, ALU.add, ALU.max))
                scans()
                link(v.tensor_copy(side[:, 0, :], fwd[:, :, P - 1]))
                v.tensor_copy(side[:, 2, :], bwd[:, :, 0]).then_inc(sides, 1)
                link(v.memset(line[:, :, 0:heads], -BIG))
                link(v.memset(line[:, :, R + heads:R + 2 * heads], -BIG))
                v.sem_inc(carried, 1)
                if beside:
                    beside(v, link)
                for k in range(2):
                    v.wait_ge(line_in, 16 * (k + 1))
                    way = 1 - 2 * k
                    for h in range(heads):
                        of = lambda r: line[:, r, heads:R + heads].rearrange("a (r h) -> a h r", h=heads)[:, h, ::way]
                        link(v.tensor_tensor_scan(of(0), of(1), of(0), -BIG, ALU.add, ALU.max))
                    v.sem_inc(carried, 1)
                v.wait_ge(cinturned, 1)
                link(v.tensor_tensor(lane0[:], lane0[:], pc[:, 0:NB], ALU.add))
                link(v.tensor_tensor(lane127[:], lane127[:], pc[:, NB:2 * NB], ALU.add))
                link(v.tensor_tensor(T[:, :, 0], T[:, :, 0], lane0[:], ALU.max))
                link(v.tensor_tensor(T[:, :, P - 1], T[:, :, P - 1], lane127[:], ALU.max))
                scans()
                v.tensor_tensor(fwd[:], fwd[:], bwd[:], ALU.max).then_inc(joined, 1)


def edge_weights(nc, name, S, M, Wt):
    with Phase(nc, name) as ph:
        shifted = ph.sem("shifted")
        raised = ph.sem("raised")
        with nc.Block() as block:
            @block.vector
            def _(v):
                v.tensor_tensor(S[:], S[:], M[:], ALU.subtract).then_inc(shifted, 1)

            @block.scalar
            def _(act):
                act.wait_ge(shifted, 1)
                nc.scalar.activation(Wt, S[:], ACT.Exp).then_inc(raised, 1)
                act.wait_ge(raised, 1)


def lane_hots(nc, act, cs, hot, dist, hot_free, hot_ready, dist_ready, act_on):
    with act.Fori(0, cs.loops) as i:
        for q in range(RING):
            act.wait_ge(hot_free, i * RING + (q + 1))
            act.sem_inc(act_on, 1)
            for u in range(PB):
                p = i * (TURN) + (q * PB + u)
                ins = nc.scalar.activation(dist[:, q, u, :], cs.count_row[:, 0:TN], ACT.Abs, bias=cs.neg_local[:, bass.ds(p, 1)])
            ins.then_inc(dist_ready, 1)
            act.wait_ge(dist_ready, i * RING + (q + 1))
            nc.scalar.activation(hot[:, q, :, :], dist[:, q, :, :], ACT.Relu, scale=-1.0, bias=1.0).then_inc(hot_ready, 1)


def weigh_values(nc, cs, v_dram, Wt, acc):
    C = D + H + 1
    with Phase(nc, "value") as ph:
        ring = ph.sb("ring", [P, TURN, D])
        idx = ph.sb("idx", [P, 2, TURN], I32)
        hot = ph.sb("hot", [P, RING, PB, TN])
        dist = ph.sb("dist", [P, RING, PB, TN])
        wv = ph.sb("wv", [P, RING, PB, D])
        part = [ph.psum(f"part{u}", [TN, 512]) for u in range(2 * PB)]
        idx_ready, hot_ready, weighed, summed, added, dist_ready, pool_on, act_on, pe_on, dve_on = (
            ph.sem(k) for k in ("idx", "hot", "weighed", "summed", "added", "dist", "pool_on", "act_on", "pe_on", "dve_on"))
        cleared = ph.sem("cleared")
        got = [ph.sem(f"got{q}") for q in range(RING)]
        HB = PB // 2
        with nc.Block() as block:
            @block.gpsimd
            def _(g):
                gather_pairs(g, cs, v_dram, ring, idx, idx_ready, weighed, got, pool_on)

            @block.scalar
            def _(act):
                lane_hots(nc, act, cs, hot, dist, summed, hot_ready, dist_ready, act_on)

            @block.vector
            def _(v):
                v.memset(acc[:], 0.0).then_inc(cleared, 1)
                v.wait_ge(cleared, 1)
                v.sem_inc(weighed, RING)
                v.sem_inc(added, 2 * PB)
                regs = [v.alloc_register(f"{ph.name}_vtile{u}") for u in range(PB)]

                def weigh(i, q):
                    v.wait_ge(got[q], i * (16 * PB) + 16 * PB)
                    v.sem_inc(dve_on, 1)
                    v.wait_ge(summed, i * RING + (q + 1))
                    v.sem_inc(dve_on, 1)
                    w = Wt[:, bass.ds(i * TURN + q * PB, PB), 0:H]
                    v.tensor_tensor(wv[:, q, :, :].rearrange("p u (h d) -> p u h d", h=H),
                                    ring[:, q * PB:(q + 1) * PB, :].rearrange("p u (h d) -> p u h d", h=H),
                                    w.unsqueeze(3).to_broadcast([P, PB, H, D // H]), ALU.mult).then_inc(weighed, 1)

                def add(i, q):
                    tiles = load_tiles(v, regs, cs, i, q)
                    v.wait_ge(summed, i * RING + (RING + q + 1))
                    v.sem_inc(dve_on, 1)
                    for u in range(PB):
                        v.wait_ge(added, i * TURN + (q * PB + u + 2 * PB))
                        v.sem_inc(dve_on, 1)
                        sum_ = acc[:, tiles[u], :]
                        v.tensor_tensor(sum_, sum_, part[(q % 2) * PB + u][:, 0:C], ALU.add).then_inc(added, 1)

                for q in range(RING):
                    weigh(0, q)
                    if q:
                        add(0, q - 1)
                with v.Fori(1, cs.loops) as i:
                    for q in range(RING):
                        weigh(i, q)
                        add(i if q else i - 1, (q - 1) % RING)
                add(cs.loops - 1, RING - 1)
                v.wait_ge(added, cs.pairs + 2 * PB)

            @block.tensor
            def _(pe):
                pe.sem_inc(summed, RING)
                with pe.Fori(0, cs.loops) as i:
                    for q in range(RING):
                        pe.wait_ge(hot_ready, i * RING + (q + 1))
                        pe.sem_inc(pe_on, 1)
                        pe.wait_ge(weighed, i * RING + (RING + q + 1))
                        pe.sem_inc(pe_on, 1)
                        pe.wait_ge(added, i * (TURN) + (q * PB + PB))
                        pe.sem_inc(pe_on, 1)
                        for u in range(PB):
                            p = i * (TURN) + (q * PB + u)
                            out = part[(q % 2) * PB + u]
                            pe.matmul(out[:, 0:D], hot[:, q, u, :], wv[:, q, u, :], start=True, stop=True)
                            ins = pe.matmul(out[:, D:C], hot[:, q, u, :], Wt[:, p, :], start=True, stop=True)
                        ins.then_inc(summed, 1)


def neighbour_sums(nc, name, cs, table, width, acc, other=None, **edges):
    per_bank = 512 // width
    with Phase(nc, name) as ph:
        ring = ph.sb("ring", [P, TURN, width])
        idx = ph.sb("idx", [P, 2, TURN], I32)
        hot = ph.sb("hot", [P, RING, PB, TN])
        dist = ph.sb("dist", [P, RING, PB, TN])
        zero = ph.sb("zero", [1, 512])
        idx_ready, hot_ready, summed, dist_ready, zeroed, pool_on, act_on, pe_on = (
            ph.sem(k) for k in ("idx", "hot", "summed", "dist", "zeroed", "pool_on", "act_on", "pe_on"))
        got = [ph.sem(f"got{q}") for q in range(RING)]
        tables = IndexTables(ph, nc, other, **edges) if other else None
        with nc.Block() as block:
            @block.vector
            def _(v):
                v.memset(zero[:], 0.0).then_inc(zeroed, 1)
                if tables:
                    tables.vector(v)

            @block.sync
            def _(sp):
                if tables:
                    tables.sync(sp)

            @block.gpsimd
            def _(g):
                gather_pairs(g, cs, table, ring, idx, idx_ready, summed, got, pool_on)

            @block.scalar
            def _(act):
                lane_hots(nc, act, cs, hot, dist, summed, hot_ready, dist_ready, act_on)

            @block.tensor
            def _(pe):
                pe.wait_ge(zeroed, 1)
                for b in range((NT + per_bank - 1) // per_bank):
                    pe.matmul(acc[:, b * 512:(b + 1) * 512], zero[:, 0:TN], zero[:], start=True, stop=True)
                pe.sem_inc(summed, RING)
                regs = [pe.alloc_register(f"{ph.name}_tile{u}") for u in range(PB)]

                def turns(low, high):
                    with pe.Fori(low, high) as i:
                        for q in range(RING):
                            pe.wait_ge(hot_ready, i * RING + (q + 1))
                            pe.sem_inc(pe_on, 1)
                            pe.wait_ge(got[q], i * (16 * PB) + 16 * PB)
                            pe.sem_inc(pe_on, 1)
                            tiles = load_tiles(pe, regs, cs, i, q)
                            for u in range(PB):
                                p = i * (TURN) + (q * PB + u)
                                tile = tiles[u]
                                ins = pe.matmul(acc[:, bass.ds(tile * width, width)], hot[:, q, u, :], ring[:, q * PB + u, :],
                                                start=False, stop=True, skip_group_check=True)
                            ins.then_inc(summed, 1)

                if tables:
                    tables.tensor[0](pe)
                    for step, (low, high) in enumerate(((0, 1), (1, 4), (4, 6))):
                        turns(low, high)
                        tables.tensor[step + 1](pe)
                turns(6 if tables else 0, cs.loops)
                pe.wait_ge(summed, cs.loops * RING + RING)


def experts(nc, name, cs, UT, Y, gates, w1, b1, w2, b2, n_experts, func, parts=None):
    assert parts is None or n_experts == 2
    F = 512
    FT = F // P
    CT = 5
    CW = CT * TN
    halves = [(0, 313), (313, CW)]
    with Phase(nc, name) as ph:
        W1 = ph.sb("W1", [P, 2, 2, F])
        W2 = ph.sb("W2", [P, 2, FT, D])
        B2 = ph.sb("B2", [TN, 2, D])
        brow = ph.sb("brow", [n_experts * FT, P])
        bcol = ph.sb("bcol", [P, n_experts * FT])
        hidden = ph.sb("hidden", [P, 2, FT, CW])
        plus = ph.sb("plus", [TN, 2, D])
        hp = [ph.psum(f"hp{k}", [P, 2, 512]) for k in range(2)]
        yp = [ph.psum(f"yp{k}", [TN, D]) for k in range(2)]
        bp = ph.psum("bp", [P, n_experts * FT])
        b_in, b_turned, b_ready, up, acted, down, added, biased, act_on, sp_on, dve_on = (
            ph.sem(k) for k in ("b_in", "b_turned", "b_ready", "up", "acted", "down", "added", "biased", "act_on", "sp_on", "dve_on"))
        w_in = [ph.sem(f"w_in{k}") for k in range(2)]
        taken = ph.sem("taken")
        NW = 3 if b2 is not None else 2
        C = 50
        with nc.Block() as block:
            @block.sync
            def _(sp):
                sp.dma_start(brow[:], b1.rearrange("e (f p) -> (e f) p", p=P)).then_inc(b_in, 16)
                with sp.Fori(0, n_experts // 2) as i:
                    for k in range(2):
                        sp.wait_ge(down, i * 50 + (25 * k + 25))
                        sp.sem_inc(sp_on, 1)
                        if b2 is not None:
                            sp.wait_ge(biased, i * 50 + (25 * k + 25))
                            sp.sem_inc(sp_on, 1)
                        e = i * 2 + k
                        sp.dma_start(W1[:, k, :, :], w1[bass.ds(e, 1), :, :].rearrange("e (c p) f -> p (e c) f", p=P)).then_inc(w_in[k], 16)
                        sp.dma_start(W2[:, k, :, :], w2[bass.ds(e, 1), :, :].rearrange("e (c p) d -> p (e c) d", p=P)).then_inc(w_in[k], 16)
                        if b2 is not None:
                            sp.dma_start(B2[:, k, :], b2[bass.ds(e, 1), :].rearrange("e d -> (e d)").partition_broadcast(TN)).then_inc(w_in[k], 16)

            @block.tensor
            def _(pe):
                pe.wait_ge(b_in, 16)
                pe.transpose(bp[:], brow[:], cs.ident[0:n_experts * FT, 0:n_experts * FT]).then_inc(b_turned, 1)
                pe.sem_inc(down, C)

                def up_products(i, n):
                    k, c = n // 5, n % 5
                    if c == 0:
                        pe.wait_ge(w_in[k], i * (16 * NW) + 16 * NW)
                        pe.sem_inc(sp_on, 1)
                    for f in range(FT):
                        pe.wait_ge(acted, i * 40 + (n * FT + f + 1))
                        for (lo, hi) in halves:
                            for kk in range(2):
                                ins = pe.matmul(hp[f % 2][:, lo // 313, 0:hi - lo], W1[:, k, kk, f * P:(f + 1) * P],
                                                UT[:, kk, c * CW + lo:c * CW + hi], start=(kk == 0), stop=(kk == 1))
                        ins.then_inc(up, 1)

                def down_products(i, n):
                    pe.wait_ge(acted, i * 40 + (n * FT + FT + 2))
                    for t in range(CT):
                        m = n * CT + t
                        pe.wait_ge(added, i * 50 + (m + 1))
                        for f in range(FT):
                            ins = pe.matmul(yp[m % 2][:], hidden[:, n % 2, f, t * TN:(t + 1) * TN], W2[:, n // 5, f, :],
                                            start=(f == 0), stop=(f == FT - 1))
                        ins.then_inc(down, 1)

                up_products(0, 0)
                last = n_experts // 2 - 1
                if last:
                    with pe.Fori(0, last) as i:
                        for n in range(10):
                            up_products(i + (n + 1) // 10, (n + 1) % 10)
                            down_products(i, n)
                for n in range(10):
                    if n < 9:
                        up_products(last, n + 1)
                    down_products(last, n)

            @block.scalar
            def _(act):
                act.sem_inc(acted, 2)
                with act.Fori(0, n_experts // 2) as i:
                    for n in range(10):
                        act.wait_ge(down, i * 50 + (5 * n + C - 5))
                        act.sem_inc(act_on, 1)
                        if n == 0:
                            act.wait_ge(b_ready, 1)
                        for f in range(FT):
                            act.wait_ge(up, i * 40 + (n * FT + f + 1))
                            act.sem_inc(act_on, 1)
                            bias = bcol[:, bass.ds(i * (2 * FT) + ((n // 5) * FT + f), 1)]
                            for (lo, hi) in halves:
                                ins = nc.scalar.activation(hidden[:, n % 2, f, lo:hi], hp[f % 2][:, lo // 313, 0:hi - lo], func, bias=bias)
                            ins.then_inc(acted, 1)

            @block.vector
            def _(v):
                v.wait_ge(b_turned, 1)
                v.tensor_copy(bcol[:], bp[:]).then_inc(b_ready, 1)
                v.sem_inc(added, 2)
                v.sem_inc(biased, C)
                with v.Fori(0, n_experts // 2) as i:
                    for m in range(50):
                        v.wait_ge(down, i * 50 + (m + 1 + C))
                        k, t = m // 25, m % 25
                        y = yp[m % 2][:]
                        if b2 is not None:
                            v.tensor_tensor(plus[:, m % 2, :], y, B2[:, k, :], ALU.add).then_inc(biased, 1)
                            v.wait_ge(biased, i * 50 + (m + 1 + C))
                            y = plus[:, m % 2, :]
                        v.sem_inc(dve_on, 1)
                        v.scalar_tensor_tensor(out=Y[:, t, :], in0=y, scalar=gates[:, t, bass.ds(i * 2 + k, 1)], in1=Y[:, t, :],
                                               op0=ALU.mult, op1=ALU.add).then_inc(added, 1)
                        if parts is not None and m > 25:
                            v.wait_ge(added, i * 50 + (m + 2))
                            v.sem_inc(dve_on, 1)
                            v.bn_stats(out=parts[:, t - 1, :], in_=Y[:, t - 1, :]).then_inc(taken, 1)
                v.wait_ge(added, n_experts * 25 + 2)
                if parts is not None:
                    v.bn_stats(out=parts[:, NT - 1, :], in_=Y[:, NT - 1, :]).then_inc(taken, 1)
                    v.wait_ge(taken, NT)


N_EXP, F_EXP = 16, 512
SLOT_TILES = (2 * N + N_EXP * (P - 1)) // P
X_TILES = SLOT_TILES + 3
OWNERS = SLOT_TILES + 4


def start_loads(nc, pairs, sem):
    with nc.Block() as block:
        @block.scalar
        def _(act):
            for dest, source in pairs:
                act.dma_start(dest, source).then_inc(sem, 16)


def wait_loads(nc, sem, count):
    with nc.Block() as block:
        @block.sync
        def _(sp):
            sp.wait_ge(sem, 16 * count)


def route(nc, cs, hots, pos, expert_of):
    W = NT * N_EXP
    with Phase(nc, "route") as ph:
        upper = ph.sb("upper", [TN, TN])
        both = ph.sb("both", [TN, NT, N_EXP])
        tot = ph.sb("tot", [TN, N_EXP, NT])
        keep = ph.sb("keep", [TN, N_EXP, NT])
        incl = ph.sb("incl", [TN, N_EXP, NT])
        tiles_i = ph.sb("tiles_i", [TN, N_EXP], I32)
        tiles, upto, zeros = (ph.sb(k, [TN, N_EXP]) for k in ("tiles", "upto", "zeros"))
        place = ph.sb("place", [TN, NT, N_EXP])
        pick = ph.sb("pick", [TN, NT, N_EXP])
        pos_f = ph.sb("pos_f", [TN, NT, 2])
        owner = ph.sb("owner", [1, OWNERS, N_EXP])
        owner_f = ph.sb("owner_f", [1, OWNERS])
        pw, pt = ph.psum("pw", [TN, 512]), ph.psum("pt", [TN, 512])
        made, ready, summed, link_s = (ph.sem(k) for k in ("made", "ready", "summed", "link"))
        by_expert = "p t e -> p e t"
        with nc.Block() as block:
            @block.gpsimd
            def _(g):
                link = chain(g, made)
                link(g.memset(upper[:], 1.0))
                link(g.affine_select(out=upper[:], in_=upper[:], compare_op=ALU.is_gt, fill=0.0, base=0,
                                     pattern=[[1, TN]], channel_multiplier=-1))

            @block.tensor
            def _(pe):
                pe.wait_ge(made, 2)
                pe.wait_ge(ready, 1)
                flat = both[:].rearrange("p t e -> p (t e)")
                pe.matmul(pw[:, 0:W], upper[:], flat, start=True, stop=True)
                pe.matmul(pt[:, 0:W], cs.ones[0:TN, 0:TN], flat, start=True, stop=True).then_inc(summed, 1)

            @block.vector
            def _(v):
                link = chain(v, link_s)
                v.tensor_tensor(both[:], hots[:, :, 0, :], hots[:, :, 1, :], ALU.add).then_inc(ready, 1)
                link(v.memset(keep[:], 1.0))
                link(v.memset(keep[:, :, 0], 0.0))
                link(v.memset(zeros[:], 0.0))
                v.wait_ge(summed, 1)
                tot_p = pt[:, 0:W].rearrange("p (t e) -> p t e", e=N_EXP).rearrange(by_expert)
                link(v.tensor_copy(tot[:], tot_p))
                link(v.tensor_tensor_scan(incl[:].rearrange("p e t -> p (e t)"), keep[:].rearrange("p e t -> p (e t)"),
                                          tot[:].rearrange("p e t -> p (e t)"), 0.0, ALU.mult, ALU.add))
                link(v.tensor_scalar(tiles_i[:], incl[:, :, NT - 1], float(P - 1), None, ALU.add))
                link(v.tensor_scalar(tiles_i[:], tiles_i[:], 7, None, ALU.arith_shift_right))
                link(v.tensor_copy(tiles[:], tiles_i[:]))
                link(v.tensor_tensor_scan(upto[:], zeros[:], tiles[:], 0.0, ALU.add, ALU.add))
                link(v.tensor_tensor(upto[:], upto[:], tiles[:], ALU.subtract))
                link(v.tensor_tensor(incl[:], incl[:], tot[:], ALU.subtract))
                link(v.tensor_tensor(place[:], pw[:, 0:W].rearrange("p (t e) -> p t e", e=N_EXP), incl[:].rearrange("p e t -> p t e"),
                                     ALU.add))
                link(v.scalar_tensor_tensor(out=tiles[:], in0=upto[:], scalar=float(P), in1=zeros[:], op0=ALU.mult, op1=ALU.add))
                link(v.tensor_tensor(place[:], place[:], tiles[:].unsqueeze(1).to_broadcast([TN, NT, N_EXP]), ALU.add))
                for k in range(2):
                    link(v.tensor_tensor(pick[:], place[:], hots[:, :, k, :], ALU.mult))
                    link(v.tensor_reduce(pos_f[:, :, k], pick[:], AX.X, ALU.add))
                link(v.tensor_copy(pos[:], pos_f[:]))
                link(v.tensor_tensor(owner[:], upto[0:1, :].unsqueeze(1).to_broadcast([1, OWNERS, N_EXP]),
                                     cs.count_row[0:1, 0:OWNERS].unsqueeze(2).to_broadcast([1, OWNERS, N_EXP]), ALU.is_le))
                link(v.tensor_reduce(owner_f[:], owner[:], AX.X, ALU.add))
                link(v.tensor_scalar(owner_f[:], owner_f[:], -1.0, None, ALU.add))
                link(v.tensor_copy(expert_of[:], owner_f[:]))


def send_rows(nc, rows, pos, x_slots, X, beta):
    with Phase(nc, "send") as ph:
        ring = ph.sb("ring", [TN, 5, D])
        at = ph.sb("at", [TN, 5, 2], I32)
        ready, pool_on, dve_on, sp_on, beta_added = (ph.sem(k) for k in ("ready", "pool_on", "dve_on", "sp_on", "beta_added"))
        row_in = [ph.sem(f"row_in{s}") for s in range(5)]
        sent = [ph.sem(f"sent{s}") for s in range(5)]
        with nc.Block() as block:
            @block.gpsimd
            def _(g):
                with g.Fori(0, 5) as i:
                    for s in range(5):
                        g.wait_ge(ready, i * 5 + (s + 1))
                        g.sem_inc(pool_on, 1)
                        g.wait_ge(row_in[s], i * 16 + 16)
                        g.sem_inc(pool_on, 1)
                        for k in range(2):
                            g.indirect_dma_start(out=x_slots, out_offset=bass.IndirectOffsetOnAxis(ap=at[:, s, k:k + 1], axis=0),
                                                 in_=ring[:, s, :], in_offset=None).then_inc(sent[s], 16)
                for s in range(5):
                    g.wait_ge(sent[s], 5 * 32)

            @block.sync
            def _(sp):
                def load(i, first):
                    for s in range(5):
                        if not first:
                            sp.wait_ge(sent[s], i * 32)
                            sp.sem_inc(sp_on, 1)
                        sp.dma_start(ring[:, s, :], rows[bass.ds((i * 5 + s) * TN, TN), :]).then_inc(row_in[s], 16)
                load(0, True)
                with sp.Fori(1, 5) as i:
                    load(i, False)

            @block.vector
            def _(v):
                def fill(i, first):
                    for s in range(5):
                        if not first:
                            v.wait_ge(sent[s], i * 32)
                            v.sem_inc(dve_on, 1)
                        v.tensor_copy(at[:, s, :], pos[:, i * 5 + s, :]).then_inc(ready, 1)
                fill(0, True)
                v.tensor_tensor(X[:], X[:], beta.unsqueeze(1).to_broadcast([TN, NT, D]), ALU.add).then_inc(beta_added, 1)
                with v.Fori(1, 5) as i:
                    fill(i, False)
                v.wait_ge(beta_added, 1)


def slot_experts(nc, cs, x_slots, y_slots, W1, W2, b1, b2, expert_of, up_in, down_in, es, joined):
    FT = F_EXP // P
    with Phase(nc, "slot") as ph:
        x = ph.sb("x", [P, 4, D])
        xT = ph.sb("xT", [P, 2, 2, P])
        h = ph.sb("h", [P, 2, F_EXP])
        hT = ph.sb("hT", [P, 2, FT, P])
        y = ph.sb("y", [P, 4, D])
        B2 = ph.sb("B2", [P, 4, D])
        brow = ph.sb("brow", [N_EXP * FT, P])
        bcol = ph.sb("bcol", [P, N_EXP * FT])
        x_ps = [ph.psum(f"x_ps{k}", [P, 4, P]) for k in range(2)]
        h_ps = [ph.psum(f"h_ps{k}", [P, F_EXP]) for k in range(2)]
        hT_ps = [ph.psum(f"hT_ps{k}", [P, FT, P]) for k in range(2)]
        y_ps = [ph.psum(f"y_ps{k}", [P, 512]) for k in range(2)]
        b_in, b_turned, b_ready, x_turned, x_copied, up, h_copied, h_turned, relued, down, y_ready, pe_on, act_on, dve_on, sp_on, pool_on = (
            ph.sem(k) for k in ("b_in", "b_turned", "b_ready", "x_turned", "x_copied", "up", "h_copied", "h_turned", "relued", "down",
                                "y_ready", "pe_on", "act_on", "dve_on", "sp_on", "pool_on"))
        x_in = [ph.sem(f"x_in{q}") for q in range(4)]
        y_out = [ph.sem(f"y_out{q}") for q in range(4)]
        bias_in = [ph.sem(f"bias_in{q}") for q in range(4)]
        b2_line = b2.rearrange("e d -> (e d)")
        at = ph.sb("at", [P, RING, PB], I32)
        payload = ph.sb("payload", [P, RING, PB, 2], I32)
        edges_copied = ph.sem("edges_copied")
        edges_out = [ph.sem(f"edges_out{q}") for q in range(RING)]
        TURNS = SLOT_TILES // 4

        def store_y(sp, i, q):
            sp.dma_start(y_slots[bass.ds(i * (4 * P) + q * P, P), :], y[:, q, :]).then_inc(y_out[q], 16)

        def load_x(sp, i, q):
            sp.dma_start(x[:, q, :], x_slots[bass.ds(i * (4 * P) + q * P, P), :]).then_inc(x_in[q], 16)

        with nc.Block() as block:
            @block.sync
            def _(sp):
                sp.dma_start(brow[:], b1.rearrange("e (f p) -> (e f) p", p=P)).then_inc(b_in, 16)
                regs = [sp.alloc_register(f"{ph.name}_sexpert{u}") for u in range(4)]

                def experts_of(i):
                    sp.load(regs, expert_of[0:1, bass.ds(i * 4, 4)])
                    return [sp.snap(r, min_val=0, max_val=N_EXP - 1) for r in regs]

                def load_bias(q, e):
                    sp.dma_start(B2[:, q, :], b2_line[bass.ds(e * D, D)].partition_broadcast(P)).then_inc(bias_in[q], 16)

                e = experts_of(0)
                for q in range(4):
                    load_x(sp, 0, q)
                    load_bias(q, e[q])
                with sp.Fori(1, TURNS) as i:
                    e = experts_of(i)
                    for q in range(4):
                        sp.wait_ge(x_turned, i * 4 + (q - 3))
                        sp.sem_inc(sp_on, 1)
                        load_x(sp, i, q)
                        sp.wait_ge(y_ready, i * 4 + (q - 1))
                        sp.sem_inc(sp_on, 1)
                        store_y(sp, i - 1, q)
                        load_bias(q, e[q])
                for q in range(3):
                    sp.wait_ge(x_turned, SLOT_TILES + q - 3)
                    load_x(sp, TURNS, q)
                for q in range(4):
                    sp.wait_ge(y_ready, SLOT_TILES + q - 1)
                    store_y(sp, TURNS - 1, q)
                for q in range(4):
                    sp.wait_ge(y_out[q], 16 * TURNS)

            @block.tensor
            def _(pe):
                regs = [pe.alloc_register(f"{ph.name}_expert{u}") for u in range(8)]

                def turn_x(i, k):
                    pe.wait_ge(x_in[k % 4], (i + k // 4) * 16 + 16)
                    pe.sem_inc(pe_on, 1)
                    pe.wait_ge(x_copied, i * 4 + (k + 1))
                    pe.sem_inc(pe_on, 1)
                    for c in range(2):
                        ins = pe.transpose(x_ps[k % 2][:, c, :], x[:, k % 4, c * P:(c + 1) * P], cs.ident[:])
                    ins.then_inc(x_turned, 1)

                def layer1(i, k, e):
                    pe.wait_ge(x_copied, i * 4 + (k + 3))
                    pe.sem_inc(pe_on, 1)
                    pe.wait_ge(h_copied, i * 4 + (k + 1))
                    pe.sem_inc(pe_on, 1)
                    for c in range(2):
                        ins = pe.matmul(h_ps[k % 2][:], xT[:, k % 2, c, :], W1[:, e, c, :], start=(c == 0), stop=(c == 1))
                    ins.then_inc(up, 1)

                def turn_h(i, k):
                    pe.wait_ge(h_copied, i * 4 + (k + 3))
                    pe.sem_inc(pe_on, 1)
                    pe.wait_ge(relued, i * 4 + (k + 1))
                    pe.sem_inc(pe_on, 1)
                    for f in range(FT):
                        ins = pe.transpose(hT_ps[k % 2][:, f, :], h[:, k % 2, f * P:(f + 1) * P], cs.ident[:])
                    ins.then_inc(h_turned, 1)

                def layer2(i, k, e):
                    pe.wait_ge(relued, i * 4 + (k + 3))
                    pe.sem_inc(pe_on, 1)
                    pe.wait_ge(y_ready, i * 4 + (k + 1))
                    pe.sem_inc(pe_on, 1)
                    for f in range(FT):
                        ins = pe.matmul(y_ps[k % 2][:, 0:D], hT[:, k % 2, f, :], W2[:, e, f, :], start=(f == 0), stop=(f == FT - 1))
                    ins.then_inc(down, 1)

                def experts_of(i):
                    pe.load(regs[0:4], expert_of[0:1, bass.ds(i * 4, 4)])
                    pe.load(regs[4:8], expert_of[0:1, bass.ds(i * 4 + 4, 4)])
                    return [pe.snap(r, min_val=0, max_val=N_EXP - 1) for r in regs]

                pe.wait_ge(b_in, 16)
                pe.transpose(h_ps[0][:, 0:N_EXP * FT], brow[:], cs.ident[0:N_EXP * FT, 0:N_EXP * FT]).then_inc(b_turned, 1)
                pe.wait_ge(b_ready, 1)
                pe.sem_inc(up, 2)
                pe.sem_inc(h_turned, 2)
                pe.sem_inc(down, 2)
                pe.wait_ge(up_in, 16)
                pe.wait_ge(down_in, 16)
                e = experts_of(0)
                for k in range(3):
                    turn_x(0, k)
                for k in range(2):
                    layer1(0, k, e[k])
                turn_h(0, 0)
                with pe.Fori(0, TURNS) as i:
                    e = experts_of(i)
                    for k in range(4):
                        layer1(i, k + 2, e[k + 2])
                        turn_x(i, k + 3)
                        turn_h(i, k + 1)
                        layer2(i, k, e[k])

            @block.scalar
            def _(act):
                regs = [act.alloc_register(f"{ph.name}_aexpert{u}") for u in range(8)]

                def copy_x(i, k):
                    act.wait_ge(x_turned, i * 4 + (k + 1))
                    act.sem_inc(act_on, 1)
                    act.wait_ge(up, i * 4 + (k + 1))
                    act.sem_inc(act_on, 1)
                    nc.scalar.copy(xT[:, k % 2, :, :], x_ps[k % 2][:, 0:2, :]).then_inc(x_copied, 1)

                def relu(i, k, e):
                    act.wait_ge(h_turned, i * 4 + (k + 3))
                    act.sem_inc(act_on, 1)
                    act.wait_ge(down, i * 4 + (k + 1))
                    act.sem_inc(act_on, 1)
                    for f in range(FT):
                        ins = nc.scalar.activation(hT[:, k % 2, f, :], hT_ps[k % 2][:, f, :], ACT.Relu, bias=bcol[:, bass.ds(e * FT + f, 1)])
                    ins.then_inc(relued, 1)

                def experts_of(i):
                    act.load(regs[0:4], expert_of[0:1, bass.ds(i * 4, 4)])
                    act.load(regs[4:8], expert_of[0:1, bass.ds(i * 4 + 4, 4)])
                    return [act.snap(r, min_val=0, max_val=N_EXP - 1) for r in regs]

                act.wait_ge(b_ready, 1)
                act.sem_inc(x_copied, 2)
                act.sem_inc(relued, 2)
                e = experts_of(0)
                for k in range(3):
                    copy_x(0, k)
                relu(0, 0, e[0])
                with act.Fori(0, TURNS) as i:
                    e = experts_of(i)
                    for k in range(4):
                        copy_x(i, k + 3)
                        relu(i, k + 1, e[k + 1])

            @block.vector
            def _(v):
                def copy_h(i, k):
                    v.wait_ge(up, i * 4 + (k + 3))
                    v.sem_inc(dve_on, 1)
                    v.wait_ge(h_turned, i * 4 + (k + 1))
                    v.sem_inc(dve_on, 1)
                    v.tensor_copy(h[:, k % 2, :], h_ps[k % 2][:]).then_inc(h_copied, 1)

                def turn(i, first):
                    for k in range(4):
                        copy_h(i, k + 2)
                        v.wait_ge(down, i * 4 + (k + 3))
                        v.sem_inc(dve_on, 1)
                        v.wait_ge(bias_in[k], i * 16 + 16)
                        v.sem_inc(dve_on, 1)
                        if not first:
                            v.wait_ge(y_out[k], i * 16)
                            v.sem_inc(dve_on, 1)
                        v.tensor_tensor(y[:, k, :], y_ps[k % 2][:, 0:D], B2[:, k, :], ALU.add).then_inc(y_ready, 1)

                v.wait_ge(b_turned, 1)
                v.tensor_copy(bcol[:], h_ps[0][:, 0:N_EXP * FT]).then_inc(b_ready, 1)
                v.sem_inc(h_copied, 2)
                v.sem_inc(y_ready, 2)
                for k in range(2):
                    copy_h(0, k)
                turn(0, True)
                with v.Fori(1, TURNS) as i:
                    turn(i, False)

            @block.gpsimd
            def _(g):
                scatter_edges(g, es, joined, at, payload, edges_out, edges_copied, pool_on)


def collect_rows(nc, y_slots, pos, weights, Y, parts):
    with Phase(nc, "coll") as ph:
        ring = ph.sb("ring", [TN, 10, D])
        at = ph.sb("at", [TN, 5, 2], I32)
        at_ready, added, half, pool_on, dve_on, taken = (ph.sem(k) for k in ("at", "added", "half", "pool_on", "dve_on", "taken"))
        got = [ph.sem(f"got{s}") for s in range(5)]
        with nc.Block() as block:
            @block.gpsimd
            def _(g):
                with g.Fori(0, 5) as i:
                    for s in range(5):
                        g.wait_ge(added, i * 5 + (s + 1))
                        g.sem_inc(pool_on, 1)
                        g.tensor_copy(at[:, s, :], pos[:, i * 5 + s, :]).then_inc(at_ready, 1)
                        g.wait_ge(at_ready, i * 5 + (s + 1))
                        g.sem_inc(pool_on, 1)
                        for k in range(2):
                            g.indirect_dma_start(out=ring[:, 2 * s + k, :], out_offset=None, in_=y_slots,
                                                 in_offset=bass.IndirectOffsetOnAxis(ap=at[:, s, k:k + 1], axis=0)).then_inc(got[s], 16)

            @block.vector
            def _(v):
                v.sem_inc(added, 5)
                with v.Fori(0, 5) as i:
                    for s in range(5):
                        t = i * 5 + s
                        v.wait_ge(got[s], i * 32 + 32)
                        v.sem_inc(dve_on, 1)
                        for k in range(2):
                            v.scalar_tensor_tensor(out=Y[:, t, :], in0=ring[:, 2 * s + k, :], scalar=weights[:, t, k:k + 1], in1=Y[:, t, :],
                                                   op0=ALU.mult, op1=ALU.add).then_inc(half if k == 0 else added, 1)
                            if k == 0:
                                v.wait_ge(half, i * 5 + (s + 1))
                                v.sem_inc(dve_on, 1)
                        v.wait_ge(added, i * 5 + (s + 6))
                        v.sem_inc(dve_on, 1)
                        v.bn_stats(out=parts[:, t, :], in_=Y[:, t, :]).then_inc(taken, 1)
                v.wait_ge(taken, NT)


def table_rows(table):
    return table.rearrange("(t p) w -> p t w", p=TN)


def move(nc, name, pairs):
    with Phase(nc, name) as ph:
        moved = ph.sem("moved")
        with nc.Block() as block:
            @block.sync
            def _(sp):
                for to, of in pairs:
                    sp.dma_start(to, of).then_inc(moved, 16)
                sp.wait_ge(moved, 16 * len(pairs))


def vector_steps(nc, name, steps, loads=()):
    with Phase(nc, name) as ph:
        link_s, asked, answered, loaded = (ph.sem(k) for k in ("link", "asked", "answered", "loaded"))
        asks = []
        with nc.Block() as block:
            @block.sync
            def _(sp):
                for to, of in loads:
                    sp.dma_start(to, of).then_inc(loaded, 16)
                if loads:
                    sp.wait_ge(loaded, 16 * len(loads))

            @block.vector
            def _(v):
                if loads:
                    v.wait_ge(loaded, 16 * len(loads))

                def act_do(*a):
                    asks.append(a)
                    v.sem_inc(asked, 1)
                    v.wait_ge(answered, len(asks))
                steps(v, chain(v, link_s), act_do)

            @block.scalar
            def _(act):
                for n, (out, in_, func) in enumerate(asks):
                    act.wait_ge(asked, n + 1)
                    nc.scalar.activation(out, in_, func).then_inc(answered, 1)


def top2_gates(nc, name, cs, scores, n, gates=None, hots=None, weights=None):
    W = scores.shape[2]
    with Phase(nc, name + "_b") as ph:
        best = ph.sb("best", [TN, NT, 8])
        at_i = ph.sb("at_i", [TN, NT, 8], U32)
        at = ph.sb("at", [TN, NT, 8])
        diff, rest = (ph.sb(k, [TN, NT]) for k in ("diff", "rest"))
        hot = ph.sb("hot", [TN, NT, n])

        def steps(v, link, act_do):
            for t in range(NT):
                link(v.max(best[:, t, :], scores[:, t, :]), early=t < NT - 1)
            for t in range(NT):
                link(v.max_index(at_i[:, t, :], best[:, t, :], scores[:, t, :]), early=t < NT - 1)
            link(v.tensor_copy(at[:], at_i[:]))
            link(v.tensor_tensor(diff[:], best[:, :, 1], best[:, :, 0], ALU.subtract))
            act_do(diff[:], diff[:], ACT.Exp)
            link(v.tensor_scalar(rest[:], diff[:], 1.0, None, ALU.add))
            link(v.reciprocal(rest[:], rest[:]))
            link(v.tensor_tensor(diff[:], diff[:], rest[:], ALU.mult))
            number = cs.count_row[0:TN, 0:n].unsqueeze(1).to_broadcast([TN, NT, n])
            wide = lambda a: a.unsqueeze(2).to_broadcast([TN, NT, n])
            if hots is not None:
                for k, w in enumerate((rest, diff)):
                    link(v.tensor_tensor(hots[:, :, k, :], number, wide(at[:, :, k]), ALU.is_equal))
                    link(v.tensor_copy(weights[:, :, k], w[:]))
                return
            link(v.tensor_tensor(hot[:], number, wide(at[:, :, 0]), ALU.is_equal))
            link(v.tensor_tensor(gates[:], hot[:], wide(rest[:]), ALU.mult))
            link(v.tensor_tensor(hot[:], number, wide(at[:, :, 1]), ALU.is_equal))
            link(v.tensor_tensor(hot[:], hot[:], wide(diff[:]), ALU.mult))
            link(v.tensor_tensor(gates[:], gates[:], hot[:], ALU.add))
        vector_steps(nc, name, steps)


def add_scaled(nc, name, Y, rstd, shift, gamma, X):
    with Phase(nc, name) as ph:
        normed, scaled, added = (ph.sem(k) for k in ("normed", "scaled", "added"))
        with nc.Block() as block:
            @block.scalar
            def _(act):
                for t in range(NT):
                    nc.scalar.activation(Y[:, t, :], Y[:, t, :], ACT.Identity, scale=rstd[:, t:t + 1], bias=shift[:, t:t + 1]).then_inc(normed, 1)

            @block.vector
            def _(v):
                def scale(t):
                    v.wait_ge(normed, t + 1)
                    v.tensor_tensor(Y[:, t, :], Y[:, t, :], gamma, ALU.mult).then_inc(scaled, 1)

                scale(0)
                for t in range(NT):
                    if t + 1 < NT:
                        scale(t + 1)
                    v.wait_ge(scaled, t + 1)
                    v.tensor_tensor(X[:, t, :], X[:, t, :], Y[:, t, :], ALU.add).then_inc(added, 1)
                v.wait_ge(added, NT)


def take_sums(nc, name, acc, rows, dinv, width):
    def steps(v, link, act_do):
        link(v.tensor_tensor(rows[:], acc[:, 0:NT * width].rearrange("p (t w) -> p t w", w=width), rows[:], ALU.add))
        link(v.tensor_tensor(rows[:], rows[:], dinv[:].unsqueeze(2).to_broadcast([TN, NT, width]), ALU.mult))
    vector_steps(nc, name, steps)


def batch_norm(nc, name, cs, rows, bias, gamma, beta, width, XT):
    with Phase(nc, name) as ph:
        cols = ph.sb("cols", [width, 3])
        parts = ph.sb("parts", [width, 7, 6])
        ms = ph.sb("ms", [width, 2])
        scale, move_ = ph.sb("scale", [width, 1]), ph.sb("shift", [width, 1])
        tp = [ph.psum(f"tp{k}", [width, TN]) for k in range(4)]
        loaded, turned, copied, link_s, asked, answered, relu = (
            ph.sem(k) for k in ("loaded", "turned", "copied", "link", "asked", "answered", "relu"))
        with nc.Block() as block:
            @block.sync
            def _(sp):
                for k, a in enumerate((bias, gamma, beta)):
                    sp.dma_start(cols[:, k:k + 1], a.rearrange("(p a) -> p a", a=1)).then_inc(loaded, 16)
                sp.wait_ge(loaded, 48)

            @block.vector
            def _(v):
                v.wait_ge(loaded, 48)
                v.wait_ge(copied, NT)
                link = chain(v, link_s)
                for k in range(7):
                    lo, hi = k * 500, min(N, k * 500 + 500)
                    link(v.bn_stats(out=parts[:, k, :], in_=XT[:, lo:hi]))
                link(v.bn_aggr(out=ms[:], in_=parts[:].rearrange("p k s -> p (k s)")))
                link(v.tensor_scalar(ms[:, 1:2], ms[:, 1:2], EPS, None, ALU.add))
                v.sem_inc(asked, 1)
                v.wait_ge(answered, 1)
                link(v.reciprocal(scale[:], ms[:, 1:2]))
                link(v.tensor_tensor(scale[:], scale[:], cols[:, 1:2], ALU.mult))
                link(v.scalar_tensor_tensor(out=move_[:], in0=scale[:], scalar=ms[:, 0:1], in1=cols[:, 2:3], op0=ALU.mult, op1=ALU.subtract))
                link(v.tensor_scalar(move_[:], move_[:], -1.0, None, ALU.mult))
                v.sem_inc(asked, 1)

            @block.tensor
            def _(pe):
                for t in range(NT):
                    if t >= 4:
                        pe.wait_ge(copied, t - 3)
                    pe.transpose(tp[t % 4][:], rows[:, t, :], cs.ident[0:TN, 0:TN]).then_inc(turned, 1)

            @block.scalar
            def _(act):
                act.wait_ge(loaded, 48)
                for t in range(NT):
                    act.wait_ge(turned, t + 1)
                    nc.scalar.activation(XT[:, t * TN:(t + 1) * TN], tp[t % 4][:], ACT.Identity, bias=cols[:, 0:1]).then_inc(copied, 1)
                act.wait_ge(asked, 1)
                nc.scalar.activation(ms[:, 1:2], ms[:, 1:2], ACT.Sqrt).then_inc(answered, 1)
                act.wait_ge(asked, 2)
                nc.scalar.activation(XT[:], XT[:], ACT.Relu, scale=scale[:], bias=move_[:]).then_inc(relu, 1)
                act.wait_ge(relu, 1)


def from_features(nc, name, groups, cols, finish, loads, stats=None):
    with Phase(nc, name) as ph:
        ps = [ph.psum(f"ps{k}", [TN, 512]) for k in range(4)]
        loaded, summed, finished, link_s, taken = (ph.sem(k) for k in ("loaded", "summed", "finished", "link", "taken"))
        with nc.Block() as block:
            @block.sync
            def _(sp):
                for to, of in loads:
                    sp.dma_start(to, of).then_inc(loaded, 16)
                sp.wait_ge(loaded, 16 * len(loads))

            @block.tensor
            def _(pe):
                pe.wait_ge(loaded, 16 * len(loads))
                for t in range(NT):
                    if t >= 4:
                        pe.wait_ge(finished, t - 3)
                    for k, (XT, W) in enumerate(groups):
                        ins = pe.matmul(ps[t % 4][:, 0:cols], XT[:, t * TN:(t + 1) * TN], W, start=(k == 0), stop=(k == len(groups) - 1))
                    ins.then_inc(summed, 1)

            @block.vector
            def _(v):
                v.wait_ge(loaded, 16 * len(loads))
                link = chain(v, link_s)
                for t in range(NT):
                    v.wait_ge(summed, t + 1)
                    finish(v, link, t, ps[t % 4][:, 0:cols]).then_inc(finished, 1)
                    if stats and t:
                        v.wait_ge(finished, t)
                        v.bn_stats(out=stats[1][:, t - 1, :], in_=stats[0][:, t - 1, :]).then_inc(taken, 1)
                v.wait_ge(finished, NT)
                if stats:
                    v.bn_stats(out=stats[1][:, NT - 1, :], in_=stats[0][:, NT - 1, :]).then_inc(taken, 1)
                    v.wait_ge(taken, NT)


def gat_scores(nc, cs, table, AD, GT, S):
    C = GH * GE + GH
    with Phase(nc, "gscore") as ph:
        ring = ph.sb("ring", [P, TURN, C])
        idx = ph.sb("idx", [P, 2, TURN], I32)
        Lb = ph.sb("Lb", [TN, RING, PB * P])
        hotT = ph.sb("hotT", [TN, RING, PB * P])
        dist = ph.sb("dist", [TN, RING, PB * P])
        ad = [ph.psum(f"ad{q}", [P, PB, GH]) for q in range(RING)]
        idx_ready, hot_ready, ad_ready, taken, dist_ready, pool_on, sp_on, act_on, pe_on, dve_on, leaked = (
            ph.sem(k) for k in ("idx", "hot", "ad", "taken", "dist", "pool_on", "sp_on", "act_on", "pe_on", "dve_on", "leaked"))
        got = [ph.sem(f"got{q}") for q in range(RING)]
        lb_got = [ph.sem(f"lb{q}") for q in range(RING)]
        with nc.Block() as block:
            @block.gpsimd
            def _(g):
                gather_pairs(g, cs, table, ring, idx, idx_ready, taken, got, pool_on)

            @block.sync
            def _(sp):
                with sp.Fori(0, cs.loops) as i:
                    for q in range(RING):
                        load_local_rows(sp, cs, Lb, lb_got, hot_ready, sp_on, i, q)

            @block.scalar
            def _(act):
                act.sem_inc(hot_ready, RING)
                with act.Fori(0, cs.loops) as i:
                    for q in range(RING):
                        act.wait_ge(ad_ready, i * RING + (q + 1))
                        act.sem_inc(act_on, 1)
                        node_hots(nc, act, cs, Lb, hotT, dist, lb_got, hot_ready, (dist_ready, act_on), i, q)

            @block.tensor
            def _(pe):
                pe.sem_inc(ad_ready, RING)
                regs = [pe.alloc_register(f"{ph.name}_tile{u}") for u in range(PB)]
                with pe.Fori(0, cs.loops) as i:
                    for q in range(RING):
                        pe.wait_ge(hot_ready, i * RING + (RING + q + 1))
                        pe.sem_inc(pe_on, 1)
                        pe.wait_ge(taken, i * RING + (q + 1))
                        pe.sem_inc(pe_on, 1)
                        tiles = load_tiles(pe, regs, cs, i, q)
                        for u in range(PB):
                            tile = tiles[u]
                            ins = pe.matmul(ad[q][:, u, :], hotT[:, q, u * P:(u + 1) * P], AD[:, tile, :], start=True, stop=True)
                        ins.then_inc(ad_ready, 1)

            @block.vector
            def _(v):
                v.sem_inc(taken, RING)
                with v.Fori(0, cs.loops) as i:
                    for q in range(RING):
                        v.wait_ge(got[q], i * (16 * PB) + 16 * PB)
                        v.sem_inc(dve_on, 1)
                        batch = bass.ds(i * (TURN) + q * PB, PB)
                        part = ring[:, q * PB:(q + 1) * PB, :]
                        v.tensor_copy(GT[:, batch, :], part)
                        v.wait_ge(ad_ready, i * RING + (RING + q + 1))
                        v.sem_inc(dve_on, 1)
                        v.tensor_tensor(S[:, batch, :], ad[q][:], part[:, :, GH * GE:C], ALU.add).then_inc(taken, 1)
                v.wait_ge(taken, cs.loops * RING + RING)
                v.scalar_tensor_tensor(out=S[:], in0=S[:], scalar=0.2, in1=S[:], op0=ALU.mult, op1=ALU.max).then_inc(leaked, 1)
                v.wait_ge(leaked, 1)


def gat_sums(nc, cs, RW, acc):
    C = RW.shape[2]
    with Phase(nc, "gsum") as ph:
        hot = ph.sb("hot", [P, RING, PB, TN])
        zero = ph.sb("zero", [1, 512])
        hot_ready, summed, zeroed, pe_on, dve_on = (ph.sem(k) for k in ("hot", "summed", "zeroed", "pe_on", "dve_on"))
        with nc.Block() as block:
            @block.vector
            def _(v):
                v.memset(zero[:], 0.0).then_inc(zeroed, 1)
                with v.Fori(0, cs.loops) as i:
                    for q in range(RING):
                        v.wait_ge(summed, i * RING + (q + 1))
                        v.sem_inc(dve_on, 1)
                        own = cs.local[:, bass.ds(i * (TURN) + q * PB, PB)]
                        v.tensor_tensor(hot[:, q, :, :], cs.count_row[:, 0:TN].unsqueeze(1).to_broadcast([P, PB, TN]),
                                        own.unsqueeze(2).to_broadcast([P, PB, TN]), ALU.is_equal).then_inc(hot_ready, 1)

            @block.tensor
            def _(pe):
                pe.wait_ge(zeroed, 1)
                for b in range(2):
                    pe.matmul(acc[:, b * 512:(b + 1) * 512], zero[:, 0:TN], zero[:], start=True, stop=True)
                pe.sem_inc(summed, RING)
                regs = [pe.alloc_register(f"{ph.name}_tile{u}") for u in range(TURN)]
                with pe.Fori(0, cs.loops) as i:
                    pe.load(regs, cs.tile_of[0:1, bass.ds(i * TURN, TURN)])
                    tiles = [pe.snap(r, min_val=0, max_val=NT - 1) for r in regs]
                    for q in range(RING):
                        pe.wait_ge(hot_ready, i * RING + (q + 1))
                        pe.sem_inc(pe_on, 1)
                        for u in range(PB):
                            p = i * (TURN) + (q * PB + u)
                            tile = tiles[q * PB + u]
                            ins = pe.matmul(acc[:, bass.ds(tile * 32, C)], hot[:, q, u, :], RW[:, p, :],
                                            start=False, stop=True, skip_group_check=True)
                        ins.then_inc(summed, 1)
                pe.wait_ge(summed, cs.loops * RING + RING)


def build(nc, a, out):
    with ExitStack() as ctx:
        def sb(name, shape, dt=F32, c=ctx):
            return c.enter_context(nc.sbuf_tensor(name, shape, dt))

        def dram(name, shape):
            return nc.dram_tensor(name, shape, F32)

        cs = Consts(sb)
        g1 = Graph("g1", sb, dram, cs, E1)
        g2 = Graph("g2", sb, dram, cs, E2)
        sorted_edges = nc.dram_tensor("sorted_edges", [E2, 2], I32).ap()
        q_dram, v_dram, h1_dram, h2_dram, g_dram = (dram(k, [N, w]).ap() for k, w in (
            ("q_rows", D), ("v_rows", D), ("h1_rows", 128), ("h2_rows", 64), ("g_rows", GH * GE + GH)))
        carries = {h: (dram(f"side{h}", [4 * pairs * h // P, P]).ap(), dram(f"cin{h}", [2 * pairs * h // P, P]).ap())
                   for h, pairs in ((H, g1.pairs), (GH, g2.pairs))}

        X = sb("X", [TN, NT, D])
        rstd, shift, parts = sb("rstd", [TN, NT]), sb("shift", [TN, NT]), sb("parts", [TN, NT, 6])
        dinv = sb("dinv", [TN, NT])
        sort_pay, sort_pos = sb("sort_pay", [P, E2 // P, 2], I32), sb("sort_pos", [P, E2 // P], I32)
        x_slots, y_slots = (dram(k, [tiles * P, D]).ap() for k, tiles in (("x_slots", X_TILES), ("y_slots", SLOT_TILES)))
        rows_dram = dram("u_rows", [N, D]).ap()
        slots_filled, up_in, down_in = (nc.alloc_semaphore(k) for k in ("slots_filled", "up_in", "down_in"))
        x_in = nc.alloc_semaphore("x_in")

        constants(nc, cs)
        index_tables(nc, g1, a["src"], a["dst"])

        with ExitStack() as l1:
            T = sb("T", [TN, NT, D], c=l1)
            bo = sb("bo", [TN, D], c=l1)
            with ExitStack() as att:
                S = sb("S", [P, g1.pairs, H], c=att)
                es = EdgeSort(lambda *k: sb(*k, c=att), E2, sort_pay, sort_pos)
                start_loads(nc, [(X[:], table_rows(a["x"]))], x_in)
                histogram(nc, cs, a["L1_ffn_edge_index"], es)
                wait_loads(nc, x_in, 1)
                zeros = sb("zeros", [P, D], c=att)

                def no_rows(v, link, act_do):
                    link(v.memset(zeros[:], 0.0))
                vector_steps(nc, "zero", no_rows)
                start_loads(nc, [(x_slots.rearrange("(t p) d -> p t d", p=P), zeros[:].unsqueeze(1).to_broadcast([P, X_TILES, D]))],
                            slots_filled)
                row_stats(nc, "st0", X, rstd, shift, parts)
                row_stats(nc, "st1", T, rstd, shift, parts, source=X)
                with ExitStack() as kq:
                    K = sb("K", [TN, NT, D], c=kq)
                    with ExitStack() as qv:
                        Q, V = sb("Q", [TN, NT, D], c=qv), sb("V", [TN, NT, D], c=qv)
                        BQ = sb("BQ", [TN, 3 * D], c=qv)
                        SCALE = D ** -0.5

                        def scale_bq(v, link, act_do):
                            link(v.tensor_scalar(BQ[:, 0:D], BQ[:, 0:D], SCALE, None, ALU.mult))
                        vector_steps(nc, "bq", scale_bq, [(BQ[:], a["L0_gnn_bqkv"].partition_broadcast(TN)),
                                                          (bo[:], a["L0_gnn_b_out"].partition_broadcast(TN))])

                        def finish(v, j, tile, s, ps):
                            if j == 0:
                                v.scalar_tensor_tensor(out=Q[:, tile, :], in0=ps[:, 0:D], scalar=SCALE, in1=BQ[:, 0:D], op0=ALU.mult, op1=ALU.add)
                                return v.tensor_tensor(K[:, tile, :], ps[:, D:2 * D], BQ[:, D:2 * D], ALU.add)
                            return v.tensor_tensor(V[:, tile, :], ps, BQ[:, 2 * D:3 * D], ALU.add)
                        project(nc, "qkv", cs, T, rstd, shift, a["L0_gnn_Wqkv"], [(0, 512), (512, 256)], finish,
                                affine=(a["L0_gnn_ln_attn_g"], a["L0_gnn_ln_attn_b"]), stores=[(q_dram, Q), (v_dram, V)])
                    edge_scores(nc, g1, q_dram, K, S, es, a["L1_ffn_edge_index"])
                with ExitStack() as mw:
                    M = sb("M", [P, g1.pairs, H], c=mw)

                    def add_b_out(v, link):
                        link(v.tensor_tensor(X[:], X[:], bo[:].unsqueeze(1).to_broadcast([TN, NT, D]), ALU.add))
                    wait_loads(nc, slots_filled, 1)
                    segment_max(nc, g1, "max8", S, H, M, carries[H], add_b_out)
                    Wt = sb("Wt", [P, g1.pairs, H + 1], c=mw)
                    edge_weights(nc, "w8", S, M, Wt[:, :, 0:H])

                    def one_column(v, link, act_do):
                        link(v.memset(Wt[:, :, H], 1.0))
                    vector_steps(nc, "one", one_column)
                    acc = sb("acc", [TN, NT, D + H + 1], c=mw)
                    weigh_values(nc, g1, v_dram, Wt, acc)

                    def combine(v, link, act_do):
                        w = acc[:, :, D:D + H]
                        link(v.tensor_scalar(w, w, 0.5, None, ALU.max))
                        link(v.reciprocal(w, w))
                        val = acc[:, :, 0:D].rearrange("p t (h d) -> p t h d", h=H)
                        link(v.tensor_tensor(val, val, w.unsqueeze(3).to_broadcast([TN, NT, H, D // H]), ALU.mult))
                        link(v.tensor_tensor(T[:], T[:], acc[:, :, 0:D], ALU.add))
                        link(v.tensor_scalar(dinv[:], acc[:, :, D + H], 1.0, None, ALU.add))
                        act_do(dinv[:], dinv[:], ACT.Sqrt)
                        link(v.reciprocal(dinv[:], dinv[:]))
                    vector_steps(nc, "comb", combine)
            with ExitStack() as ff:
                UT = sb("UT0", [P, 2, N], c=ff)
                gate1 = sb("gate1", [TN, NT, 2], c=ff)
                row_stats(nc, "st2", T, rstd, shift, parts)
                project(nc, "ln2", cs, T, rstd, shift, None, [], None,
                        affine=(a["L0_gnn_ln_res_g"], a["L0_gnn_ln_res_b"]), UT=UT)

                def start(v, link, act_do):
                    link(v.memset(gate1[:], 1.0))
                    link(v.tensor_tensor(X[:], X[:], T[:], ALU.add))
                vector_steps(nc, "y0", start)
                w_in = a["L0_gnn_W_in"].rearrange("d (e f) -> e d f", e=2)
                experts(nc, "ff0", cs, UT, X, gate1, w_in, a["L0_gnn_b_in"].rearrange("(e f) -> e f", e=2),
                        a["L0_gnn_W_out"].rearrange("(e f) d -> e f d", e=2), None, 2, ACT.Gelu, parts)
        with ExitStack() as moe:
            logits = sb("logits", [TN, NT, N_EXP], c=moe)
            hots, weights = sb("hots", [TN, NT, 2, N_EXP], c=moe), sb("weights", [TN, NT, 2], c=moe)
            pos, expert_of = sb("pos", [TN, NT, 2], I32, c=moe), sb("expert_of", [1, OWNERS], I32, c=moe)
            gb = sb("gb", [TN, 3 * D], c=moe)
            with ExitStack() as big:
                UP = sb("UP", [P, N_EXP, 2, F_EXP], c=big)
                start_loads(nc, [(UP[:], a["L0_ffn_w1"].rearrange("e (c p) f -> p e c f", p=P))], up_in)
                row_stats(nc, "st3", X, rstd, shift, parts, taken_before=True)
                move(nc, "gb", [(gb[:, 0:N_EXP], a["L0_ffn_gate_b"].partition_broadcast(TN)),
                                (gb[:, D:2 * D], a["L0_ffn_gamma"].partition_broadcast(TN)),
                                (gb[:, 2 * D:3 * D], a["L0_ffn_beta"].partition_broadcast(TN))])
                with ExitStack() as norm:
                    U = sb("U1", [TN, NT, D], c=norm)
                    project(nc, "gate", cs, X, rstd, shift, a["L0_ffn_gate_w"], [(0, N_EXP)],
                            lambda v, j, tile, s, ps: v.tensor_tensor(logits[:, tile, :], ps, gb[:, 0:N_EXP], ALU.add),
                            rows_out=U, stores=[(rows_dram, U)])
                DOWN = sb("DOWN", [P, N_EXP, F_EXP // P, D], c=big)
                start_loads(nc, [(DOWN[:], a["L0_ffn_w2"].rearrange("e (f p) d -> p e f d", p=P))], down_in)
                top2_gates(nc, "top16", cs, logits, N_EXP, hots=hots, weights=weights)
                route(nc, cs, hots, pos, expert_of)
                send_rows(nc, rows_dram, pos, x_slots, X, gb[:, 2 * D:3 * D])
                slot_experts(nc, cs, x_slots, y_slots, UP, DOWN, a["L0_ffn_b1"], a["L0_ffn_b2"], expert_of,
                             up_in, down_in, es, sorted_edges)
            Y = sb("Y1", [TN, NT, D], c=moe)
            move(nc, "back", [(Y[:], table_rows(rows_dram))])
            collect_rows(nc, y_slots, pos, weights, Y, parts)
            row_stats(nc, "st4", Y, rstd, shift, parts, taken_before=True)
            add_scaled(nc, "addm", Y, rstd, shift, gb[:, D:2 * D], X)
        with ExitStack() as gcn:
            UT = sb("UT2", [P, 2, N], c=gcn)
            H1 = sb("H1", [TN, NT, 128], c=gcn)
            H2 = sb("H2", [TN, NT, 64], c=gcn)
            XT1 = sb("XT1", [128, N], c=gcn)
            XT2 = sb("XT2", [64, N], c=gcn)
            W2, Wfc, Wfc2 = sb("gW2", [128, 64], c=gcn), sb("Wfc", [P, 3, D], c=gcn), sb("Wfc2", [64, D], c=gcn)
            bfc = sb("bfc", [TN, D], c=gcn)
            relu = sb("relu", [TN, 4, D], c=gcn)
            row_stats(nc, "st5", X, rstd, shift, parts)
            project(nc, "gc1", cs, X, rstd, shift, a["L1_gnn_W1"], [(0, 128)],
                    lambda v, j, tile, s, ps: v.tensor_scalar(H1[:, tile, :], ps, dinv[:, bass.ds(tile, 1)], None, ALU.mult),
                    UT=UT, stores=[(h1_dram, H1)])
            with nc.psum_tensor("acc1", [TN, 7 * 512], F32) as acc1:
                neighbour_sums(nc, "sum1", g1, h1_dram, 128, acc1)
                take_sums(nc, "take1", acc1, H1, dinv, 128)
            batch_norm(nc, "bn1", cs, H1, a["L1_gnn_b1"], a["L1_gnn_g1"], a["L1_gnn_be1"], 128, XT1)
            from_features(nc, "gc2", [(XT1, W2[:])], 64,
                          lambda v, link, t, ps: v.tensor_scalar(H2[:, t, :], ps, dinv[:, t:t + 1], None, ALU.mult),
                          [(W2[:], a["L1_gnn_W2"])])
            move(nc, "h2", [(table_rows(h2_dram), H2[:])])
            with nc.psum_tensor("acc2", [TN, 4 * 512], F32) as acc2:
                neighbour_sums(nc, "sum2", g1, h2_dram, 64, acc2, other=g2, joined=sorted_edges)
                take_sums(nc, "take2", acc2, H2, dinv, 64)
            batch_norm(nc, "bn2", cs, H2, a["L1_gnn_b2"], a["L1_gnn_g2"], a["L1_gnn_be2"], 64, XT2)

            def add_fc(v, link, t, ps):
                r = relu[:, t % 4, :]
                link(v.tensor_tensor(r, ps, bfc[:], ALU.add))
                return v.scalar_tensor_tensor(out=X[:, t, :], in0=r, scalar=0.0, in1=X[:, t, :], op0=ALU.max, op1=ALU.add)
            from_features(nc, "fc", [(UT[:, 0, :], Wfc[:, 0, :]), (UT[:, 1, :], Wfc[:, 1, :]), (XT1, Wfc[:, 2, :]), (XT2, Wfc2[:])],
                          D, add_fc, [(Wfc[:], a["L1_gnn_Wfc"][0:384, :].rearrange("(k p) n -> p k n", p=P)),
                                      (Wfc2[:], a["L1_gnn_Wfc"][384:448, :]),
                                      (bfc[:], a["L1_gnn_bfc"].partition_broadcast(TN))], stats=(X, parts))
        with ExitStack() as gat:
            UT = sb("UT3", [P, 2, N], c=gat)
            gates = sb("gates4", [TN, NT, 4], c=gat)
            HG = sb("HG", [TN, NT, 20], c=gat)
            AD = sb("AD", [TN, NT, 4], c=gat)
            tmp = sb("tmpg", [TN, NT, 16], c=gat)
            vec = sb("vecg", [TN, 5, 16], c=gat)
            row_stats(nc, "st6", X, rstd, shift, parts, taken_before=True)
            project(nc, "gat", cs, X, rstd, shift, a["L1_ffn_W_gat"], [(0, 16)],
                    lambda v, j, tile, s, ps: v.tensor_copy(HG[:, tile, 0:16], ps), UT=UT)
            wide16 = lambda k: vec[:, k, :].unsqueeze(1).to_broadcast([TN, NT, 16])

            def attend(v, link, act_do):
                for k, dest in ((0, HG[:, :, 16:20]), (1, AD[:])):
                    link(v.tensor_tensor(tmp[:], HG[:, :, 0:16], wide16(k), ALU.mult))
                    link(v.tensor_reduce(dest, tmp[:].rearrange("p t (h e) -> p t h e", h=GH), AX.X, ALU.add))
            vector_steps(nc, "att", attend, [(vec[:, k, :], v.partition_broadcast(TN)) for k, v in enumerate(
                (a["L1_ffn_att_src"].rearrange("h e -> (h e)"), a["L1_ffn_att_dst"].rearrange("h e -> (h e)"),
                 a["L1_ffn_b_gat"], a["L1_ffn_ln_gamma"], a["L1_ffn_ln_beta"]))])
            move(nc, "g", [(table_rows(g_dram), HG[:])])
            accs = sb("accs", [TN, NT, 25], c=gat)
            with ExitStack() as edges:
                S = sb("Sg", [P, g2.pairs, GH], c=edges)
                M = sb("Mg", [P, g2.pairs, GH], c=edges)
                RW = sb("RW", [P, g2.pairs, 25], c=edges)
                with ExitStack() as gt:
                    GT = sb("GT", [P, g2.pairs, 20], c=gt)
                    gat_scores(nc, g2, g_dram, AD, GT, S)
                    segment_max(nc, g2, "max4", S, GH, M, carries[GH])
                    edge_weights(nc, "w4", S, M, RW[:, :, 16:20])

                    def rows25(v, link, act_do):
                        w = RW[:, :, 16:20].unsqueeze(3).to_broadcast([P, g2.pairs, GH, GE])
                        link(v.tensor_tensor(RW[:, :, 0:16].rearrange("p t (h e) -> p t h e", h=GH),
                                             GT[:, :, 0:16].rearrange("p t (h e) -> p t h e", h=GH), w, ALU.mult))
                        link(v.tensor_tensor(RW[:, :, 20:24], M[:], g2.last_of[:].unsqueeze(2).to_broadcast([P, g2.pairs, GH]), ALU.mult))
                        link(v.tensor_copy(RW[:, :, 24], g2.last_of[:]))
                    vector_steps(nc, "rw", rows25)
                with nc.psum_tensor("acc3", [TN, 1024], F32) as acc3:
                    gat_sums(nc, g2, RW, acc3)

                    def keep(v, link, act_do):
                        link(v.tensor_copy(accs[:], acc3[:, 0:800].rearrange("p (t c) -> p t c", c=32)[:, :, 0:25]))
                    vector_steps(nc, "keep", keep)
            with ExitStack() as node:
                m1, own, m = (sb(k, [TN, NT, GH], c=node) for k in ("m1", "own", "mx"))
                agg, sq = sb("agg", [TN, NT, 16], c=node), sb("sq", [TN, NT, 16], c=node)
                mean, var = sb("mean", [TN, NT], c=node), sb("var", [TN, NT], c=node)
                sc8 = sb("sc8", [TN, NT, 8], c=node)

                def finish_gat(v, link, act_do):
                    four = lambda x: x.unsqueeze(3).to_broadcast([TN, NT, GH, GE])
                    heads = lambda x: x.rearrange("p t (h e) -> p t h e", h=GH)
                    link(v.tensor_scalar(mean[:], accs[:, :, 24], -1.0, BIG, ALU.add, ALU.mult))
                    link(v.tensor_tensor(m1[:], accs[:, :, 20:24], mean[:].unsqueeze(2).to_broadcast([TN, NT, GH]), ALU.add))
                    link(v.tensor_tensor(own[:], HG[:, :, 16:20], AD[:], ALU.add))
                    link(v.scalar_tensor_tensor(out=own[:], in0=own[:], scalar=0.2, in1=own[:], op0=ALU.mult, op1=ALU.max))
                    link(v.tensor_tensor(m[:], m1[:], own[:], ALU.max))
                    link(v.tensor_tensor(m1[:], m1[:], m[:], ALU.subtract))
                    link(v.tensor_tensor(own[:], own[:], m[:], ALU.subtract))
                    act_do(m1[:], m1[:], ACT.Exp)
                    act_do(own[:], own[:], ACT.Exp)
                    link(v.tensor_tensor(m[:], accs[:, :, 16:20], m1[:], ALU.mult))
                    link(v.tensor_tensor(m[:], m[:], own[:], ALU.add))
                    link(v.tensor_scalar(m[:], m[:], 1e-16, None, ALU.add))
                    link(v.reciprocal(m[:], m[:]))
                    link(v.tensor_tensor(heads(agg[:]), heads(accs[:, :, 0:16]), four(m1[:]), ALU.mult))
                    link(v.tensor_tensor(heads(sq[:]), heads(HG[:, :, 0:16]), four(own[:]), ALU.mult))
                    link(v.tensor_tensor(agg[:], agg[:], sq[:], ALU.add))
                    link(v.tensor_tensor(heads(agg[:]), heads(agg[:]), four(m[:]), ALU.mult))
                    link(v.tensor_tensor(agg[:], agg[:], wide16(2), ALU.add))
                    w16 = lambda x: x.unsqueeze(2).to_broadcast([TN, NT, 16])
                    link(v.tensor_reduce(mean[:], agg[:], AX.X, ALU.add))
                    link(v.tensor_scalar(mean[:], mean[:], 1.0 / 16, None, ALU.mult))
                    link(v.tensor_tensor(agg[:], agg[:], w16(mean[:]), ALU.subtract))
                    link(v.tensor_tensor(sq[:], agg[:], agg[:], ALU.mult))
                    link(v.tensor_reduce(var[:], sq[:], AX.X, ALU.add))
                    link(v.tensor_scalar(var[:], var[:], 1.0 / 16, EPS, ALU.mult, ALU.add))
                    act_do(var[:], var[:], ACT.Sqrt)
                    link(v.reciprocal(var[:], var[:]))
                    link(v.tensor_tensor(agg[:], agg[:], w16(var[:]), ALU.mult))
                    link(v.tensor_tensor(agg[:], agg[:], wide16(3), ALU.mult))
                    link(v.tensor_tensor(agg[:], agg[:], wide16(4), ALU.add))
                    link(v.memset(sc8[:], -BIG))
                    link(v.tensor_reduce(sc8[:, :, 0:4], agg[:].rearrange("p t (h e) -> p t e h", h=GH), AX.X, ALU.add))
                    link(v.tensor_scalar(sc8[:, :, 0:4], sc8[:, :, 0:4], 0.25, None, ALU.mult))
                vector_steps(nc, "fin", finish_gat)
                top2_gates(nc, "top4", cs, sc8, 4, gates)
            experts(nc, "ff1", cs, UT, X, gates, a["L1_ffn_W1"], a["L1_ffn_b1"], a["L1_ffn_W2"], a["L1_ffn_b2"], 4, ACT.Gelu)
        move(nc, "out", [(table_rows(out), X[:])])


NAMES = ['x', 'src', 'dst', 'L0_gnn_Wqkv', 'L0_gnn_bqkv', 'L0_gnn_ln_attn_g', 'L0_gnn_ln_attn_b', 'L0_gnn_ln_res_g',
         'L0_gnn_ln_res_b', 'L0_gnn_W_in', 'L0_gnn_b_in', 'L0_gnn_W_out', 'L0_gnn_b_out', 'L0_ffn_gate_w', 'L0_ffn_gate_b',
         'L0_ffn_w1', 'L0_ffn_b1', 'L0_ffn_w2', 'L0_ffn_b2', 'L0_ffn_gamma', 'L0_ffn_beta', 'L1_gnn_W1', 'L1_gnn_b1',
         'L1_gnn_g1', 'L1_gnn_be1', 'L1_gnn_W2', 'L1_gnn_b2', 'L1_gnn_g2', 'L1_gnn_be2', 'L1_gnn_Wfc', 'L1_gnn_bfc',
         'L1_ffn_W_gat', 'L1_ffn_att_src', 'L1_ffn_att_dst', 'L1_ffn_b_gat', 'L1_ffn_ln_gamma', 'L1_ffn_ln_beta',
         'L1_ffn_W1', 'L1_ffn_b1', 'L1_ffn_W2', 'L1_ffn_b2',
         'L1_ffn_edge_index']


def kernel(**inputs):
    import concourse.bacc as bacc
    from concourse.bass_utils import run_bass_kernel_spmd

    nc = bacc.Bacc("TRN2", target_bir_lowering=False, num_devices=1)
    arrays, aps = {}, {}
    for name in NAMES:
        arrays[f"in_{name}"] = np.ascontiguousarray(inputs[name])
        aps[name] = nc.dram_tensor(f"in_{name}", arrays[f"in_{name}"].shape, mybir.dt.from_np(arrays[f"in_{name}"].dtype),
                                   kind="ExternalInput").ap()
    out = nc.dram_tensor("out_x", (N, D), F32, kind="ExternalOutput").ap()
    build(nc, aps, out)
    got = run_bass_kernel_spmd(nc, [arrays], core_ids=[0])
    return got.results[0]["out_x"]
```
